# Optimizing a Trainium2 kernel written in Bass

```python
import numpy as np
import jax
import jax.numpy as jnp

def _softmax(x, axis=-1):
    return jax.nn.softmax(x, axis=axis)

def _gelu(x):
    return jax.nn.gelu(x, approximate=True)

def _silu(x):
    return jax.nn.silu(x)

def _sigmoid(x):
    return jax.nn.sigmoid(x)

def _layernorm(x, axis=-1, eps=1e-05):
    m = jnp.mean(x, axis=axis, keepdims=True)
    v = jnp.var(x, axis=axis, keepdims=True)
    return (x - m) / jnp.sqrt(v + eps)

def _scatter_add(tgt, idx, src, axis=0):
    return tgt.at[idx].add(src)

def _segment_sum(src, seg, n):
    return jax.ops.segment_sum(src, seg, n)
kernel_name = 'mk_gnn_ffn_d2_gnn_r16_54af93'

def setup_inputs(seed: int=0):
    np.random.seed(seed)
    _w = jnp.asarray

    def _rec_inputs():
        import jax
        import jax.numpy as jnp
        _gk = jax.random.key(seed)
        x = -0.0003713 + 1 * jax.random.normal(jax.random.fold_in(_gk, 1), (3125, 256), jnp.float32)
        _s = jax.random.randint(jax.random.fold_in(_gk, 2), (50000,), 0, 3125, jnp.int32)
        _d = jax.random.randint(jax.random.fold_in(_gk, 3), (50000,), 0, 3125, jnp.int32)
        _loop = jnp.arange(3125, dtype=jnp.int32)
        src = jnp.concatenate([_s, _d, _loop])
        dst = jnp.concatenate([_d, _s, _loop])
        _o = jnp.argsort(dst, stable=True)
        src = src[_o]
        dst = dst[_o]
        return (x, src, dst)
    x, src, dst = _rec_inputs()

    def _L0_gnn_setup():
        import jax, jax.numpy as jnp
        import numpy as np
        N, E, IN_DIM, H, D = (3125, 50000, 256, 8, 32)
        ALPHA = 0.2
        key = jax.random.key(seed)
        ks = jax.random.split(key, 6)
        feat = jax.random.normal(ks[0], (N, IN_DIM), dtype=jnp.float32)
        src = jax.random.randint(ks[1], (E,), 0, N, dtype=jnp.int32)
        dst = jax.random.randint(ks[2], (E,), 0, N, dtype=jnp.int32)
        W = jax.random.normal(ks[3], (IN_DIM, H * D), dtype=jnp.float32) * 0.05
        attn_l = jax.random.normal(ks[4], (H, D), dtype=jnp.float32)
        attn_r = jax.random.normal(ks[5], (H, D), dtype=jnp.float32)
        return {'feat': feat, 'src': src, 'dst': dst, 'W': W, 'attn_l': attn_l, 'attn_r': attn_r}
    _L0_gnn_all = _L0_gnn_setup()
    _L0_gnn_in = {k: v for k, v in _L0_gnn_all.items() if k in ('W', 'attn_l', 'attn_r')}
    del _L0_gnn_all

    def _L0_ffn_setup():
        import jax, jax.numpy as jnp
        import numpy as np
        E, D, H, TOP_K = (6, 256, 256, 2)
        ROUTER_H = D // 2
        key = jax.random.key(seed)
        ks = jax.random.split(key, 12)
        s = 1.0 / np.sqrt(D)
        sh = 1.0 / np.sqrt(H)
        sr = 1.0 / np.sqrt(ROUTER_H)
        return {'features': jax.random.normal(ks[0], (8, 256, D), dtype=jnp.float32), 'router_w1': jax.random.uniform(ks[1], (D, ROUTER_H), jnp.float32, -s, s), 'router_b1': jnp.zeros((ROUTER_H,), jnp.float32), 'router_w2': jax.random.uniform(ks[2], (ROUTER_H, E), jnp.float32, -sr, sr), 'router_b2': jnp.zeros((E,), jnp.float32), 'expert_w1': jax.random.uniform(ks[3], (E, D, H), jnp.float32, -s, s), 'expert_b1': jnp.zeros((E, H), jnp.float32), 'expert_w2': jax.random.uniform(ks[4], (E, H, H), jnp.float32, -sh, sh), 'expert_b2': jnp.zeros((E, H), jnp.float32), 'expert_w3': jax.random.uniform(ks[5], (E, H, D), jnp.float32, -sh, sh), 'expert_b3': jnp.zeros((E, D), jnp.float32)}
    _L0_ffn_all = _L0_ffn_setup()
    _L0_ffn_in = {k: v for k, v in _L0_ffn_all.items() if k in ('router_w1', 'router_b1', 'router_w2', 'router_b2', 'expert_w1', 'expert_b1', 'expert_w2', 'expert_b2', 'expert_w3', 'expert_b3')}
    del _L0_ffn_all

    def _L1_gnn_setup():
        import jax, jax.numpy as jnp
        import numpy as np
        N_NODES = 6250
        N_EDGES = 200000
        NFEAT = 256
        NHID = 256
        key = jax.random.key(seed)
        k_x, k_ws, k_wn, k_src, k_dst = jax.random.split(key, 5)
        x = jax.random.normal(k_x, (N_NODES, NFEAT), dtype=jnp.float32)
        W_self = jax.random.normal(k_ws, (NFEAT, NHID), dtype=jnp.float32) * (1.0 / np.sqrt(NFEAT))
        W_neigh = jax.random.normal(k_wn, (NFEAT, NHID), dtype=jnp.float32) * (1.0 / np.sqrt(NFEAT))
        b = jnp.zeros((NHID,), dtype=jnp.float32)
        edge_src = jax.random.randint(k_src, (N_EDGES,), 0, N_NODES, dtype=jnp.int32)
        edge_dst = jax.random.randint(k_dst, (N_EDGES,), 0, N_NODES, dtype=jnp.int32)
        return {'x': x, 'W_self': W_self, 'W_neigh': W_neigh, 'b': b, 'edge_src': edge_src, 'edge_dst': edge_dst}
    _L1_gnn_all = _L1_gnn_setup()
    _L1_gnn_in = {k: v for k, v in _L1_gnn_all.items() if k in ('W_self', 'W_neigh', 'b')}
    del _L1_gnn_all

    def _L1_ffn_setup():
        import jax, jax.numpy as jnp
        import numpy as np
        B, S, H, F, E, K = (8, 256, 256, 512, 16, 2)
        EPS = 1e-05
        key = jax.random.key(seed)
        ks = jax.random.split(key, 9)
        sc = 0.02
        return {'x': jax.random.normal(ks[0], (B, S, H), dtype=jnp.float32), 'gate_w': jax.random.normal(ks[1], (H, E), dtype=jnp.float32) * sc, 'gate_b': jnp.zeros((E,), dtype=jnp.float32), 'w1': jax.random.normal(ks[2], (E, H, F), dtype=jnp.float32) * sc, 'b1': jnp.zeros((E, F), dtype=jnp.float32), 'w2': jax.random.normal(ks[3], (E, F, H), dtype=jnp.float32) * sc, 'b2': jnp.zeros((E, H), dtype=jnp.float32), 'gamma': jnp.ones((H,), dtype=jnp.float32), 'beta': jnp.zeros((H,), dtype=jnp.float32)}
    _L1_ffn_all = _L1_ffn_setup()
    _L1_ffn_in = {k: v for k, v in _L1_ffn_all.items() if k in ('gate_w', 'gate_b', 'w1', 'b1', 'w2', 'b2', 'gamma', 'beta')}
    del _L1_ffn_all
    return {'x': x, 'src': src, 'dst': dst, 'L0_gnn_W': _L0_gnn_in['W'], 'L0_gnn_attn_l': _L0_gnn_in['attn_l'], 'L0_gnn_attn_r': _L0_gnn_in['attn_r'], 'L0_ffn_router_w1': _L0_ffn_in['router_w1'], 'L0_ffn_router_b1': _L0_ffn_in['router_b1'], 'L0_ffn_router_w2': _L0_ffn_in['router_w2'], 'L0_ffn_router_b2': _L0_ffn_in['router_b2'], 'L0_ffn_expert_w1': _L0_ffn_in['expert_w1'], 'L0_ffn_expert_b1': _L0_ffn_in['expert_b1'], 'L0_ffn_expert_w2': _L0_ffn_in['expert_w2'], 'L0_ffn_expert_b2': _L0_ffn_in['expert_b2'], 'L0_ffn_expert_w3': _L0_ffn_in['expert_w3'], 'L0_ffn_expert_b3': _L0_ffn_in['expert_b3'], 'L1_gnn_W_self': _L1_gnn_in['W_self'], 'L1_gnn_W_neigh': _L1_gnn_in['W_neigh'], 'L1_gnn_b': _L1_gnn_in['b'], 'L1_ffn_gate_w': _L1_ffn_in['gate_w'], 'L1_ffn_gate_b': _L1_ffn_in['gate_b'], 'L1_ffn_w1': _L1_ffn_in['w1'], 'L1_ffn_b1': _L1_ffn_in['b1'], 'L1_ffn_w2': _L1_ffn_in['w2'], 'L1_ffn_b2': _L1_ffn_in['b2'], 'L1_ffn_gamma': _L1_ffn_in['gamma'], 'L1_ffn_beta': _L1_ffn_in['beta']}

def reference(x, src, dst, L0_gnn_W, L0_gnn_attn_l, L0_gnn_attn_r, L0_ffn_router_w1, L0_ffn_router_b1, L0_ffn_router_w2, L0_ffn_router_b2, L0_ffn_expert_w1, L0_ffn_expert_b1, L0_ffn_expert_w2, L0_ffn_expert_b2, L0_ffn_expert_w3, L0_ffn_expert_b3, L1_gnn_W_self, L1_gnn_W_neigh, L1_gnn_b, L1_ffn_gate_w, L1_ffn_gate_b, L1_ffn_w1, L1_ffn_b1, L1_ffn_w2, L1_ffn_b2, L1_ffn_gamma, L1_ffn_beta):
    import jax
    import jax.numpy as jnp

    def _L0_gnn_ref(feat, src, dst, W, attn_l, attn_r):
        import jax, jax.numpy as jnp
        import numpy as np
        N, E, IN_DIM, H, D = (3125, 50000, 256, 8, 32)
        ALPHA = 0.2
        n = feat.shape[0]
        ft = (feat @ W).reshape(n, H, D)
        a1 = jnp.einsum('nhd,hd->nh', ft, attn_l)
        a2 = jnp.einsum('nhd,hd->nh', ft, attn_r)
        e = jax.nn.leaky_relu(a1[src] + a2[dst], negative_slope=ALPHA)
        m = jax.ops.segment_max(e, dst, num_segments=n)
        ex = jnp.exp(e - m[dst])
        s = jax.ops.segment_sum(ex, dst, num_segments=n)
        alpha = ex / s[dst]
        msg = ft[src] * alpha[:, :, None]
        out = jax.ops.segment_sum(msg, dst, num_segments=n)
        return jax.nn.elu(out.reshape(n, H * D))

    def _L0_ffn_ref(features, router_w1, router_b1, router_w2, router_b2, expert_w1, expert_b1, expert_w2, expert_b2, expert_w3, expert_b3):
        import jax, jax.numpy as jnp
        import numpy as np
        E, D, H, TOP_K = (6, 256, 256, 2)
        ROUTER_H = D // 2
        rh = jax.nn.relu(features @ router_w1 + router_b1)
        expert_logits = jax.nn.softmax(rh @ router_w2 + router_b2, axis=-1)
        top_w, top_i = jax.lax.top_k(expert_logits, TOP_K)
        routing_weights = jax.nn.softmax(top_w, axis=-1)
        h1 = jax.nn.relu(jnp.einsum('bsd,edh->bseh', features, expert_w1) + expert_b1)
        h2 = jax.nn.relu(jnp.einsum('bseh,ehf->bsef', h1, expert_w2) + expert_b2)
        expert_out = jnp.einsum('bsef,efo->bseo', h2, expert_w3) + expert_b3
        sel = jnp.take_along_axis(expert_out, top_i[:, :, :, None], axis=2)
        combined = jnp.sum(sel * routing_weights[..., None], axis=2)
        return combined

    def _L1_gnn_ref(x, W_self, W_neigh, b, edge_src, edge_dst):
        import jax, jax.numpy as jnp
        import numpy as np
        N_NODES = 6250
        N_EDGES = 200000
        NFEAT = 256
        NHID = 256
        n = x.shape[0]
        msg = x[edge_src]
        agg = jax.ops.segment_sum(msg, edge_dst, num_segments=n)
        deg = jax.ops.segment_sum(jnp.ones_like(edge_dst, dtype=x.dtype), edge_dst, num_segments=n)
        h_neigh = agg / jnp.maximum(deg, 1.0)[:, None]
        out = x @ W_self + h_neigh @ W_neigh + b
        return jax.nn.relu(out)

    def _L1_ffn_ref(x, gate_w, gate_b, w1, b1, w2, b2, gamma, beta):
        import jax, jax.numpy as jnp
        import numpy as np
        B, S, H, F, E, K = (8, 256, 256, 512, 16, 2)
        EPS = 1e-05
        gate_logits = x @ gate_w + gate_b
        topk_vals, topk_idx = jax.lax.top_k(gate_logits, K)
        topk_w = jax.nn.softmax(topk_vals, axis=-1)
        h = jax.nn.relu(jnp.einsum('bsh,ehf->bsef', x, w1) + b1)
        expert_out = jnp.einsum('bsef,efh->bseh', h, w2) + b2
        sel = jnp.take_along_axis(expert_out, topk_idx[:, :, :, None], axis=2)
        moe = jnp.sum(topk_w[..., None] * sel, axis=2)
        y = x + moe
        mu = jnp.mean(y, axis=-1, keepdims=True)
        var = jnp.var(y, axis=-1, keepdims=True)
        return (y - mu) / jnp.sqrt(var + EPS) * gamma + beta
    x = x + _L0_gnn_ref(_layernorm(x, axis=-1), src, dst, L0_gnn_W, L0_gnn_attn_l, L0_gnn_attn_r)
    x = x + _L0_ffn_ref(_layernorm(x, axis=-1)[None], L0_ffn_router_w1, L0_ffn_router_b1, L0_ffn_router_w2, L0_ffn_router_b2, L0_ffn_expert_w1, L0_ffn_expert_b1, L0_ffn_expert_w2, L0_ffn_expert_b2, L0_ffn_expert_w3, L0_ffn_expert_b3)[0]
    x = x + _L1_gnn_ref(_layernorm(x, axis=-1), L1_gnn_W_self, L1_gnn_W_neigh, L1_gnn_b, src, dst)
    x = x + _L1_ffn_ref(_layernorm(x, axis=-1)[None], L1_ffn_gate_w, L1_ffn_gate_b, L1_ffn_w1, L1_ffn_b1, L1_ffn_w2, L1_ffn_b2, L1_ffn_gamma, L1_ffn_beta)[0]
    return x

_drawn_inputs = setup_inputs


def setup_inputs(seed=0):
    import zlib

    import numpy as np

    out = dict(_drawn_inputs(seed))
    spreads = {'L0_ffn_router_b1': (0.0, 0.1),
     'L0_ffn_router_b2': (0.0, 0.1),
     'L0_ffn_expert_b1': (0.0, 0.64),
     'L0_ffn_expert_b2': (0.0, 0.289),
     'L0_ffn_expert_b3': (0.0, 0.1),
     'L1_gnn_b': (0.0, 0.1),
     'L1_ffn_gate_b': (0.0, 0.295),
     'L1_ffn_b1': (0.0, 0.8),
     'L1_ffn_b2': (0.0, 0.1),
     'L1_ffn_gamma': (1.0, 0.2),
     'L1_ffn_beta': (0.0, 0.1)}
    factors = {}
    for name, (base, spread) in spreads.items():
        noise = np.random.default_rng([zlib.crc32(name.encode()), seed]).standard_normal(out[name].shape)
        drawn = base * np.exp(spread * noise) if base else spread * noise
        out[name] = jnp.asarray(drawn.astype(out[name].dtype))
    for name, factor in factors.items():
        out[name] = (out[name] * factor).astype(out[name].dtype)
    return out
```

```python
from contextlib import ExitStack

import numpy as np
import concourse.bass as bass
from concourse import mybir

F32 = mybir.dt.float32
BF16 = mybir.dt.bfloat16
I32 = mybir.dt.int32
U32 = mybir.dt.uint32
ALU = mybir.AluOpType
ACT = mybir.ActivationFunctionType
AX_X = mybir.AxisListType.X

N, E, D = 3125, 103125, 256
HEADS, HD = 8, 32
TP, NT = 125, 25
GT = 4
GE = GT * 128
NG = -(-E // GE)
NG2 = NG // 2
ETILES = -(-E // 128)
CH = 7
W32, W64 = 32, 64
NPAD = N + W64
FTW = D + HEADS
BIG = 1.0e30
BT = 5
NB = NT // BT
TOK = BT * TP
CUTS = ((0, 313), (313, 312))
EPS = 1e-5
OPEN = 1
assert NG % 2 == 0 and TP * NT == N and (CH - 1) * 128 < NG * GT <= CH * 128


def bc(ap, axis, n):
    a = ap.unsqueeze(axis)
    shape = list(a.shape)
    shape[axis] = n
    return a.broadcast_to(shape)


def rows(ap, n):
    return ap.partition_broadcast(n)


def open_counts(sp, *sems):
    for sem in sems:
        for one in sem if isinstance(sem, list) else [sem]:
            sp.sem_inc(one, OPEN)


def stage_edges(nc, s):
    with ExitStack() as ctx:
        sem = lambda name: ctx.enter_context(nc.semaphore("e_" + name))
        sb = lambda name, shape, dt: ctx.enter_context(nc.sbuf_tensor("e_" + name, shape, dt))
        d_rows, s_rows = sb("d_rows", [128, CH, 128], I32), sb("s_rows", [128, CH, 128], I32)
        d_f, s_f = sb("d_f", [128, CH, 128], F32), sb("s_f", [128, CH, 128], F32)
        tail = sb("tail", [1, 512], I32)
        zrow = sb("zrow", [W64, 24], F32)
        d_grp = sb("d_grp", [NG2, 2, GE], I32)
        low = sb("low", [NG2, 2, GE], F32)
        ext = sb("ext", [NG2, 2, 2], F32)
        span = sb("span", [128, NG], F32)
        smax = sb("smax", [128, 1], F32)
        ioti = sb("ioti", [128, W64], I32)
        parti = sb("parti", [128, 2], I32)
        cleared, padded, loaded, floats, turned, stats, stored, spread, pool_c = [
            sem(n) for n in ("cleared", "padded", "loaded", "floats", "turned", "stats", "stored", "spread", "pool_c")]
        ps = s.ps
        full = ETILES - 1
        rest = E - full * 128
        block = ctx.enter_context(nc.Block())

        @block.gpsimd
        def _(pool):
            nc.gpsimd.memset(tail[:], -1).then_inc(cleared, 1)
            nc.gpsimd.memset(s.sel[:], 0.0)
            nc.gpsimd.memset(s.tick[:], 0.0)
            nc.gpsimd.memset(s_rows[:, CH - 1, :], 0).then_inc(cleared, 1)
            nc.gpsimd.memset(d_rows[:, CH - 1, :], -1).then_inc(cleared, 1)
            nc.gpsimd.memset(zrow[:], 0.0).then_inc(cleared, 1)
            nc.gpsimd.memset(s.ident[:], 0.0)
            pool.drain()
            nc.gpsimd.affine_select(out=s.ident[:], in_=s.ident[:], compare_op=ALU.not_equal, fill=1.0, base=0,
                                    pattern=[[-1, 128]], channel_multiplier=1).then_inc(pool_c, 1)
            nc.gpsimd.affine_select(out=s.sel[:], in_=s.sel[:], compare_op=ALU.not_equal, fill=1.0, base=0,
                                    pattern=[[-1, HEADS], [-HEADS, GT], [0, W32]], channel_multiplier=1)
            nc.gpsimd.iota(ioti[:], pattern=[[1, W64]], base=0, channel_multiplier=0).then_inc(pool_c, 1)
            nc.gpsimd.iota(parti[:, 0:1], pattern=[[1, 1]], base=0, channel_multiplier=1).then_inc(pool_c, 1)
            for j in range(GT):
                pool.drain()
                nc.gpsimd.iota(parti[32 * j:32 * j + 32, 1:2], pattern=[[1, 1]], base=0,
                               channel_multiplier=1).then_inc(pool_c, 1)

        @block.sync
        def _(sp):
            sp.wait_ge(cleared, 4)
            sp.dma_start(s.dpad[0:E], s.dst).then_inc(padded, 16)
            sp.dma_start(s.dpad[E:NG * GE], tail[0:1, 0:NG * GE - E]).then_inc(padded, 16)
            sp.dma_start(s.tab[N:N + W64, :], zrow[:]).then_inc(padded, 16)
            for c in range(CH - 1):
                sp.dma_start(s_rows[:, c, :], s.src[c * 16384:(c + 1) * 16384].rearrange("(p e) -> p e", e=128)).then_inc(loaded, 16)
            a = (CH - 1) * 16384
            sp.dma_start(s_rows[0:full - 128 * (CH - 1), CH - 1, :], s.src[a:full * 128].rearrange("(p e) -> p e", e=128)).then_inc(loaded, 16)
            r = full - 128 * (CH - 1)
            sp.dma_start(s_rows[r:r + 1, CH - 1, 0:rest], s.src[full * 128:E].rearrange("(p e) -> p e", p=1)).then_inc(loaded, 16)
            sp.wait_ge(padded, 48)
            for c in range(CH):
                n = min(128, NG * GT - c * 128)
                sp.dma_start(d_rows[0:n, c, :], s.dpad[c * 16384:c * 16384 + n * 128].rearrange("(p e) -> p e", e=128)).then_inc(loaded, 16)
            sp.dma_start(d_grp[:], s.dpad[0:NG * GE].rearrange("(q p e) -> p q e", q=2, e=GE)).then_inc(loaded, 16)
            sp.wait_ge(stats, 1)
            with nc.allow_non_contiguous_dma(reason="one number per group"):
                for q in range(2):
                    sp.dma_start(s.grp[q * NG2:(q + 1) * NG2, :], ext[:, q, :]).then_inc(stored, 16)
            sp.wait_ge(stored, 32)
            sp.dma_start(s.gmm[:], rows(s.grp.rearrange("g m -> (g m)"), 128)).then_inc(spread, 16)
            sp.wait_ge(spread, 16)

        @block.vector
        def _(dve):
            dve.wait_ge(loaded, 16 * (CH + 1 + CH + 1))
            nc.vector.tensor_copy(s_f[:], s_rows[:]).then_inc(floats, 1)
            nc.vector.tensor_copy(d_f[:], d_rows[:]).then_inc(floats, 1)
            nc.vector.tensor_scalar(low[:], d_grp[:], 0.0, 8192.0, ALU.is_lt, ALU.mult)
            dve.drain()
            nc.vector.tensor_tensor(low[:], low[:], d_grp[:], ALU.add)
            dve.drain()
            nc.vector.tensor_reduce(ext[:, :, 0:1], low[:], AX_X, ALU.min)
            nc.vector.tensor_reduce(ext[:, :, 1:2], d_grp[:], AX_X, ALU.max)
            dve.drain()
            nc.vector.tensor_copy(smax[0:1, :], ext[0:1, 0, 0:1]).then_inc(stats, 1)
            dve.wait_ge(pool_c, 7)
            nc.vector.tensor_copy(s.iota64[:], ioti[:])
            nc.vector.tensor_copy(s.part[:], parti[:])
            nc.vector.tensor_copy(s.identb[:], s.ident[:])
            nc.vector.memset(s.ones[:], 1.0)
            dve.wait_ge(turned, 1)
            nc.vector.tensor_copy(s.scol[:], ps[:, 0:2, :].rearrange("p b c -> p (b c)")[:, 0:CH * 128])
            nc.vector.tensor_copy(s.dcol[:], ps[:, 2:4, :].rearrange("p b c -> p (b c)")[:, 0:CH * 128])
            dve.wait_ge(spread, 16)
            g = s.gmm[:].rearrange("p (g m) -> p g m", m=2)
            nc.vector.tensor_tensor(span[:], g[:, :, 1], g[:, :, 0], ALU.subtract)
            dve.drain()
            nc.vector.tensor_reduce(smax[:], span[:], AX_X, ALU.max)
            dve.drain()
            nc.vector.tensor_copy(s.widest[:], smax[:])

        @block.tensor
        def _(pe):
            pe.wait_ge(pool_c, 7)
            pe.wait_ge(floats, 2)
            for k, f in ((0, s_f), (2, d_f)):
                for c in range(CH):
                    o = ps[:, k + c // 4, 128 * (c % 4):128 * (c % 4) + 128]
                    last = nc.tensor.transpose(o, f[:, c, :], s.ident[:])
            last.then_inc(turned, 1)


def stage_project(nc, s):
    with ExitStack() as ctx:
        sem = lambda name: ctx.enter_context(nc.semaphore("p_" + name))
        sb = lambda name, shape, dt: ctx.enter_context(nc.sbuf_tensor("p_" + name, shape, dt))
        wide = sb("wide", [128, 2, D + 2 * HEADS], F32)
        prod = sb("prod", [128, 2, D], F32)
        attn = sb("attn", [128, 2, D], F32)
        st6, mv = sb("st6", [TP, NT, 6], F32), sb("mv", [TP, NT, 2], F32)
        eps, half, rstd = sb("eps", [TP, NT], F32), sb("half", [TP, NT], F32), sb("rstd", [TP, NT], F32)
        xn, xT, row = sb("xn", [TP, D], F32), sb("xT", [128, 2, TP], F32), sb("row", [TP, FTW], F32)
        x_in, w_in, moments, scales, xn_ready, turned, xT_ready, summed, row_ready, row_out, row_free = [
            sem(n) for n in ("x_in", "w_in", "moments", "scales", "xn_ready", "turned", "xT_ready", "summed", "row_ready", "row_out", "row_free")]
        ps = s.ps
        block = ctx.enter_context(nc.Block())

        @block.sync
        def _(sp):
            open_counts(sp, moments, scales, xn_ready, turned, xT_ready, summed, row_ready, row_free)
            sp.dma_start(s.x[:], s.x_dram.rearrange("(t p) d -> p t d", p=TP)).then_inc(x_in, 16)
            sp.dma_start(wide[:, :, 0:D], s.W.rearrange("(c k) n -> k c n", k=128)).then_inc(w_in, 16)
            sp.dma_start(attn[:, 0, :], rows(s.attn_l.rearrange("h d -> (h d)"), 128)).then_inc(w_in, 16)
            sp.dma_start(attn[:, 1, :], rows(s.attn_r.rearrange("h d -> (h d)"), 128)).then_inc(w_in, 16)
            with sp.Fori(0, NT) as t:
                sp.wait_ge(row_ready, OPEN + t + 1)
                sp.dma_start(s.ftab[bass.ds(t * TP, TP), :], row[:]).then_inc(row_out, 16)
                sp.dma_start(s.a1tab[bass.ds(t * TP, TP), :], row[:, D:FTW]).then_inc(row_out, 16)
                sp.wait_ge(row_out, 32 * t + 32)
                sp.sem_inc(row_free, 1)

        @block.gpsimd
        def _(pool):
            pool.wait_ge(moments, OPEN + 1)
            nc.gpsimd.tensor_tensor(rstd[:], eps[:], half[:], ALU.pow).then_inc(scales, 1)

        @block.vector
        def _(dve):
            dve.wait_ge(w_in, 48)
            for side in range(2):
                nc.vector.tensor_tensor(prod[:], wide[:, :, 0:D], bc(attn[:, side, :], 1, 2), ALU.mult)
                dve.drain()
                for c in range(2):
                    nc.vector.tensor_reduce(wide[:, c, D + HEADS * side:D + HEADS * (side + 1)],
                                            prod[:, c, :].rearrange("p (h d) -> p h d", h=HEADS), AX_X, ALU.add)
                dve.drain()
            dve.wait_ge(x_in, 16)
            ln_moments(nc, dve, s.x, st6, mv, eps, half)
            nc.vector.memset(s.ndT[:], -BIG).then_inc(moments, 1)
            dve.wait_ge(scales, OPEN + 1)
            with dve.Fori(0, NT) as t:
                dve.wait_ge(turned, OPEN + t)
                nc.vector.tensor_scalar(xn[:], s.x[:, bass.ds(t, 1), :].rearrange("p t d -> p (t d)"),
                                        mv[:, bass.ds(t, 1), 0], rstd[:, bass.ds(t, 1)],
                                        ALU.subtract, ALU.mult).then_inc(xn_ready, 1)

        @block.tensor
        def _(pe):
            with pe.Fori(0, NT) as t:
                pe.wait_ge(xn_ready, OPEN + t + 1)
                pe.wait_ge(xT_ready, OPEN + t)
                for c in range(2):
                    last = nc.tensor.transpose(ps[:, 0, c * 128:c * 128 + TP], xn[:, c * 128:(c + 1) * 128], s.ident[0:TP, 0:TP])
                last.then_inc(turned, 1)
                pe.wait_ge(xT_ready, OPEN + t + 1)
                pe.wait_ge(row_ready, OPEN + t)
                for c in range(2):
                    last = nc.tensor.matmul(ps[0:TP, 1, 0:D + 2 * HEADS], xT[:, c, :], wide[:, c, :], start=c == 0, stop=c == 1)
                last.then_inc(summed, 1)

        @block.scalar
        def _(act):
            with act.Fori(0, NT) as t:
                act.wait_ge(turned, OPEN + t + 1)
                act.wait_ge(summed, OPEN + t)
                nc.scalar.copy(xT[:], ps[:, 0, 0:256].rearrange("p (c n) -> p c n", c=2)[:, :, 0:TP]).then_inc(xT_ready, 1)
                act.wait_ge(summed, OPEN + t + 1)
                act.wait_ge(row_free, OPEN + t)
                nc.scalar.copy(s.a2[:, bass.ds(t, 1), :].rearrange("p t h -> p (t h)"), ps[0:TP, 1, FTW:FTW + HEADS])
                nc.scalar.copy(row[:], ps[0:TP, 1, 0:FTW]).then_inc(row_ready, 1)


def ln_moments(nc, dve, x, st6, mv, eps, half):
    with dve.Fori(0, NT) as t:
        nc.vector.bn_stats(st6[:, bass.ds(t, 1), :].rearrange("p t k -> p (t k)"),
                           x[:, bass.ds(t, 1), :].rearrange("p t d -> p (t d)"))
    dve.drain()
    for t in range(NT):
        nc.vector.bn_aggr(mv[:, t, :], st6[:, t, :])
    dve.drain()
    nc.vector.tensor_scalar(eps[:], mv[:, :, 1], EPS, None, ALU.add)
    nc.vector.memset(half[:], -0.5)
    dve.drain()


def passes(eng, s, width):
    return eng.value_load(s.widest[0:1, 0:1], min_val=0, max_val=N - 1) // width + 1


def gather_rows(nc, pool, s, width, sidx, dest, table, idx_ready, gathered, free):
    with pool.Fori(0, passes(pool, s, width)) as r:
        with pool.Fori(0, NG2) as k:
            i = r * NG2 + k
            for u in range(2):
                pool.wait_ge(free[u], OPEN + i)
                nc.gpsimd.tensor_copy(sidx[u][:], s.scol[:, bass.ds(k * (2 * GT) + u * GT, GT)]).then_inc(idx_ready[u], 1)
                pool.wait_ge(idx_ready[u], OPEN + i + 1)
                nc.gpsimd.tensor_tensor(s.tick[0:1, u:u + 1], s.tick[0:1, 2:3], s.tick[0:1, 3:4], ALU.add)
                for j in range(GT):
                    nc.gpsimd.indirect_dma_start(out=dest[u][:, j, :], out_offset=None, in_=table,
                                                 in_offset=bass.IndirectOffsetOnAxis(ap=sidx[u][:, j:j + 1], axis=0)
                                                 ).then_inc(gathered[u], 16)


def stage_maxima(nc, s):
    with ExitStack() as ctx:
        sem = lambda name: ctx.enter_context(nc.semaphore("m_" + name))
        sb = lambda name, shape, dt: ctx.enter_context(nc.sbuf_tensor("m_" + name, shape, dt))
        sidx = [sb(f"sidx{u}", [128, GT], I32) for u in range(2)]
        a1g = [sb(f"a1g{u}", [128, GT, HEADS], F32) for u in range(2)]
        a1T = [sb(f"a1T{u}", [GT * HEADS, 128], F32) for u in range(2)]
        drow = [sb(f"drow{u}", [128, 128], I32) for u in range(2)]
        mask = [sb(f"mask{u}", [128, 128], BF16) for u in range(2)]
        mx = [sb(f"mx{u}", [128, HEADS], F32) for u in range(2)]
        win = [sb(f"win{u}", [HEADS, W32], F32) for u in range(2)]
        first = sb("first", [128, NG], F32)
        firstw = sb("firstw", [128, NG], F32)
        base = sb("base", [1, NG], I32)
        tabs = sb("tabs", [TP, NT, 24], F32)
        z = sb("z", [TP, NT, HEADS], F32)
        two = lambda name: [sem(f"{name}{u}") for u in range(2)]
        idx_ready, gathered, turned, a1T_ready, d_in, mask_ready, spread, mx_ready, mxT_ready = map(
            two, ("idx_ready", "gathered", "turned", "a1T_ready", "d_in", "mask_ready", "spread", "mx_ready", "mxT_ready"))
        maxima, nodes_turned, tab_ready, tab_out = [sem(n) for n in ("maxima", "nodes_turned", "tab_ready", "tab_out")]
        ps = s.ps
        wide = [ps[:, 2 * u:2 * u + 2, :].rearrange("p b c -> p (b c)").rearrange("p (h e) -> p h e", h=HEADS) for u in range(2)]
        block = ctx.enter_context(nc.Block())

        @block.gpsimd
        def _(pool):
            gather_rows(nc, pool, s, W32, sidx, a1g, s.a1tab, idx_ready, gathered, turned)

        @block.sync
        def _(sp):
            open_counts(sp, idx_ready, turned, a1T_ready, mask_ready, spread, mx_ready, mxT_ready, maxima, nodes_turned, tab_ready)
            with sp.Fori(0, passes(sp, s, W32)) as r:
                with sp.Fori(0, NG2) as k:
                    i = r * NG2 + k
                    for u in range(2):
                        sp.wait_ge(mask_ready[u], OPEN + i)
                        e = s.dpad[bass.ds(k * 2 * GE + u * GE, GE)].rearrange("(j e) -> j e", j=GT)
                        sp.dma_start(drow[u][:], bc(e, 1, W32)).then_inc(d_in[u], 16)
            sp.wait_ge(tab_ready, OPEN + 1)
            sp.dma_start(s.tab[0:N, :].rearrange("(t p) c -> p t c", p=TP), tabs[:]).then_inc(tab_out, 16)
            sp.wait_ge(tab_out, 16)

        @block.tensor
        def _(pe):
            with pe.Fori(0, passes(pe, s, W32)) as r:
                with pe.Fori(0, NG2) as k:
                    i = r * NG2 + k
                    for u in range(2):
                        pe.wait_ge(gathered[u], i * 16 * GT + 16 * GT)
                        pe.wait_ge(a1T_ready[u], OPEN + i)
                        nc.tensor.transpose(ps[0:GT * HEADS, 4 + u, 0:128], a1g[u][:].rearrange("p j h -> p (j h)"),
                                            s.ident[:]).then_inc(turned[u], 1)
                    for u in range(2):
                        pe.wait_ge(a1T_ready[u], OPEN + i + 1)
                        pe.wait_ge(mask_ready[u], OPEN + i + 1)
                        pe.wait_ge(mx_ready[u], OPEN + i)
                        for h in range(HEADS):
                            nc.tensor.matmul(wide[u][:, h, :], s.sel[:, h, :], a1T[u][:], start=h % 4 == 0, stop=False, skip_group_check=True)
                        for h in range(HEADS):
                            last = nc.tensor.matmul(wide[u][:, h, :], s.identb[:], mask[u][:], start=False, stop=True, skip_group_check=True)
                        last.then_inc(spread[u], 1)
                    for u in range(2):
                        pe.wait_ge(mx_ready[u], OPEN + i + 1)
                        nc.tensor.transpose(ps[0:HEADS, 6 + u, 0:128], mx[u][:], s.ident[:]).then_inc(mxT_ready[u], 1)
            pe.wait_ge(maxima, OPEN + 1)
            for t in range(NT):
                last = nc.tensor.transpose(ps[0:TP, 0, t * HEADS:(t + 1) * HEADS], s.ndT[0:HEADS, t * TP:(t + 1) * TP], s.ident[0:HEADS, 0:HEADS])
            last.then_inc(nodes_turned, 1)

        @block.scalar
        def _(act):
            with act.Fori(0, passes(act, s, W32)) as r:
                with act.Fori(0, NG2) as k:
                    i = r * NG2 + k
                    for u in range(2):
                        act.wait_ge(turned[u], OPEN + i + 1)
                        act.wait_ge(spread[u], OPEN + i)
                        nc.scalar.copy(a1T[u][:], ps[0:GT * HEADS, 4 + u, 0:128]).then_inc(a1T_ready[u], 1)

        @block.vector
        def _(dve):
            start_windows(nc, dve, s, first, firstw, 1)
            with dve.Fori(0, passes(dve, s, W32)) as r:
                nc.vector.tensor_scalar(base[:], first[0:1, :], float(N), None, ALU.min)
                dve.drain()
                with dve.Fori(0, NG2) as k:
                    i = r * NG2 + k
                    for u in range(2):
                        dve.wait_ge(d_in[u], i * 16 + 16)
                        dve.wait_ge(spread[u], OPEN + i)
                        nc.vector.tensor_scalar(mask[u][:], drow[u][:], firstw[:, bass.ds(k * 2 + u, 1)], -BIG,
                                                ALU.not_equal, ALU.mult).then_inc(mask_ready[u], 1)
                    for u in range(2):
                        dve.wait_ge(spread[u], OPEN + i + 1)
                        dve.wait_ge(mxT_ready[u], OPEN + i)
                        nc.vector.tensor_reduce(mx[u][:], wide[u], AX_X, ALU.max).then_inc(mx_ready[u], 1)
                    for u in range(2):
                        dve.wait_ge(mxT_ready[u], OPEN + i + 1)
                        nc.vector.tensor_reduce(win[u][:], ps[0:HEADS, 6 + u, 0:128].rearrange("h (j w) -> h w j", j=GT), AX_X, ALU.max)
                    for u in range(2):
                        at = dve.value_load(base[0:1, bass.ds(k * 2 + u, 1)], min_val=0, max_val=N)
                        w = s.ndT[0:HEADS, bass.ds(at, W32)]
                        dve.drain()
                        nc.vector.tensor_tensor(w, w, win[u][:], ALU.max)
                next_windows(nc, dve, first, firstw, W32)
            nc.vector.memset(tabs[:], 1.0).then_inc(maxima, 1)
            dve.wait_ge(nodes_turned, OPEN + 1)
            nc.vector.tensor_tensor(z[:], s.a2[:], ps[0:TP, 0, 0:NT * HEADS].rearrange("p (t h) -> p t h", t=NT), ALU.add)
            dve.drain()
            nc.vector.scalar_tensor_tensor(out=tabs[:, :, HEADS:2 * HEADS], in0=z[:], scalar=0.2, in1=z[:], op0=ALU.mult, op1=ALU.max)
            nc.vector.tensor_copy(tabs[:, :, 0:HEADS], s.a2[:])
            nc.vector.memset(s.accT[:], 0.0)
            nc.vector.memset(s.ndT[:], 0.0)
            dve.drain()
            nc.vector.memset(z[:], 0.0).then_inc(tab_ready, 1)


def start_windows(nc, dve, s, first, firstw, col):
    g = s.gmm[:].rearrange("p (g m) -> p g m", m=2)
    nc.vector.tensor_copy(first[:], g[:, :, 0])
    nc.vector.tensor_scalar(firstw[:], g[:, :, 0], s.part[:, col:col + 1], None, ALU.add)
    dve.drain()


def next_windows(nc, dve, first, firstw, width):
    dve.drain()
    nc.vector.tensor_scalar(first[:], first[:], float(width), None, ALU.add)
    nc.vector.tensor_scalar(firstw[:], firstw[:], float(width), None, ALU.add)
    dve.drain()


def stage_attend(nc, s):
    with ExitStack() as ctx:
        sem = lambda name: ctx.enter_context(nc.semaphore("w_" + name))
        sb = lambda name, shape, dt: ctx.enter_context(nc.sbuf_tensor("w_" + name, shape, dt))
        two_sb = lambda name, shape, dt: [sb(f"{name}{u}", shape, dt) for u in range(2)]
        sidx, ftg = two_sb("sidx", [128, GT], I32), two_sb("ftg", [128, GT, FTW], F32)
        drow, ohT = two_sb("drow", [W64, GE], I32), two_sb("ohT", [W64, GE], F32)
        tabw = two_sb("tabw", [W64, 24], F32)
        z, pen, zl = two_sb("z", [128, GT, HEADS], F32), two_sb("pen", [128, GT, HEADS], F32), two_sb("zl", [128, GT, HEADS], F32)
        arg = two_sb("arg", [128, GT, HEADS], F32)
        ex = two_sb("ex", [128, GT, HEADS + 1], F32)
        drel, oh = two_sb("drel", [128, GT], F32), two_sb("oh", [128, GT, W64], F32)
        msg = two_sb("msg", [128, GT, D], F32)
        first, firstw, base = sb("first", [128, NG], F32), sb("firstw", [128, NG], F32), sb("base", [1, NG], I32)
        two = lambda name: [sem(f"{name}{u}") for u in range(2)]
        idx_ready, gathered, d_in, tab_in, ohT_ready, looked, arg_ready, ex_ready, msg_ready, summed, added = map(
            two, ("idx_ready", "gathered", "d_in", "tab_in", "ohT_ready", "looked", "arg_ready", "ex_ready", "msg_ready", "summed", "added"))
        base_ready, ones_ready = sem("base_ready"), sem("ones_ready")
        ps = s.ps
        look = [ps[:, u, 0:GT * 24].rearrange("p (j c) -> p j c", j=GT) for u in range(2)]
        acc = [ps[:, 2 + u, 0:3 * W64].rearrange("p (c w) -> p c w", c=3) for u in range(2)]
        block = ctx.enter_context(nc.Block())

        @block.gpsimd
        def _(pool):
            gather_rows(nc, pool, s, W64, sidx, ftg, s.ftab, idx_ready, gathered, msg_ready)

        @block.sync
        def _(sp):
            open_counts(sp, idx_ready, ohT_ready, looked, arg_ready, ex_ready, msg_ready, summed, added, base_ready, ones_ready)
            with sp.Fori(0, passes(sp, s, W64)) as r:
                with sp.Fori(0, NG2) as k:
                    i = r * NG2 + k
                    for u in range(2):
                        sp.wait_ge(base_ready, OPEN + r + 1)
                        sp.wait_ge(ohT_ready[u], OPEN + i)
                        sp.dma_start(drow[u][:], rows(s.dpad[bass.ds(k * 2 * GE + u * GE, GE)], W64)).then_inc(d_in[u], 16)
                        sp.wait_ge(looked[u], OPEN + i)
                        at = sp.value_load(base[0:1, bass.ds(k * 2 + u, 1)], min_val=0, max_val=N)
                        sp.dma_start(tabw[u][:], s.tab[bass.ds(at, W64), :]).then_inc(tab_in[u], 16)

        @block.tensor
        def _(pe):
            pe.wait_ge(ones_ready, OPEN + 1)
            with pe.Fori(0, passes(pe, s, W64)) as r:
                with pe.Fori(0, NG2) as k:
                    i = r * NG2 + k
                    for u in range(2):
                        pe.wait_ge(ohT_ready[u], OPEN + i + 1)
                        pe.wait_ge(tab_in[u], i * 16 + 16)
                        pe.wait_ge(arg_ready[u], OPEN + i)
                        for j in range(GT):
                            last = nc.tensor.matmul(look[u][:, j, :], ohT[u][:, j * 128:(j + 1) * 128], tabw[u][:], start=True, stop=True)
                        last.then_inc(looked[u], 1)
                    for u in range(2):
                        pe.wait_ge(msg_ready[u], OPEN + i + 1)
                        pe.wait_ge(added[u], OPEN + i)
                        for c in range(2):
                            for j in range(GT):
                                nc.tensor.matmul(acc[u][:, c, :], msg[u][:, j, c * 128:(c + 1) * 128], oh[u][:, j, :], start=j == 0, stop=j == GT - 1)
                        for j in range(GT):
                            last = nc.tensor.matmul(acc[u][0:HEADS + 1, 2, :], ex[u][:, j, :], oh[u][:, j, :], start=j == 0, stop=j == GT - 1)
                        last.then_inc(summed[u], 1)

        @block.scalar
        def _(act):
            act.wait_ge(ones_ready, OPEN + 1)
            with act.Fori(0, passes(act, s, W64)) as r:
                with act.Fori(0, NG2) as k:
                    i = r * NG2 + k
                    for u in range(2):
                        act.wait_ge(arg_ready[u], OPEN + i + 1)
                        act.wait_ge(summed[u], OPEN + i)
                        nc.scalar.activation(ex[u][:, :, 0:HEADS], arg[u][:], ACT.Exp).then_inc(ex_ready[u], 1)

        @block.vector
        def _(dve):
            for u in range(2):
                nc.vector.memset(ex[u][:], 1.0)
            start_windows(nc, dve, s, first, firstw, 0)
            nc.vector.memset(z[0][:], 0.0).then_inc(ones_ready, 1)
            with dve.Fori(0, passes(dve, s, W64)) as r:
                nc.vector.tensor_scalar(base[:], first[0:1, :], float(N), None, ALU.min).then_inc(base_ready, 1)
                dve.drain()
                with dve.Fori(0, NG2) as k:
                    i = r * NG2 + k
                    for u in range(2):
                        dve.wait_ge(d_in[u], i * 16 + 16)
                        dve.wait_ge(looked[u], OPEN + i)
                        nc.vector.tensor_scalar(ohT[u][:], drow[u][:], firstw[0:W64, bass.ds(k * 2 + u, 1)], None,
                                                ALU.is_equal).then_inc(ohT_ready[u], 1)
                    for u in range(2):
                        nc.vector.tensor_scalar(drel[u][:], s.dcol[:, bass.ds(k * 2 * GT + u * GT, GT)], first[:, bass.ds(k * 2 + u, 1)], None, ALU.subtract)
                        dve.wait_ge(gathered[u], i * 16 * GT + 16 * GT)
                        dve.wait_ge(looked[u], OPEN + i + 1)
                        nc.vector.tensor_tensor(z[u][:], ftg[u][:, :, D:FTW], look[u][:, :, 0:HEADS], ALU.add)
                        nc.vector.tensor_scalar(pen[u][:], look[u][:, :, 2 * HEADS:3 * HEADS], 1.0, BIG, ALU.subtract, ALU.mult)
                        dve.drain()
                        nc.vector.scalar_tensor_tensor(out=zl[u][:], in0=z[u][:], scalar=0.2, in1=z[u][:], op0=ALU.mult, op1=ALU.max)
                        dve.wait_ge(summed[u], OPEN + i)
                        nc.vector.tensor_tensor(oh[u][:], bc(s.iota64[:], 1, GT), bc(drel[u][:], 2, W64), ALU.is_equal)
                        dve.drain()
                        dve.wait_ge(ex_ready[u], OPEN + i)
                        nc.vector.tensor_tensor(z[u][:], zl[u][:], look[u][:, :, HEADS:2 * HEADS], ALU.subtract)
                        dve.drain()
                        nc.vector.tensor_tensor(arg[u][:], z[u][:], pen[u][:], ALU.min).then_inc(arg_ready[u], 1)
                    for u in range(2):
                        dve.wait_ge(ex_ready[u], OPEN + i + 1)
                        nc.vector.tensor_tensor(msg[u][:].rearrange("p j (h d) -> p j h d", h=HEADS),
                                                ftg[u][:, :, 0:D].rearrange("p j (h d) -> p j h d", h=HEADS),
                                                bc(ex[u][:, :, 0:HEADS], 3, HD), ALU.mult).then_inc(msg_ready[u], 1)
                    for u in range(2):
                        at = dve.value_load(base[0:1, bass.ds(k * 2 + u, 1)], min_val=0, max_val=N)
                        dve.drain()
                        dve.wait_ge(summed[u], OPEN + i + 1)
                        w = s.accT[:, :, bass.ds(at, W64)]
                        nc.vector.tensor_tensor(w, w, acc[u][:, 0:2, :], ALU.add)
                        w = s.ndT[:, bass.ds(at, W64)]
                        nc.vector.tensor_tensor(w, w, acc[u][0:HEADS + 1, 2, :], ALU.add).then_inc(added[u], 1)
                next_windows(nc, dve, first, firstw, W64)


def normalise(nc, s, prefix, times):
    with ExitStack() as ctx:
        moments, scales = s.moments, s.scales
        sb = lambda name, shape: ctx.enter_context(nc.sbuf_tensor(prefix + name, shape, F32))
        st6, eps, half = sb("st6", [TP, NT, 6]), sb("eps", [TP, NT]), sb("half", [TP, NT])
        block = ctx.enter_context(nc.Block())

        @block.vector
        def _(dve):
            ln_moments(nc, dve, s.x, st6, s.mv, eps, half)
            nc.vector.memset(st6[:], 0.0).then_inc(moments, 1)
            dve.wait_ge(scales, times)

        @block.gpsimd
        def _(pool):
            pool.wait_ge(moments, times)
            nc.gpsimd.tensor_tensor(s.rstd[:], eps[:], half[:], ALU.pow).then_inc(scales, 1)


def tile_of(buf, t):
    return buf[:, bass.ds(t, 1), :].rearrange("p t d -> p (t d)")


def stage_join(nc, s):
    with ExitStack() as ctx:
        sem = lambda name: ctx.enter_context(nc.semaphore("j_" + name))
        sb = lambda name, shape, dt: ctx.enter_context(nc.sbuf_tensor("j_" + name, shape, dt))
        sums, weights = sb("sums", [128, 2, TP], F32), sb("weights", [HEADS + 1, TP], F32)
        rs, v, low, ev, part = sb("rs", [TP, HEADS + 1], F32), sb("v", [TP, D], F32), sb("low", [TP, D], F32), sb("ev", [TP, D], F32), sb("part", [TP, D], F32)
        taken, turned, low_ready, exp_ready, read = [sem(n) for n in ("taken", "turned", "low_ready", "exp_ready", "read")]
        ps = s.ps
        block = ctx.enter_context(nc.Block())

        @block.sync
        def _(sp):
            open_counts(sp, taken, turned, low_ready, exp_ready, read)

        @block.scalar
        def _(act):
            with act.Fori(0, NT) as t:
                act.wait_ge(turned, OPEN + t)
                nc.scalar.copy(weights[:], s.ndT[:, bass.ds(t * TP, TP)])
                nc.scalar.copy(sums[:], s.accT[:, :, bass.ds(t * TP, TP)]).then_inc(taken, 1)
                act.wait_ge(low_ready, OPEN + t + 1)
                nc.scalar.activation(ev[:], low[:], ACT.Exp).then_inc(exp_ready, 1)

        @block.tensor
        def _(pe):
            with pe.Fori(0, NT) as t:
                pe.wait_ge(taken, OPEN + t + 1)
                pe.wait_ge(read, OPEN + t)
                for c in range(2):
                    nc.tensor.transpose(ps[0:TP, 0, c * 128:(c + 1) * 128], sums[:, c, :], s.ident[:])
                nc.tensor.transpose(ps[0:TP, 1, 0:HEADS + 1], weights[:], s.ident[0:HEADS + 1, 0:HEADS + 1]).then_inc(turned, 1)

        @block.vector
        def _(dve):
            with dve.Fori(0, NT) as t:
                dve.wait_ge(turned, OPEN + t + 1)
                nc.vector.tensor_scalar(rs[:, 0:HEADS], ps[0:TP, 1, 0:HEADS], 1e-30, None, ALU.max)
                nc.vector.tensor_scalar(rs[:, HEADS:HEADS + 1], ps[0:TP, 1, HEADS:HEADS + 1], 1.0, None, ALU.max)
                dve.drain()
                nc.vector.reciprocal(rs[:], rs[:])
                dve.drain()
                nc.vector.tensor_tensor(v[:].rearrange("p (h d) -> p h d", h=HEADS), ps[0:TP, 0, 0:D].rearrange("p (h d) -> p h d", h=HEADS),
                                        bc(rs[:, 0:HEADS], 2, HD), ALU.mult).then_inc(read, 1)
                nc.vector.tensor_copy(s.rdeg[:, bass.ds(t, 1)], rs[:, HEADS:HEADS + 1])
                dve.drain()
                nc.vector.tensor_scalar(low[:], v[:], 0.0, None, ALU.min).then_inc(low_ready, 1)
                nc.vector.scalar_tensor_tensor(out=part[:], in0=v[:], scalar=0.0, in1=tile_of(s.x, t), op0=ALU.max, op1=ALU.add)
                dve.drain()
                dve.wait_ge(exp_ready, OPEN + t + 1)
                nc.vector.scalar_tensor_tensor(out=tile_of(s.x, t), in0=ev[:], scalar=-1.0, in1=part[:], op0=ALU.add, op1=ALU.add)
            nc.vector.memset(s.accT[:], 0.0)
    normalise(nc, s, "n1_", 1)


def stage_share(nc, s):
    with ExitStack() as ctx:
        sem = lambda name: ctx.enter_context(nc.semaphore("s_" + name))
        sb = lambda name, shape, dt: ctx.enter_context(nc.sbuf_tensor("s_" + name, shape, dt))
        w, brow = sb("w", [128, 2, D], F32), sb("brow", [1, D], F32)
        h, hT = sb("h", [TP, D], F32), sb("hT", [128, 2, TP], F32)
        w_in, h_ready, h_out, h_free, turned, hT_ready, summed, kept = [sem(n) for n in ("w_in", "h_ready", "h_out", "h_free", "turned", "hT_ready", "summed", "kept")]
        ps = s.ps
        block = ctx.enter_context(nc.Block())

        @block.sync
        def _(sp):
            open_counts(sp, h_ready, h_free, turned, hT_ready, summed, kept)
            sp.dma_start(w[:], s.ins["L1_gnn_W_self"].rearrange("(c k) n -> k c n", k=128)).then_inc(w_in, 16)
            sp.dma_start(brow[:], rows(s.ins["L1_gnn_b"], 1)).then_inc(w_in, 16)
            with sp.Fori(0, NT) as t:
                sp.wait_ge(h_ready, OPEN + t + 1)
                sp.dma_start(s.htab[bass.ds(t * TP, TP), :], h[:]).then_inc(h_out, 16)
                sp.wait_ge(h_out, 16 * t + 16)
                sp.sem_inc(h_free, 1)

        @block.vector
        def _(dve):
            with dve.Fori(0, NT) as t:
                dve.wait_ge(turned, OPEN + t)
                dve.wait_ge(h_free, OPEN + t)
                nc.vector.tensor_scalar(h[:], tile_of(s.x, t), s.mv[:, bass.ds(t, 1), 0], s.rstd[:, bass.ds(t, 1)],
                                        ALU.subtract, ALU.mult).then_inc(h_ready, 1)
                dve.wait_ge(summed, OPEN + t + 1)
                nc.vector.tensor_copy(tile_of(s.own, t), ps[0:TP, 1, 0:D]).then_inc(kept, 1)

        @block.tensor
        def _(pe):
            pe.wait_ge(w_in, 32)
            with pe.Fori(0, NT) as t:
                pe.wait_ge(h_ready, OPEN + t + 1)
                pe.wait_ge(hT_ready, OPEN + t)
                for c in range(2):
                    last = nc.tensor.transpose(ps[:, 0, c * 128:c * 128 + TP], h[:, c * 128:(c + 1) * 128], s.ident[0:TP, 0:TP])
                last.then_inc(turned, 1)
                pe.wait_ge(hT_ready, OPEN + t + 1)
                pe.wait_ge(kept, OPEN + t)
                nc.tensor.matmul(ps[0:TP, 1, 0:D], s.ones[0:1, 0:TP], brow[:], start=True, stop=False)
                for c in range(2):
                    last = nc.tensor.matmul(ps[0:TP, 1, 0:D], hT[:, c, :], w[:, c, :], start=False, stop=c == 1)
                last.then_inc(summed, 1)

        @block.scalar
        def _(act):
            with act.Fori(0, NT) as t:
                act.wait_ge(turned, OPEN + t + 1)
                act.wait_ge(summed, OPEN + t)
                nc.scalar.copy(hT[:], ps[:, 0, 0:256].rearrange("p (c n) -> p c n", c=2)[:, :, 0:TP]).then_inc(hT_ready, 1)


def stage_aggregate(nc, s):
    with ExitStack() as ctx:
        sem = lambda name: ctx.enter_context(nc.semaphore("g_" + name))
        sb = lambda name, shape, dt: ctx.enter_context(nc.sbuf_tensor("g_" + name, shape, dt))
        two_sb = lambda name, shape, dt: [sb(f"{name}{u}", shape, dt) for u in range(2)]
        sidx, hg = two_sb("sidx", [128, GT], I32), two_sb("hg", [128, GT, D], F32)
        drel, oh = two_sb("drel", [128, GT], F32), two_sb("oh", [128, GT, W64], F32)
        first, firstw, base = sb("first", [128, NG], F32), sb("firstw", [128, NG], F32), sb("base", [1, NG], I32)
        two = lambda name: [sem(f"{name}{u}") for u in range(2)]
        idx_ready, gathered, oh_ready, summed, added = map(two, ("idx_ready", "gathered", "oh_ready", "summed", "added"))
        ps = s.ps
        acc = [ps[:, 2 + u, 0:2 * W64].rearrange("p (c w) -> p c w", c=2) for u in range(2)]
        block = ctx.enter_context(nc.Block())

        @block.sync
        def _(sp):
            open_counts(sp, idx_ready, oh_ready, summed, added)

        @block.gpsimd
        def _(pool):
            gather_rows(nc, pool, s, W64, sidx, hg, s.htab, idx_ready, gathered, summed)

        @block.tensor
        def _(pe):
            with pe.Fori(0, passes(pe, s, W64)) as r:
                with pe.Fori(0, NG2) as k:
                    i = r * NG2 + k
                    for u in range(2):
                        pe.wait_ge(oh_ready[u], OPEN + i + 1)
                        pe.wait_ge(added[u], OPEN + i)
                        pe.wait_ge(gathered[u], i * 16 * GT + 16 * GT)
                        for c in range(2):
                            for j in range(GT):
                                last = nc.tensor.matmul(acc[u][:, c, :], hg[u][:, j, c * 128:(c + 1) * 128], oh[u][:, j, :], start=j == 0, stop=j == GT - 1)
                        last.then_inc(summed[u], 1)

        @block.vector
        def _(dve):
            start_windows(nc, dve, s, first, firstw, 0)
            with dve.Fori(0, passes(dve, s, W64)) as r:
                nc.vector.tensor_scalar(base[:], first[0:1, :], float(N), None, ALU.min)
                dve.drain()
                with dve.Fori(0, NG2) as k:
                    i = r * NG2 + k
                    for u in range(2):
                        nc.vector.tensor_scalar(drel[u][:], s.dcol[:, bass.ds(k * 2 * GT + u * GT, GT)], first[:, bass.ds(k * 2 + u, 1)], None, ALU.subtract)
                    dve.drain()
                    for u in range(2):
                        dve.wait_ge(summed[u], OPEN + i)
                        nc.vector.tensor_tensor(oh[u][:], bc(s.iota64[:], 1, GT), bc(drel[u][:], 2, W64), ALU.is_equal).then_inc(oh_ready[u], 1)
                    for u in range(2):
                        at = dve.value_load(base[0:1, bass.ds(k * 2 + u, 1)], min_val=0, max_val=N)
                        dve.drain()
                        dve.wait_ge(summed[u], OPEN + i + 1)
                        w = s.accT[:, :, bass.ds(at, W64)]
                        nc.vector.tensor_tensor(w, w, acc[u], ALU.add).then_inc(added[u], 1)
                next_windows(nc, dve, first, firstw, W64)


def stage_join2(nc, s):
    with ExitStack() as ctx:
        sem = lambda name: ctx.enter_context(nc.semaphore("k_" + name))
        sb = lambda name, shape, dt: ctx.enter_context(nc.sbuf_tensor("k_" + name, shape, dt))
        w, sums, v = sb("w", [128, 2, D], F32), sb("sums", [128, 2, TP], F32), sb("v", [TP, D], F32)
        w_in, taken, summed, read = [sem(n) for n in ("w_in", "taken", "summed", "read")]
        ps = s.ps
        block = ctx.enter_context(nc.Block())

        @block.sync
        def _(sp):
            open_counts(sp, taken, summed, read)
            sp.dma_start(w[:], s.ins["L1_gnn_W_neigh"].rearrange("(c k) n -> k c n", k=128)).then_inc(w_in, 16)

        @block.scalar
        def _(act):
            with act.Fori(0, NT) as t:
                act.wait_ge(summed, OPEN + t)
                nc.scalar.copy(sums[:], s.accT[:, :, bass.ds(t * TP, TP)]).then_inc(taken, 1)

        @block.tensor
        def _(pe):
            pe.wait_ge(w_in, 16)
            with pe.Fori(0, NT) as t:
                pe.wait_ge(taken, OPEN + t + 1)
                pe.wait_ge(read, OPEN + t)
                for c in range(2):
                    last = nc.tensor.matmul(ps[0:TP, 0, 0:D], sums[:, c, :], w[:, c, :], start=c == 0, stop=c == 1)
                last.then_inc(summed, 1)

        @block.vector
        def _(dve):
            with dve.Fori(0, NT) as t:
                dve.wait_ge(summed, OPEN + t + 1)
                nc.vector.scalar_tensor_tensor(out=v[:], in0=ps[0:TP, 0, 0:D], scalar=s.rdeg[:, bass.ds(t, 1)], in1=tile_of(s.own, t),
                                               op0=ALU.mult, op1=ALU.add).then_inc(read, 1)
                dve.drain()
                nc.vector.scalar_tensor_tensor(out=tile_of(s.x, t), in0=v[:], scalar=0.0, in1=tile_of(s.x, t), op0=ALU.max, op1=ALU.add)
                dve.drain()
    normalise(nc, s, "n2_", 3)


class Mixture:

    def __init__(self, prefix, experts, hidden, out, out_chunks, out_bias, width):
        self.prefix, self.experts, self.hidden, self.out = prefix, experts, hidden, out
        self.out_chunks, self.out_bias, self.width = out_chunks, out_bias, width


def stage_mixture(nc, s, m, second):
    X = m.experts
    XP = max(X, 8)
    with ExitStack() as ctx:
        sem = lambda name: ctx.enter_context(nc.semaphore(m.prefix + name))
        sb = lambda name, shape, dt: ctx.enter_context(nc.sbuf_tensor(m.prefix + name, shape, dt))
        xn, xT = sb("xn", [TP, BT, D], F32), sb("xT", [128, 2, TOK], F32)
        h = [sb(f"h{u}", [128, 4, TOK], F32) for u in range(2)]
        wts = [sb(f"wts{u}", [128, m.width], F32) for u in range(2)]
        bias = [sb(f"bias{i}", [128, X, n], F32) for i, (_, _, n, _, _) in enumerate(m.hidden)]
        obias = sb("obias", [X, D], F32)
        gw, gb = sb("gw", [128, 2, 128], F32), sb("gb", [1, 16], F32)
        rh, rb1, rw2 = sb("rh", [128, TOK], F32), sb("rb1", [128, 1], F32), sb("rw2", [128, 16], F32)
        score, mxs, ex, tot = sb("score", [TP, BT, XP], F32), sb("mxs", [TP, BT], F32), sb("ex", [TP, BT, XP], F32), sb("tot", [TP, BT], F32)
        top, topi, chosen = sb("top", [TP, BT, 8], F32), sb("topi", [TP, BT, 8], U32), sb("chosen", [TP, BT, 2], F32)
        gap, q, w12, iox = sb("gap", [TP, BT], F32), sb("q", [TP, BT], F32), sb("w12", [TP, BT, 2], F32), sb("iox", [TP, XP], F32)
        eq, gates, gT = sb("eq", [TP, BT, X], F32), sb("gates", [TP, BT, X], F32), sb("gT", [X, BT, 128], F32)
        two = lambda name: [sem(f"{name}{u}") for u in range(2)]
        w_in, hid_sum, hid_ready = two("w_in"), two("hid_sum"), two("hid_ready")
        out_sum, added = [[sem(f"{n}{k}") for k in range(3)] for n in ("out_sum", "added")]
        consts, xn_ready, turned, xT_ready, scored, gap_in, gap_out, gates_ready, gates_turned, gT_ready = [sem(n) for n in (
            "consts", "xn_ready", "turned", "xT_ready", "scored", "gap_in", "gap_out", "gates_ready", "gates_turned", "gT_ready")]
        if second:
            moments, scales, ob_ready, ob_out, ob_free = [sem(n) for n in ("moments", "scales", "ob_ready", "ob_out", "ob_free")]
            own = [moments, scales, ob_ready, ob_free]
        else:
            rh_sum, rh_ready, exp_in, exp_out = own = [sem(n) for n in ("rh_sum", "rh_ready", "exp_in", "exp_out")]
        if second:
            gamma, beta, ob = sb("gamma", [TP, D], F32), sb("beta", [TP, D], F32), sb("ob", [TP, BT, D], F32)
            st6, mv, eps, half, rstd = sb("st6", [TP, BT, 6], F32), sb("mv", [TP, BT, 2], F32), sb("eps", [TP, BT], F32), sb("half", [TP, BT], F32), sb("rstd", [TP, BT], F32)
        ps = s.ps
        hid = [ps[:, 2 * u:2 * u + 2, :] for u in range(2)]
        outs = ((4, (0, 1)), (5, (2, 3)), (6, (4,)))
        HX = X // 2
        block = ctx.enter_context(nc.Block())

        @block.sync
        def _(sp):
            open_counts(sp, hid_sum, hid_ready, out_sum, added, xn_ready, turned, xT_ready, scored,
                        gap_in, gap_out, gates_ready, gates_turned, gT_ready, own)
            i = s.ins
            cols = nc.allow_non_contiguous_dma(reason="biases by partition")
            if second:
                sp.dma_start(gw[:, :, 0:X], i["L1_ffn_gate_w"].rearrange("(c k) n -> k c n", k=128)).then_inc(consts, 16)
                sp.dma_start(gb[:, 0:X], rows(i["L1_ffn_gate_b"], 1)).then_inc(consts, 16)
                sp.dma_start(gamma[:], rows(i["L1_ffn_gamma"], TP)).then_inc(consts, 16)
                sp.dma_start(beta[:], rows(i["L1_ffn_beta"], TP)).then_inc(consts, 16)
            else:
                sp.dma_start(gw[:], i["L0_ffn_router_w1"].rearrange("(c k) n -> k c n", k=128)).then_inc(consts, 16)
                sp.dma_start(gb[:, 0:X], rows(i["L0_ffn_router_b2"], 1)).then_inc(consts, 16)
                sp.dma_start(rb1[:], i["L0_ffn_router_b1"].rearrange("(p a) -> p a", a=1)).then_inc(consts, 16)
                sp.dma_start(rw2[:, 0:X], i["L0_ffn_router_w2"]).then_inc(consts, 16)
            sp.dma_start(obias[:], i[m.out_bias]).then_inc(consts, 16)
            with cols:
                for k, (_, bname, n, _, _) in enumerate(m.hidden):
                    for c in range(n):
                        src = i[bname][:, c * 128:(c + 1) * 128].rearrange("x p -> p x")
                        d = sp.dma_start(bias[k][:, :, c], src)
                        d.then_inc(consts, 16)
            with sp.Fori(0, NB) as b:
                for x in range(X):
                    u = x % 2
                    sp.wait_ge(out_sum[2], OPEN + b * (X + 1) + x)
                    at = 0
                    for name, _, n, kc, _ in m.hidden:
                        src = i[name][x].rearrange("(c k) n -> k c n", k=128)
                        sp.dma_start(wts[u][:, at:at + kc * n * 128].rearrange("p (c n) -> p c n", c=kc), src).then_inc(w_in[u], 16)
                        at += kc * n * 128
                    src = i[m.out][x].rearrange("(c k) n -> k c n", k=128)
                    sp.dma_start(wts[u][:, at:at + m.out_chunks * D].rearrange("p (c n) -> p c n", c=m.out_chunks), src).then_inc(w_in[u], 16)
                if second:
                    sp.wait_ge(ob_ready, OPEN + b + 1)
                    sp.dma_start(s.out[bass.ds(b * TOK, TOK), :].rearrange("(t p) d -> p t d", p=TP), ob[:]).then_inc(ob_out, 16)
                    sp.wait_ge(ob_out, 16 * b + 16)
                    sp.sem_inc(ob_free, 1)

        @block.gpsimd
        def _(pool):
            if second:
                with pool.Fori(0, NB) as b:
                    pool.wait_ge(moments, OPEN + b + 1)
                    nc.gpsimd.tensor_tensor(rstd[:], eps[:], half[:], ALU.pow).then_inc(scales, 1)

        @block.tensor
        def _(pe):
            pe.wait_ge(consts, 16 * consts_n(m, second))
            with pe.Fori(0, NB) as b:
                pe.wait_ge(xn_ready, OPEN + b + 1)
                for u in range(2):
                    pe.wait_ge(hid_ready[u], OPEN + b * X * 2)
                pe.wait_ge(added[0], OPEN + b * (X + 1))
                for j in range(BT):
                    for c in range(2):
                        last = nc.tensor.transpose(ps[:, j, c * 128:c * 128 + TP], xn[:, j, c * 128:(c + 1) * 128], s.ident[0:TP, 0:TP])
                last.then_inc(turned, 1)
                pe.wait_ge(xT_ready, OPEN + b + 1)
                if second:
                    for j in range(BT):
                        o = ps[0:TP, 7, j * 16:j * 16 + X]
                        for c in range(2):
                            nc.tensor.matmul(o, xT[:, c, j * TP:(j + 1) * TP], gw[:, c, 0:X], start=c == 0, stop=False)
                        last = nc.tensor.matmul(o, s.ones[0:1, 0:TP], gb[0:1, 0:X], start=False, stop=True)
                else:
                    for k, (a, n) in enumerate(CUTS):
                        for c in range(2):
                            last = nc.tensor.matmul(ps[:, k, 0:n], gw[:, c, :], xT[:, c, a:a + n], start=c == 0, stop=c == 1)
                    last.then_inc(rh_sum, 1)
                    pe.wait_ge(rh_ready, OPEN + b + 1)
                    for j in range(BT):
                        o = ps[0:TP, 7, j * 16:j * 16 + X]
                        nc.tensor.matmul(o, rh[:, j * TP:(j + 1) * TP], rw2[:, 0:X], start=True, stop=False)
                        last = nc.tensor.matmul(o, s.ones[0:1, 0:TP], gb[0:1, 0:X], start=False, stop=True)
                last.then_inc(scored, 1)
                pe.wait_ge(gates_ready, OPEN + b + 1)
                for j in range(BT):
                    last = nc.tensor.transpose(ps[0:X, 7 - j // 4, (j % 4) * 128:(j % 4) * 128 + TP], gates[:, j, :], s.ident[0:TP, 0:TP])
                last.then_inc(gates_turned, 1)
                pe.wait_ge(gT_ready, OPEN + b + 1)
                for k, (bank, tiles) in enumerate(outs):
                    pe.wait_ge(added[k], OPEN + b * (X + 1))
                    for a, j in enumerate(tiles):
                        last = nc.tensor.matmul(ps[0:TP, bank, a * D:(a + 1) * D], gT[:, j, 0:TP], obias[:], start=True, stop=True)
                    last.then_inc(out_sum[k], 1)
                for x in range(X):
                    u = x % 2
                    pe.wait_ge(w_in[u], (b * HX + x // 2 + 1) * 16 * (len(m.hidden) + 1))
                    at, q, frm, fro = 0, 0, xT, 0
                    for name, _, n, kc, to in m.hidden:
                        for f in range(n):
                            z = q % 2
                            use = b * (X * 2) + x * 2 + q // 2
                            pe.wait_ge(hid_ready[z], OPEN + use)
                            if frm is not xT and f == 0:
                                for y in range(2):
                                    pe.wait_ge(hid_ready[y], OPEN + use)
                            for c in range(kc):
                                w = wts[u][:, at + c * n * 128 + f * 128:at + c * n * 128 + (f + 1) * 128]
                                for k, (a, nn) in enumerate(CUTS):
                                    last = nc.tensor.matmul(hid[z][:, k, 0:nn], w, frm[:, fro + c, a:a + nn], start=c == 0, stop=c == kc - 1)
                            last.then_inc(hid_sum[z], 1)
                            q += 1
                        at += kc * n * 128
                        frm, fro = h[u], to
                    for y in range(2):
                        pe.wait_ge(hid_ready[y], OPEN + b * (X * 2) + x * 2 + 2)
                    for k, (bank, tiles) in enumerate(outs):
                        pe.wait_ge(added[k], OPEN + b * (X + 1) + x + 1)
                        for a, j in enumerate(tiles):
                            for c in range(m.out_chunks):
                                last = nc.tensor.matmul(ps[0:TP, bank, a * D:(a + 1) * D], h[u][:, fro + c, j * TP:(j + 1) * TP],
                                                        wts[u][:, at + c * D:at + (c + 1) * D], start=c == 0, stop=c == m.out_chunks - 1)
                        last.then_inc(out_sum[k], 1)

        @block.scalar
        def _(act):
            act.wait_ge(consts, 16 * consts_n(m, second))
            with act.Fori(0, NB) as b:
                act.wait_ge(turned, OPEN + b + 1)
                act.wait_ge(out_sum[2], OPEN + b * (X + 1))
                nc.scalar.copy(xT[:].rearrange("p c (j n) -> p j c n", j=BT),
                               ps[:, 0:BT, 0:256].rearrange("p j (c n) -> p j c n", c=2)[:, :, :, 0:TP]).then_inc(xT_ready, 1)
                if not second:
                    act.wait_ge(rh_sum, OPEN + b + 1)
                    for k, (a, n) in enumerate(CUTS):
                        last = nc.scalar.activation(rh[:, a:a + n], ps[:, k, 0:n], ACT.Relu, bias=rb1[:])
                    last.then_inc(rh_ready, 1)
                    act.wait_ge(exp_in, OPEN + b + 1)
                    nc.scalar.activation(ex[:, :, 0:X], score[:, :, 0:X], ACT.Exp).then_inc(exp_out, 1)
                act.wait_ge(gap_in, OPEN + b + 1)
                nc.scalar.activation(q[:], gap[:], ACT.Exp).then_inc(gap_out, 1)
                act.wait_ge(gates_turned, OPEN + b + 1)
                nc.scalar.copy(gT[:, 0:4, 0:TP], ps[0:X, 7, :].rearrange("p (j n) -> p j n", j=4)[:, :, 0:TP])
                nc.scalar.copy(gT[:, 4, 0:TP], ps[0:X, 6, 0:TP]).then_inc(gT_ready, 1)
                for x in range(X):
                    u = x % 2
                    act.wait_ge(out_sum[2], OPEN + b * (X + 1) + x)
                    n = 0
                    for k, (_, _, chunks, _, to) in enumerate(m.hidden):
                        for f in range(chunks):
                            z = n % 2
                            act.wait_ge(hid_sum[z], OPEN + b * (X * 2) + x * 2 + n // 2 + 1)
                            nc.scalar.activation(h[u][:, to + f, 0:CUTS[0][1]], hid[z][:, 0, 0:CUTS[0][1]], ACT.Relu, bias=bias[k][:, x, f:f + 1])
                            nc.scalar.activation(h[u][:, to + f, CUTS[1][0]:TOK], hid[z][:, 1, 0:CUTS[1][1]], ACT.Relu,
                                                 bias=bias[k][:, x, f:f + 1]).then_inc(hid_ready[z], 1)
                            n += 1

        @block.vector
        def _(dve):
            nc.vector.memset(score[:], -1.0)
            nc.vector.tensor_copy(iox[:], s.iota64[0:TP, 0:XP])
            if second:
                nc.vector.memset(half[:], -0.5)
                dve.wait_ge(consts, 16 * consts_n(m, second))
            dve.drain()
            with dve.Fori(0, NB) as b:
                for j in range(BT):
                    t = b * BT + j
                    last = nc.vector.tensor_scalar(xn[:, j, :], tile_of(s.x, t), s.mv[:, bass.ds(t, 1), 0], s.rstd[:, bass.ds(t, 1)],
                                                   ALU.subtract, ALU.mult)
                last.then_inc(xn_ready, 1)
                dve.wait_ge(scored, OPEN + b + 1)
                logits = ps[0:TP, 7, 0:BT * 16].rearrange("p (j x) -> p j x", j=BT)[:, :, 0:X]
                if second:
                    nc.vector.tensor_copy(score[:, :, 0:X], logits)
                else:
                    nc.vector.tensor_reduce(mxs[:], logits, AX_X, ALU.max)
                    dve.drain()
                    nc.vector.tensor_tensor(score[:, :, 0:X], logits, bc(mxs[:], 2, X), ALU.subtract).then_inc(exp_in, 1)
                    dve.wait_ge(exp_out, OPEN + b + 1)
                    nc.vector.tensor_reduce(tot[:], ex[:, :, 0:X], AX_X, ALU.add)
                    dve.drain()
                    nc.vector.reciprocal(tot[:], tot[:])
                    dve.drain()
                    nc.vector.tensor_tensor(score[:, :, 0:X], ex[:, :, 0:X], bc(tot[:], 2, X), ALU.mult)
                dve.drain()
                for j in range(BT):
                    nc.vector.max(top[:, j, :], score[:, j, :])
                dve.drain()
                for j in range(BT):
                    nc.vector.max_index(topi[:, j, :], top[:, j, :], score[:, j, :])
                nc.vector.tensor_tensor(gap[:], top[:, :, 1], top[:, :, 0], ALU.subtract).then_inc(gap_in, 1)
                dve.drain()
                nc.vector.tensor_copy(chosen[:], topi[:, :, 0:2])
                dve.wait_ge(gap_out, OPEN + b + 1)
                nc.vector.tensor_scalar(tot[:], q[:], 1.0, None, ALU.add)
                dve.drain()
                nc.vector.reciprocal(w12[:, :, 0], tot[:])
                dve.drain()
                nc.vector.tensor_tensor(w12[:, :, 1], q[:], w12[:, :, 0], ALU.mult)
                nc.vector.tensor_tensor(gates[:], bc(iox[:, 0:X], 1, BT), bc(chosen[:, :, 0], 2, X), ALU.is_equal)
                nc.vector.tensor_tensor(eq[:], bc(iox[:, 0:X], 1, BT), bc(chosen[:, :, 1], 2, X), ALU.is_equal)
                dve.drain()
                nc.vector.tensor_tensor(gates[:], gates[:], bc(w12[:, :, 0], 2, X), ALU.mult)
                nc.vector.tensor_tensor(eq[:], eq[:], bc(w12[:, :, 1], 2, X), ALU.mult)
                dve.drain()
                nc.vector.tensor_tensor(gates[:], gates[:], eq[:], ALU.add).then_inc(gates_ready, 1)
                dve.drain()
                row = lambda j: xn[:, j, :] if second else tile_of(s.x, b * BT + j)
                for x in range(-1, X):
                    for k, (bank, tiles) in enumerate(outs):
                        dve.wait_ge(out_sum[k], OPEN + b * (X + 1) + x + 2)
                        for a, j in enumerate(tiles):
                            o = ps[0:TP, bank, a * D:(a + 1) * D]
                            if x < 0:
                                last = nc.vector.tensor_tensor(row(j), row(j), o, ALU.add)
                            else:
                                last = nc.vector.scalar_tensor_tensor(out=row(j), in0=o, scalar=gates[:, j, x:x + 1], in1=row(j), op0=ALU.mult, op1=ALU.add)
                        last.then_inc(added[k], 1)
                    dve.drain()
                if second:
                    for j in range(BT):
                        nc.vector.bn_stats(st6[:, j, :], xn[:, j, :])
                    dve.drain()
                    for j in range(BT):
                        nc.vector.bn_aggr(mv[:, j, :], st6[:, j, :])
                    dve.drain()
                    nc.vector.tensor_scalar(eps[:], mv[:, :, 1], EPS, None, ALU.add).then_inc(moments, 1)
                    dve.wait_ge(scales, OPEN + b + 1)
                    dve.wait_ge(ob_free, OPEN + b)
                    for j in range(BT):
                        nc.vector.tensor_scalar(ob[:, j, :], xn[:, j, :], mv[:, j, 0:1], rstd[:, j:j + 1], ALU.subtract, ALU.mult)
                    dve.drain()
                    nc.vector.tensor_tensor(ob[:], ob[:], bc(gamma[:], 1, BT), ALU.mult)
                    dve.drain()
                    nc.vector.tensor_tensor(ob[:], ob[:], bc(beta[:], 1, BT), ALU.add)
                    dve.drain()
                    nc.vector.tensor_tensor(ob[:], ob[:], s.x[:, bass.ds(b * BT, BT), :], ALU.add).then_inc(ob_ready, 1)


def consts_n(m, second):
    return 5 + sum(n for _, _, n, _, _ in m.hidden)


def stage_experts(nc, s):
    m = Mixture("x_", 6, (("L0_ffn_expert_w1", "L0_ffn_expert_b1", 2, 2, 0), ("L0_ffn_expert_w2", "L0_ffn_expert_b2", 2, 2, 2)),
                "L0_ffn_expert_w3", 2, "L0_ffn_expert_b3", 3 * 2 * D)
    stage_mixture(nc, s, m, False)
    normalise(nc, s, "n3_", 2)


def stage_experts2(nc, s):
    m = Mixture("y_", 16, (("L1_ffn_w1", "L1_ffn_b1", 4, 2, 0),), "L1_ffn_w2", 4, "L1_ffn_b2", 2 * 4 * D)
    stage_mixture(nc, s, m, True)


class Shared:
    pass


def program(nc, ins, out, stages=99):
    s = Shared()
    s.x_dram, s.src, s.dst, s.W, s.attn_l, s.attn_r = [ins[n] for n in ("x", "src", "dst", "L0_gnn_W", "L0_gnn_attn_l", "L0_gnn_attn_r")]
    s.ins, s.out = ins, out
    s.dpad = nc.dram_tensor("dpad", (NG * GE,), I32, kind="Internal").ap()
    s.grp = nc.dram_tensor("grp", (NG, 2), F32, kind="Internal").ap()
    s.a1tab = nc.dram_tensor("a1tab", (N, HEADS), F32, kind="Internal").ap()
    s.ftab = nc.dram_tensor("ftab", (N, FTW), F32, kind="Internal").ap()
    s.tab = nc.dram_tensor("tab", (NPAD, 24), F32, kind="Internal").ap()
    s.htab = nc.dram_tensor("htab", (N, D), F32, kind="Internal").ap()
    with ExitStack() as ctx:
        sb = lambda name, shape, dt: ctx.enter_context(nc.sbuf_tensor(name, shape, dt))
        s.moments, s.scales = [ctx.enter_context(nc.semaphore(n)) for n in ("moments", "scales")]
        s.ps = ctx.enter_context(nc.psum_tensor("ps", [128, 8, 512], F32))
        s.ident, s.identb = sb("ident", [128, 128], F32), sb("identb", [128, 128], BF16)
        s.sel = sb("sel", [GT * HEADS, HEADS, 128], F32)
        s.iota64, s.part = sb("iota64", [128, W64], F32), sb("part", [128, 2], F32)
        s.tick = sb("tick", [1, 4], F32)
        s.ones = sb("ones", [1, 128], F32)
        s.dcol, s.scol = sb("dcol", [128, CH * 128], F32), sb("scol", [128, CH * 128], I32)
        s.gmm, s.widest = sb("gmm", [128, 2 * NG], F32), sb("widest", [128, 1], I32)
        s.x = sb("x", [TP, NT, D], F32)
        s.a2 = sb("a2", [TP, NT, HEADS], F32)
        s.accT = sb("accT", [128, 2, NPAD], F32)
        s.ndT = sb("ndT", [HEADS + 1, NPAD], F32)
        s.mv, s.rstd = sb("mv", [TP, NT, 2], F32), sb("rstd", [TP, NT], F32)
        s.rdeg = sb("rdeg", [TP, NT], F32)
        s.own = sb("own", [TP, NT, D], F32)
        for n, stage in enumerate((stage_edges, stage_project, stage_maxima, stage_attend, stage_join, stage_experts, stage_share, stage_aggregate, stage_join2, stage_experts2)):
            if n < stages:
                stage(nc, s)


def kernel(**inputs):
    import concourse.bacc as bacc
    from concourse.bass_utils import run_bass_kernel_spmd

    nc = bacc.Bacc("TRN2", target_bir_lowering=False, num_devices=1)
    arrays, aps = {}, {}
    for name, value in inputs.items():
        a = np.ascontiguousarray(value)
        arrays[f"in_{name}_dram"] = a
        aps[name] = nc.dram_tensor(f"in_{name}_dram", a.shape, mybir.dt.from_np(a.dtype), kind="ExternalInput").ap()
    out = nc.dram_tensor("out_dram", (N, D), F32, kind="ExternalOutput").ap()
    program(nc, aps, out)
    r = run_bass_kernel_spmd(nc, [arrays], core_ids=[0])
    return r.results[0]["out_dram"]
```

```python
from contextlib import ExitStack

import numpy as np
import concourse.bass as bass
from concourse import mybir

F32 = mybir.dt.float32
BF16 = mybir.dt.bfloat16
I32 = mybir.dt.int32
U32 = mybir.dt.uint32
ALU = mybir.AluOpType
ACT = mybir.ActivationFunctionType
AX_X = mybir.AxisListType.X

N, E, D = 3125, 103125, 256
HEADS, HD = 8, 32
TP, NT = 125, 25
GT = 4
GE = GT * 128
SL = 4
NG = -(-E // (GE * SL)) * SL
NGS = NG // SL
NG2 = NG // 2
ETILES = -(-E // 128)
CH = 7
W32, W64 = 32, 64
NPAD = N + W64
FTW = D + HEADS
BIG = 1.0e30
TM = 64
BT = 5
NB = NT // BT
TOK = BT * TP
CUTS = ((0, 313), (313, 312))
EPS = 1e-5
A1P = 3
TW = A1P * 2 * HEADS + HEADS
OPEN = SL
assert NG % SL == 0 and (2 * N + 16 * 127) // 128 <= TM and TM % SL == 0 and TP * NT == N and (CH - 1) * 128 < NG * GT <= CH * 128


def bc(ap, axis, n):
    a = ap.unsqueeze(axis)
    shape = list(a.shape)
    shape[axis] = n
    return a.broadcast_to(shape)


def rows(ap, n):
    return ap.partition_broadcast(n)


def open_counts(sp, *sems):
    for sem in sems:
        for one in sem if isinstance(sem, list) else [sem]:
            sp.sem_inc(one, OPEN)


def stage_edges(nc, s):
    with ExitStack() as ctx:
        sem = lambda name: ctx.enter_context(nc.semaphore("e_" + name))
        sb = lambda name, shape, dt: ctx.enter_context(nc.sbuf_tensor("e_" + name, shape, dt))
        d_rows, s_rows = sb("d_rows", [128, CH, 128], I32), sb("s_rows", [128, CH, 128], I32)
        d_f, s_f = sb("d_f", [128, CH, 128], F32), sb("s_f", [128, CH, 128], F32)
        tail = sb("tail", [1, NG * GE - E], I32)
        zrow = sb("zrow", [W64, TW], BF16)
        d_grp = sb("d_grp", [NG2, 2, GE], I32)
        low = sb("low", [NG2, 2, GE], F32)
        ext = sb("ext", [NG2, 2, 2], F32)
        span = sb("span", [128, NG], F32)
        smax = sb("smax", [128, 1], F32)
        sel_f = sb("sel_f", [GT * A1P * HEADS, HEADS, 128], F32)
        ioti = sb("ioti", [128, W64], I32)
        parti = sb("parti", [128, 2], I32)
        cleared, padded, loaded, floats, turned, stats, stored, spread, pool_c = [
            sem(n) for n in ("cleared", "padded", "loaded", "floats", "turned", "stats", "stored", "spread", "pool_c")]
        ps = s.ps
        full = ETILES - 1
        rest = E - full * 128
        block = ctx.enter_context(nc.Block())

        @block.gpsimd
        def _(pool):
            nc.gpsimd.memset(tail[:], -1).then_inc(cleared, 1)
            nc.gpsimd.memset(sel_f[:], 0.0)
            nc.gpsimd.memset(s.tick[:], 0.0)
            nc.gpsimd.memset(s_rows[:, CH - 1, :], 0).then_inc(cleared, 1)
            nc.gpsimd.memset(d_rows[:, CH - 1, :], -1).then_inc(cleared, 1)
            nc.gpsimd.memset(zrow[:], 0.0).then_inc(cleared, 1)
            nc.gpsimd.memset(s.ident[:], 0.0)
            nc.gpsimd.memset(s.fold[:], 0.0)
            pool.drain()
            nc.gpsimd.affine_select(out=s.ident[:], in_=s.ident[:], compare_op=ALU.not_equal, fill=1.0, base=0,
                                    pattern=[[-1, 128]], channel_multiplier=1).then_inc(pool_c, 1)
            for a in range(A1P):
                pool.drain()
                nc.gpsimd.affine_select(out=sel_f[:], in_=sel_f[:], compare_op=ALU.not_equal, fill=1.0, base=-a * HEADS,
                                        pattern=[[-1, HEADS], [-A1P * HEADS, GT], [0, W32]], channel_multiplier=1)
            pool.drain()
            for a in range(A1P):
                nc.gpsimd.affine_select(out=s.fold[:], in_=s.fold[:], compare_op=ALU.not_equal, fill=1.0, base=-a * (HEADS + 1),
                                        pattern=[[-1, HEADS + 1]], channel_multiplier=1)
                pool.drain()
            nc.gpsimd.iota(ioti[:], pattern=[[1, W64]], base=0, channel_multiplier=0).then_inc(pool_c, 1)
            nc.gpsimd.iota(parti[:, 0:1], pattern=[[1, 1]], base=0, channel_multiplier=1).then_inc(pool_c, 1)
            for j in range(GT):
                pool.drain()
                nc.gpsimd.iota(parti[32 * j:32 * j + 32, 1:2], pattern=[[1, 1]], base=0,
                               channel_multiplier=1).then_inc(pool_c, 1)

        @block.sync
        def _(sp):
            sp.wait_ge(cleared, 4)
            sp.dma_start(s.dpad[0:E], s.dst).then_inc(padded, 16)
            sp.dma_start(s.dpad[E:NG * GE], tail[:]).then_inc(padded, 16)
            sp.dma_start(s.tab[N:N + W64, :], zrow[:]).then_inc(padded, 16)
            for c in range(CH - 1):
                sp.dma_start(s_rows[:, c, :], s.src[c * 16384:(c + 1) * 16384].rearrange("(p e) -> p e", e=128)).then_inc(loaded, 16)
            a = (CH - 1) * 16384
            sp.dma_start(s_rows[0:full - 128 * (CH - 1), CH - 1, :], s.src[a:full * 128].rearrange("(p e) -> p e", e=128)).then_inc(loaded, 16)
            r = full - 128 * (CH - 1)
            sp.dma_start(s_rows[r:r + 1, CH - 1, 0:rest], s.src[full * 128:E].rearrange("(p e) -> p e", p=1)).then_inc(loaded, 16)
            sp.wait_ge(padded, 48)
            for c in range(CH):
                n = min(128, NG * GT - c * 128)
                sp.dma_start(d_rows[0:n, c, :], s.dpad[c * 16384:c * 16384 + n * 128].rearrange("(p e) -> p e", e=128)).then_inc(loaded, 16)
            sp.dma_start(d_grp[:], s.dpad[0:NG * GE].rearrange("(q p e) -> p q e", q=2, e=GE)).then_inc(loaded, 16)
            sp.wait_ge(stats, 1)
            with nc.allow_non_contiguous_dma(reason="one number per group"):
                for q in range(2):
                    sp.dma_start(s.grp[q * NG2:(q + 1) * NG2, :], ext[:, q, :]).then_inc(stored, 16)
            sp.wait_ge(stored, 32)
            sp.dma_start(s.gmm[:], rows(s.grp.rearrange("g m -> (g m)"), 128)).then_inc(spread, 16)
            sp.wait_ge(spread, 16)

        @block.vector
        def _(dve):
            dve.wait_ge(loaded, 16 * (CH + 1 + CH + 1))
            nc.vector.tensor_copy(s_f[:], s_rows[:]).then_inc(floats, 1)
            nc.vector.tensor_copy(d_f[:], d_rows[:]).then_inc(floats, 1)
            nc.vector.tensor_scalar(low[:], d_grp[:], 0.0, 8192.0, ALU.is_lt, ALU.mult)
            dve.drain()
            nc.vector.tensor_tensor(low[:], low[:], d_grp[:], ALU.add)
            dve.drain()
            nc.vector.tensor_reduce(ext[:, :, 0:1], low[:], AX_X, ALU.min)
            nc.vector.tensor_reduce(ext[:, :, 1:2], d_grp[:], AX_X, ALU.max)
            dve.drain()
            nc.vector.tensor_copy(smax[0:1, :], ext[0:1, 0, 0:1]).then_inc(stats, 1)
            dve.wait_ge(pool_c, 7)
            nc.vector.tensor_copy(s.iota64[:], ioti[:])
            nc.vector.tensor_copy(s.part[:], parti[:])
            nc.vector.tensor_copy(s.identb[:], s.ident[:])
            nc.vector.tensor_copy(s.sel[:], sel_f[:])
            nc.vector.memset(s.ones[:], 1.0)
            dve.wait_ge(turned, 1)
            nc.vector.tensor_copy(s.scol[:], ps[:, 0:2, :].rearrange("p b c -> p (b c)")[:, 0:CH * 128])
            nc.vector.tensor_copy(s.dcol[:], ps[:, 2:4, :].rearrange("p b c -> p (b c)")[:, 0:CH * 128])
            dve.wait_ge(spread, 16)
            g = s.gmm[:].rearrange("p (g m) -> p g m", m=2)
            nc.vector.tensor_tensor(span[:], g[:, :, 1], g[:, :, 0], ALU.subtract)
            dve.drain()
            nc.vector.tensor_reduce(smax[:], span[:], AX_X, ALU.max)
            dve.drain()
            nc.vector.tensor_copy(s.widest[:], smax[:])

        @block.tensor
        def _(pe):
            pe.wait_ge(pool_c, 7)
            pe.wait_ge(floats, 2)
            for k, f in ((0, s_f), (2, d_f)):
                for c in range(CH):
                    o = ps[:, k + c // 4, 128 * (c % 4):128 * (c % 4) + 128]
                    last = nc.tensor.transpose(o, f[:, c, :], s.ident[:])
            last.then_inc(turned, 1)


def stage_project(nc, s):
    with ExitStack() as ctx:
        sem = lambda name: ctx.enter_context(nc.semaphore("p_" + name))
        sb = lambda name, shape, dt: ctx.enter_context(nc.sbuf_tensor("p_" + name, shape, dt))
        wide = sb("wide", [128, 2, D + 2 * HEADS], F32)
        prod = sb("prod", [128, 2, D], F32)
        attn = sb("attn", [128, 2, D], F32)
        st6, mv = sb("st6", [TP, NT, 6], F32), sb("mv", [TP, NT, 2], F32)
        eps, half, rstd = sb("eps", [TP, NT], F32), sb("half", [TP, NT], F32), sb("rstd", [TP, NT], F32)
        xn, xT, row = sb("xn", [TP, D], F32), sb("xT", [128, 2, TP], F32), sb("row", [TP, FTW], F32)
        a1 = sb("a1", [TP, NT, HEADS], F32)
        parts, left = sb("parts", [TP, NT, A1P, HEADS], BF16), sb("left", [TP, NT, HEADS], F32)
        x_in, w_in, moments, scales, xn_ready, turned, xT_ready, summed, row_ready, row_out, row_free, parts_ready = [
            sem(n) for n in ("x_in", "w_in", "moments", "scales", "xn_ready", "turned", "xT_ready", "summed", "row_ready", "row_out", "row_free", "parts_ready")]
        ps = s.ps
        block = ctx.enter_context(nc.Block())

        @block.sync
        def _(sp):
            open_counts(sp, moments, scales, xn_ready, turned, xT_ready, summed, row_ready, row_free, parts_ready)
            sp.dma_start(s.x[:], s.x_dram.rearrange("(t p) d -> p t d", p=TP)).then_inc(x_in, 16)
            sp.dma_start(wide[:, :, 0:D], s.W.rearrange("(c k) n -> k c n", k=128)).then_inc(w_in, 16)
            sp.dma_start(attn[:, 0, :], rows(s.attn_l.rearrange("h d -> (h d)"), 128)).then_inc(w_in, 16)
            sp.dma_start(attn[:, 1, :], rows(s.attn_r.rearrange("h d -> (h d)"), 128)).then_inc(w_in, 16)
            with sp.Fori(0, NT) as t:
                sp.wait_ge(row_ready, OPEN + t + 1)
                sp.dma_start(s.ftab[bass.ds(t * TP, TP), :], row[:]).then_inc(row_out, 16)
                sp.wait_ge(row_out, 16 * t + 16)
                sp.sem_inc(row_free, 1)
            sp.wait_ge(parts_ready, OPEN + 1)
            sp.dma_start(s.a1tab.rearrange("(t p) c -> p t c", p=TP), parts[:].rearrange("p t a h -> p t (a h)")).then_inc(row_out, 16)
            sp.wait_ge(row_out, 16 * NT + 16)

        @block.gpsimd
        def _(pool):
            pool.wait_ge(moments, OPEN + 1)
            nc.gpsimd.tensor_tensor(rstd[:], eps[:], half[:], ALU.pow).then_inc(scales, 1)

        @block.vector
        def _(dve):
            dve.wait_ge(w_in, 48)
            for side in range(2):
                nc.vector.tensor_tensor(prod[:], wide[:, :, 0:D], bc(attn[:, side, :], 1, 2), ALU.mult)
                dve.drain()
                for c in range(2):
                    nc.vector.tensor_reduce(wide[:, c, D + HEADS * side:D + HEADS * (side + 1)],
                                            prod[:, c, :].rearrange("p (h d) -> p h d", h=HEADS), AX_X, ALU.add)
                dve.drain()
            dve.wait_ge(x_in, 16)
            ln_moments(nc, dve, s.x, st6, mv, eps, half)
            nc.vector.memset(s.ndT[:], -BIG).then_inc(moments, 1)
            dve.wait_ge(scales, OPEN + 1)
            with dve.Fori(0, NT) as t:
                dve.wait_ge(turned, OPEN + t)
                nc.vector.tensor_scalar(xn[:], s.x[:, bass.ds(t, 1), :].rearrange("p t d -> p (t d)"),
                                        mv[:, bass.ds(t, 1), 0], rstd[:, bass.ds(t, 1)],
                                        ALU.subtract, ALU.mult).then_inc(xn_ready, 1)
            dve.wait_ge(row_ready, OPEN + NT)
            for a in range(A1P):
                nc.vector.tensor_copy(parts[:, :, a, :], (left if a else a1)[:])
                dve.drain()
                if a < A1P - 1:
                    nc.vector.tensor_tensor(left[:], (left if a else a1)[:], parts[:, :, a, :], ALU.subtract)
                    dve.drain()
            nc.vector.memset(s.accT[:, 0, 0:1], 0.0).then_inc(parts_ready, 1)

        @block.tensor
        def _(pe):
            with pe.Fori(0, NT) as t:
                pe.wait_ge(xn_ready, OPEN + t + 1)
                pe.wait_ge(xT_ready, OPEN + t)
                for c in range(2):
                    last = nc.tensor.transpose(ps[:, 0, c * 128:c * 128 + TP], xn[:, c * 128:(c + 1) * 128], s.ident[0:TP, 0:TP])
                last.then_inc(turned, 1)
                pe.wait_ge(xT_ready, OPEN + t + 1)
                pe.wait_ge(row_ready, OPEN + t)
                for c in range(2):
                    last = nc.tensor.matmul(ps[0:TP, 1, 0:D + 2 * HEADS], xT[:, c, :], wide[:, c, :], start=c == 0, stop=c == 1)
                last.then_inc(summed, 1)

        @block.scalar
        def _(act):
            with act.Fori(0, NT) as t:
                act.wait_ge(turned, OPEN + t + 1)
                act.wait_ge(summed, OPEN + t)
                nc.scalar.copy(xT[:], ps[:, 0, 0:256].rearrange("p (c n) -> p c n", c=2)[:, :, 0:TP]).then_inc(xT_ready, 1)
                act.wait_ge(summed, OPEN + t + 1)
                act.wait_ge(row_free, OPEN + t)
                nc.scalar.copy(s.a2[:, bass.ds(t, 1), :].rearrange("p t h -> p (t h)"), ps[0:TP, 1, FTW:FTW + HEADS])
                nc.scalar.copy(a1[:, bass.ds(t, 1), :].rearrange("p t h -> p (t h)"), ps[0:TP, 1, D:FTW])
                nc.scalar.copy(row[:], ps[0:TP, 1, 0:FTW]).then_inc(row_ready, 1)


def ln_moments(nc, dve, x, st6, mv, eps, half):
    with dve.Fori(0, NT) as t:
        nc.vector.bn_stats(st6[:, bass.ds(t, 1), :].rearrange("p t k -> p (t k)"),
                           x[:, bass.ds(t, 1), :].rearrange("p t d -> p (t d)"))
    dve.drain()
    for t in range(NT):
        nc.vector.bn_aggr(mv[:, t, :], st6[:, t, :])
    dve.drain()
    nc.vector.tensor_scalar(eps[:], mv[:, :, 1], EPS, None, ALU.add)
    nc.vector.memset(half[:], -0.5)
    dve.drain()


def passes(eng, s, width):
    return eng.value_load(s.widest[0:1, 0:1], min_val=0, max_val=N - 1) // width + 1


def gather_rows(nc, pool, s, width, sidx, dest, table, idx_ready, gathered, free):
    with pool.Fori(0, passes(pool, s, width)) as r:
        with pool.Fori(0, NGS) as k:
            b = r * NGS + k
            i = b * SL
            for p in range(2):
                pool.wait_ge(free, OPEN + i + 2 * p + 2 - SL)
                nc.gpsimd.tensor_copy(sidx[p][:], s.scol[:, bass.ds(k * (SL * GT) + p * 2 * GT, 2 * GT)]).then_inc(idx_ready, 1)
                pool.wait_ge(idx_ready, OPEN + b * 2 + p + 1)
                nc.gpsimd.tensor_tensor(s.tick[0:1, p:p + 1], s.tick[0:1, 2:3], s.tick[0:1, 3:4], ALU.add)
                for u in (2 * p, 2 * p + 1):
                    for j in range(GT):
                        at = (u - 2 * p) * GT + j
                        nc.gpsimd.indirect_dma_start(out=dest[u][:, j, :], out_offset=None, in_=table,
                                                     in_offset=bass.IndirectOffsetOnAxis(ap=sidx[p][:, at:at + 1], axis=0)
                                                     ).then_inc(gathered[u], 16)


def stage_maxima(nc, s):
    with ExitStack() as ctx:
        sem = lambda name: ctx.enter_context(nc.semaphore("m_" + name))
        sb = lambda name, shape, dt: ctx.enter_context(nc.sbuf_tensor("m_" + name, shape, dt))
        AW = A1P * HEADS
        slots = lambda name, shape, dt, n=SL: [sb(f"{name}{u}", shape, dt) for u in range(n)]
        sidx = slots("sidx", [128, 2 * GT], I32, 2)
        a1g, a1T = slots("a1g", [128, GT, AW], BF16), slots("a1T", [GT * AW, 128], BF16)
        drow, mask = sb("drow", [128, SL, 128], I32), slots("mask", [128, 128], BF16)
        mx, win = slots("mx", [128, HEADS], F32), slots("win", [HEADS, W32], F32)
        first = sb("first", [128, NG], F32)
        firstw = sb("firstw", [128, NG], F32)
        base = sb("base", [1, NG], I32)
        tabs, vals, left = sb("tabs", [TP, NT, TW], BF16), sb("vals", [TP, NT, 2 * HEADS], F32), sb("left", [TP, NT, 2 * HEADS], F32)
        z = sb("z", [TP, NT, HEADS], F32)
        gathered = [sem(f"gathered{u}") for u in range(SL)]
        idx_ready, turned, a1T_ready, d_in, mask_ready, spread, mx_ready, mxT_ready, won = [
            sem(n) for n in ("idx_ready", "turned", "a1T_ready", "d_in", "mask_ready", "spread", "mx_ready", "mxT_ready", "won")]
        maxima, nodes_turned, tab_ready, tab_out = [sem(n) for n in ("maxima", "nodes_turned", "tab_ready", "tab_out")]
        zero_rows, zeroed, xs_out = sb("zero_rows", [128, D], F32), sem("zeroed"), sem("xs_out")
        ps = s.ps
        wide = [ps[:, 2 * z:2 * z + 2, :].rearrange("p b c -> p (b c)").rearrange("p (h e) -> p h e", h=HEADS) for z in range(2)]
        a1T_ps = [ps[0:GT * AW, 4 + u % 2, (u // 2) * 128:(u // 2) * 128 + 128] for u in range(SL)]
        mxT_ps = [ps[0:HEADS, 6 + u % 2, (u // 2) * 128:(u // 2) * 128 + 128] for u in range(SL)]
        block = ctx.enter_context(nc.Block())

        @block.gpsimd
        def _(pool):
            nc.gpsimd.memset(zero_rows[:], 0.0).then_inc(zeroed, 1)
            gather_rows(nc, pool, s, W32, sidx, a1g, s.a1tab, idx_ready, gathered, turned)

        @block.sync
        def _(sp):
            open_counts(sp, idx_ready, turned, a1T_ready, mask_ready, spread, mx_ready, mxT_ready, won, maxima, nodes_turned, tab_ready)
            sp.wait_ge(zeroed, 1)
            sp.dma_start(s.xs.rearrange("(t p) d -> p t d", p=128), bc(zero_rows[:], 1, TM)).then_inc(xs_out, 16)
            least = 2 * N // 128
            sp.dma_start(s.ys[least * 128:, :].rearrange("(t p) d -> p t d", p=128), bc(zero_rows[:], 1, TM - least)).then_inc(xs_out, 16)
            with sp.Fori(0, passes(sp, s, W32)) as r:
                with sp.Fori(0, NGS) as k:
                    b = r * NGS + k
                    sp.wait_ge(mask_ready, OPEN + b * SL)
                    e = s.dpad[bass.ds(k * SL * GE, SL * GE)].rearrange("(u j e) -> j u e", j=GT, e=128)
                    for j in range(GT):
                        sp.dma_start(drow[j * W32:(j + 1) * W32, :, :], bc(e[j], 0, W32)).then_inc(d_in, 16)
            sp.wait_ge(tab_ready, OPEN + 1)
            sp.dma_start(s.tab[0:N, :].rearrange("(t p) c -> p t c", p=TP), tabs[:]).then_inc(tab_out, 16)
            sp.wait_ge(tab_out, 16)
            sp.wait_ge(xs_out, 32)

        @block.tensor
        def _(pe):
            with pe.Fori(0, passes(pe, s, W32)) as r:
                with pe.Fori(0, NGS) as k:
                    b = r * NGS + k
                    i = b * SL

                    def turn(u):
                        pe.wait_ge(gathered[u], b * (16 * GT) + 16 * GT)
                        pe.wait_ge(a1T_ready, OPEN + i + u + 1 - SL)
                        nc.tensor.matmul(a1T_ps[u], a1g[u][:].rearrange("p j h -> p (j h)"), s.identb[:],
                                         start=True, stop=True).then_inc(turned, 1)

                    def scatter(u):
                        pe.wait_ge(a1T_ready, OPEN + i + u + 1)
                        pe.wait_ge(mask_ready, OPEN + i + u + 1)
                        pe.wait_ge(mx_ready, OPEN + i + u + 1 - 2)
                        for h in range(HEADS):
                            nc.tensor.matmul(wide[u % 2][:, h, :], s.sel[:, h, :], a1T[u][:], start=h % 4 == 0, stop=False, skip_group_check=True)
                        for h in range(HEADS):
                            last = nc.tensor.matmul(wide[u % 2][:, h, :], s.identb[:], mask[u][:], start=False, stop=True, skip_group_check=True)
                        last.then_inc(spread, 1)

                    def fold(u):
                        pe.wait_ge(mx_ready, OPEN + i + u + 1)
                        pe.wait_ge(won, OPEN + i + u + 1 - SL)
                        nc.tensor.transpose(mxT_ps[u], mx[u][:], s.ident[:]).then_inc(mxT_ready, 1)

                    turn(0)
                    turn(1)
                    scatter(0)
                    turn(2)
                    scatter(1)
                    fold(0)
                    turn(3)
                    scatter(2)
                    fold(1)
                    scatter(3)
                    fold(2)
                    fold(3)
            pe.wait_ge(maxima, OPEN + 1)
            for t in range(NT):
                last = nc.tensor.transpose(ps[0:TP, 0, t * HEADS:(t + 1) * HEADS], s.ndT[0:HEADS, t * TP:(t + 1) * TP], s.ident[0:HEADS, 0:HEADS])
            last.then_inc(nodes_turned, 1)

        @block.scalar
        def _(act):
            with act.Fori(0, passes(act, s, W32)) as r:
                with act.Fori(0, NGS) as k:
                    i = (r * NGS + k) * SL
                    for u in range(SL):
                        act.wait_ge(turned, OPEN + i + u + 1)
                        act.wait_ge(spread, OPEN + i + u + 1 - SL)
                        nc.scalar.copy(a1T[u][:], a1T_ps[u]).then_inc(a1T_ready, 1)

        @block.vector
        def _(dve):
            start_windows(nc, dve, s, first, firstw, 1)
            with dve.Fori(0, passes(dve, s, W32)) as r:
                nc.vector.tensor_scalar(base[:], first[0:1, :], float(N), None, ALU.min)
                dve.drain()
                with dve.Fori(0, NGS) as k:
                    b = r * NGS + k
                    i = b * SL

                    def maximum(u):
                        dve.wait_ge(spread, OPEN + i + u + 1)
                        dve.wait_ge(mxT_ready, OPEN + i + u + 1 - SL)
                        nc.vector.tensor_reduce(mx[u][:], wide[u % 2], AX_X, ALU.max).then_inc(mx_ready, 1)

                    def keep(u):
                        at = dve.value_load(base[0:1, bass.ds(k * SL + u, 1)], min_val=0, max_val=N)
                        dve.wait_ge(mxT_ready, OPEN + i + u + 1)
                        nc.vector.tensor_reduce(win[u][:], mxT_ps[u].rearrange("h (j w) -> h w j", j=GT), AX_X, ALU.max).then_inc(won, 1)
                        w = s.ndT[0:HEADS, bass.ds(at, W32)]
                        dve.drain()
                        nc.vector.tensor_tensor(w, w, win[u][:], ALU.max)

                    dve.wait_ge(d_in, b * (16 * GT) + 16 * GT)
                    for u in range(SL):
                        dve.wait_ge(spread, OPEN + i + u + 1 - SL)
                        nc.vector.tensor_scalar(mask[u][:], drow[:, u, :], firstw[:, bass.ds(k * SL + u, 1)], -BIG,
                                                ALU.not_equal, ALU.mult).then_inc(mask_ready, 1)
                    maximum(0)
                    maximum(1)
                    keep(0)
                    maximum(2)
                    keep(1)
                    maximum(3)
                    keep(2)
                    keep(3)
                next_windows(nc, dve, first, firstw, W32)
            nc.vector.memset(tabs[:], 1.0).then_inc(maxima, 1)
            dve.wait_ge(nodes_turned, OPEN + 1)
            nc.vector.tensor_tensor(z[:], s.a2[:], ps[0:TP, 0, 0:NT * HEADS].rearrange("p (t h) -> p t h", t=NT), ALU.add)
            dve.drain()
            nc.vector.scalar_tensor_tensor(out=vals[:, :, HEADS:2 * HEADS], in0=z[:], scalar=0.2, in1=z[:], op0=ALU.mult, op1=ALU.max)
            nc.vector.tensor_copy(vals[:, :, 0:HEADS], s.a2[:])
            dve.drain()
            for a in range(A1P):
                part = tabs[:, :, a * 2 * HEADS:(a + 1) * 2 * HEADS]
                nc.vector.tensor_copy(part, (left if a else vals)[:])
                dve.drain()
                if a < A1P - 1:
                    nc.vector.tensor_tensor(left[:], (left if a else vals)[:], part, ALU.subtract)
                    dve.drain()
            nc.vector.memset(s.accT[:], 0.0)
            nc.vector.memset(s.ndT[:], 0.0)
            dve.drain()
            nc.vector.memset(z[:], 0.0).then_inc(tab_ready, 1)


def start_windows(nc, dve, s, first, firstw, col):
    g = s.gmm[:].rearrange("p (g m) -> p g m", m=2)
    nc.vector.tensor_copy(first[:], g[:, :, 0])
    nc.vector.tensor_scalar(firstw[:], g[:, :, 0], s.part[:, col:col + 1], None, ALU.add)
    dve.drain()


def next_windows(nc, dve, first, firstw, width):
    dve.drain()
    nc.vector.tensor_scalar(first[:], first[:], float(width), None, ALU.add)
    nc.vector.tensor_scalar(firstw[:], firstw[:], float(width), None, ALU.add)
    dve.drain()


def pair_offsets(nc, s, drel, first, k, p):
    nc.vector.tensor_tensor(drel[:].rearrange("p (g j) -> p g j", g=2),
                            s.dcol[:, bass.ds(k * (SL * GT) + p * 2 * GT, 2 * GT)].rearrange("p (g j) -> p g j", g=2),
                            bc(first[:, bass.ds(k * SL + 2 * p, 2)], 2, GT), ALU.subtract)


def stage_attend(nc, s):
    with ExitStack() as ctx:
        sem = lambda name: ctx.enter_context(nc.semaphore("w_" + name))
        sb = lambda name, shape, dt: ctx.enter_context(nc.sbuf_tensor("w_" + name, shape, dt))
        two_sb = lambda name, shape, dt: [sb(f"{name}{p}", shape, dt) for p in range(2)]
        PT = 2 * GT
        EW = A1P * (HEADS + 1)
        sidx, ftp = two_sb("sidx", [128, PT], I32), two_sb("ftp", [128, PT, FTW], F32)
        drow, ohT = two_sb("drow", [W64, 2 * GE], I32), [sb(f"ohT{u}", [W64, GE], BF16) for u in range(SL)]
        tabw = [sb(f"tabw{u}", [W64, TW], BF16) for u in range(SL)]
        z, pen, zl = two_sb("z", [128, PT, HEADS], F32), two_sb("pen", [128, PT, HEADS], F32), two_sb("zl", [128, PT, HEADS], F32)
        looked_up, ohb = two_sb("looked_up", [128, PT, 2 * HEADS], F32), two_sb("ohb", [128, PT, W64], BF16)
        exb, rem = two_sb("exb", [128, PT, A1P, HEADS + 1], BF16), two_sb("rem", [128, PT, HEADS + 1], F32)
        arg = two_sb("arg", [128, PT, HEADS], F32)
        ex = two_sb("ex", [128, PT, HEADS + 1], F32)
        drel, oh = two_sb("drel", [128, PT], F32), two_sb("oh", [128, PT, W64], F32)
        msg = two_sb("msg", [128, PT, D], F32)
        away, nfirstw, one = sb("away", [W64, 2 * GE], F32), sb("nfirstw", [W64, NG], F32), sb("one", [W64, 1], F32)
        first, firstw, base = sb("first", [128, NG], F32), sb("firstw", [128, NG], F32), sb("base", [1, NG], I32)
        slot = lambda pairs, u: pairs[u // 2][:, (u % 2) * GT:(u % 2 + 1) * GT]
        ftg = [slot(ftp, u) for u in range(SL)]
        gathered, tab_in = [[sem(f"{n}{u}") for u in range(SL)] for n in ("gathered", "tab_in")]
        d_in = [sem(f"d_in{p}") for p in range(2)]
        idx_ready, ohT_ready, looked, arg_ready, ex_ready, ohb_ready, parts_ready, msg_ready, summed, added, base_ready, ones_ready = [sem(n) for n in (
            "idx_ready", "ohT_ready", "looked", "arg_ready", "ex_ready", "ohb_ready", "parts_ready", "msg_ready", "summed", "added", "base_ready", "ones_ready")]
        ps = s.ps
        look = [ps[:, p, 0:PT * TW].rearrange("p (j c) -> p j c", j=PT) for p in range(2)]
        acc = [ps[:, 4 + u, 0:3 * W64].rearrange("p (c w) -> p c w", c=3) for u in range(SL)]
        block = ctx.enter_context(nc.Block())

        @block.gpsimd
        def _(pool):
            gather_rows(nc, pool, s, W64, sidx, ftg, s.ftab, idx_ready, gathered, msg_ready)

        @block.sync
        def _(sp):
            open_counts(sp, idx_ready, ohT_ready, looked, arg_ready, ex_ready, ohb_ready, parts_ready, msg_ready, summed, added,
                        base_ready, ones_ready)
            with sp.Fori(0, passes(sp, s, W64)) as r:
                with sp.Fori(0, NGS) as k:
                    i = (r * NGS + k) * SL
                    sp.wait_ge(base_ready, OPEN + r + 1)
                    for p in range(2):
                        sp.wait_ge(ohT_ready, OPEN + i + 2 * p + 2 - SL)
                        sp.dma_start(drow[p][:], rows(s.dpad[bass.ds(k * SL * GE + p * 2 * GE, 2 * GE)], W64)).then_inc(d_in[p], 16)
                        for u in (2 * p, 2 * p + 1):
                            sp.wait_ge(looked, OPEN + i + u + 1 - SL)
                            at = sp.value_load(base[0:1, bass.ds(k * SL + u, 1)], min_val=0, max_val=N)
                            sp.dma_start(tabw[u][:], s.tab[bass.ds(at, W64), :]).then_inc(tab_in[u], 16)

        @block.tensor
        def _(pe):
            pe.wait_ge(ones_ready, OPEN + 1)
            with pe.Fori(0, passes(pe, s, W64)) as r:
                def look_up(k, p):
                    b = r * NGS + k
                    for u in (2 * p, 2 * p + 1):
                        pe.wait_ge(ohT_ready, OPEN + b * SL + u + 1)
                        pe.wait_ge(tab_in[u], b * 16 + 16)
                        pe.wait_ge(arg_ready, OPEN + b * 2 + p - 1)
                        for j in range(GT):
                            last = nc.tensor.matmul(look[p][:, (u % 2) * GT + j, :], ohT[u][:, j * 128:(j + 1) * 128], tabw[u][:], start=True, stop=True)
                        last.then_inc(looked, 1)

                def sum_up(k, p):
                    i = (r * NGS + k) * SL
                    for u in (2 * p, 2 * p + 1):
                        m, o, w, ob = slot(msg, u), slot(oh, u), slot(exb, u), slot(ohb, u)
                        pe.wait_ge(msg_ready, OPEN + i + u + 1)
                        pe.wait_ge(added, OPEN + i + u + 1 - SL)
                        for c in range(2):
                            for j in range(GT):
                                nc.tensor.matmul(acc[u][:, c, :], m[:, j, c * 128:(c + 1) * 128], o[:, j, :], start=j == 0, stop=j == GT - 1)
                        pe.wait_ge(parts_ready, OPEN + (r * NGS + k) * 2 + p + 1)
                        pe.wait_ge(ohb_ready, OPEN + (r * NGS + k) * 2 + p + 1)
                        for j in range(GT):
                            last = nc.tensor.matmul(acc[u][0:EW, 2, :], w[:, j].rearrange("p a h -> p (a h)"), ob[:, j, :], start=j == 0, stop=j == GT - 1)
                        last.then_inc(summed, 1)

                def body(k, last_body):
                    look_up(k, 1)
                    sum_up(k, 0)
                    if not last_body:
                        look_up(k + 1, 0)
                    sum_up(k, 1)

                look_up(0, 0)
                with pe.Fori(0, NGS - 1) as k:
                    body(k, False)
                body(NGS - 1, True)

        @block.scalar
        def _(act):
            act.wait_ge(ones_ready, OPEN + 1)
            with act.Fori(0, passes(act, s, W64)) as r:
                def one_hot(k, p):
                    b = r * NGS + k
                    act.drain()
                    act.wait_ge(base_ready, OPEN + r + 1)
                    act.wait_ge(d_in[p], b * 16 + 16)
                    for q in range(2):
                        nc.scalar.activation(away[:, q * GE:(q + 1) * GE], drow[p][:, q * GE:(q + 1) * GE], ACT.Abs,
                                             bias=nfirstw[:, bass.ds(k * SL + 2 * p + q, 1)])
                    act.drain()
                    for q in range(2):
                        act.wait_ge(looked, OPEN + b * SL + 2 * p + q + 1 - SL)
                        nc.scalar.activation(ohT[2 * p + q][:], away[:, q * GE:(q + 1) * GE], ACT.Relu, bias=one[:], scale=-1.0).then_inc(ohT_ready, 1)

                def weights(k, p):
                    b = r * NGS + k
                    act.wait_ge(arg_ready, OPEN + b * 2 + p + 1)
                    act.wait_ge(summed, OPEN + b * SL + 2 * p + 2 - SL)
                    nc.scalar.activation(ex[p][:, :, 0:HEADS], arg[p][:], ACT.Exp)
                    act.drain()
                    nc.scalar.copy(exb[p][:, :, 0, :], ex[p][:]).then_inc(ex_ready, 1)
                    nc.scalar.copy(ohb[p][:], oh[p][:]).then_inc(ohb_ready, 1)

                def body(k, last_body):
                    one_hot(k, 1)
                    weights(k, 0)
                    if not last_body:
                        one_hot(k + 1, 0)
                    weights(k, 1)

                one_hot(0, 0)
                with act.Fori(0, NGS - 1) as k:
                    body(k, False)
                body(NGS - 1, True)

        @block.vector
        def _(dve):
            for p in range(2):
                nc.vector.memset(ex[p][:], 1.0)
            start_windows(nc, dve, s, first, firstw, 0)
            nc.vector.memset(one[:], 1.0)
            nc.vector.memset(z[0][:], 0.0).then_inc(ones_ready, 1)
            with dve.Fori(0, passes(dve, s, W64)) as r:
                nc.vector.tensor_scalar(nfirstw[:], firstw[0:W64, :], -1.0, None, ALU.mult)
                nc.vector.tensor_scalar(base[:], first[0:1, :], float(N), None, ALU.min)
                dve.drain()
                nc.vector.memset(z[0][:], 0.0).then_inc(base_ready, 1)
                def arguments(k, p):
                    b = r * NGS + k
                    pair_offsets(nc, s, drel[p], first, k, p)
                    dve.drain()
                    dve.wait_ge(summed, OPEN + b * SL + 2 * p + 2 - SL)
                    nc.vector.tensor_tensor(oh[p][:], bc(s.iota64[:], 1, PT), bc(drel[p][:], 2, W64), ALU.is_equal)
                    dve.wait_ge(looked, OPEN + b * SL + 2 * p + 2)
                    nc.vector.tensor_scalar(pen[p][:], look[p][:, :, TW - HEADS:TW], 1.0, BIG, ALU.subtract, ALU.mult)
                    parts = [look[p][:, :, a * 2 * HEADS:(a + 1) * 2 * HEADS] for a in range(A1P)]
                    nc.vector.tensor_copy(looked_up[p][:], parts[0])
                    for part in parts[1:]:
                        dve.drain()
                        nc.vector.tensor_tensor(looked_up[p][:], looked_up[p][:], part, ALU.add)
                    dve.drain()
                    for u in (2 * p, 2 * p + 1):
                        dve.wait_ge(gathered[u], b * (16 * GT) + 16 * GT)
                    nc.vector.tensor_tensor(z[p][:], ftp[p][:, :, D:FTW], looked_up[p][:, :, 0:HEADS], ALU.add)
                    dve.drain()
                    nc.vector.scalar_tensor_tensor(out=zl[p][:], in0=z[p][:], scalar=0.2, in1=z[p][:], op0=ALU.mult, op1=ALU.max)
                    dve.drain()
                    dve.wait_ge(ex_ready, OPEN + b * 2 + p - 1)
                    nc.vector.tensor_tensor(z[p][:], zl[p][:], looked_up[p][:, :, HEADS:2 * HEADS], ALU.subtract)
                    dve.drain()
                    nc.vector.tensor_tensor(arg[p][:], z[p][:], pen[p][:], ALU.min).then_inc(arg_ready, 1)

                def messages(k, p):
                    dve.wait_ge(ex_ready, OPEN + (r * NGS + k) * 2 + p + 1)
                    hi, mid, lo = [exb[p][:, :, a, :] for a in range(A1P)]
                    nc.vector.tensor_tensor(rem[p][:], ex[p][:], hi, ALU.subtract)
                    for u in (2 * p, 2 * p + 1):
                        nc.vector.tensor_tensor(slot(msg, u).rearrange("p j (h d) -> p j h d", h=HEADS),
                                                ftg[u][:, :, 0:D].rearrange("p j (h d) -> p j h d", h=HEADS),
                                                bc(slot(ex, u)[:, :, 0:HEADS], 3, HD), ALU.mult).then_inc(msg_ready, 1)
                        dve.drain()
                        if u % 2 == 0:
                            nc.vector.tensor_copy(mid, rem[p][:])
                        else:
                            nc.vector.tensor_tensor(lo, rem[p][:], mid, ALU.subtract).then_inc(parts_ready, 1)

                def add(k, p):
                    for u in (2 * p, 2 * p + 1):
                        at = dve.value_load(base[0:1, bass.ds(k * SL + u, 1)], min_val=0, max_val=N)
                        dve.drain()
                        dve.wait_ge(summed, OPEN + (r * NGS + k) * SL + u + 1)
                        w = s.accT[:, :, bass.ds(at, W64)]
                        nc.vector.tensor_tensor(w, w, acc[u][:, 0:2, :], ALU.add)
                        w = s.ndT[:, bass.ds(at, W64)]
                        nc.vector.tensor_tensor(w, w, acc[u][0:EW, 2, :], ALU.add).then_inc(added, 1)

                def body(k, last_body):
                    arguments(k, 1)
                    messages(k, 1)
                    add(k, 0)
                    if not last_body:
                        arguments(k + 1, 0)
                        messages(k + 1, 0)
                    add(k, 1)

                arguments(0, 0)
                messages(0, 0)
                with dve.Fori(0, NGS - 1) as k:
                    body(k, False)
                body(NGS - 1, True)
                next_windows(nc, dve, first, firstw, W64)


def normalise(nc, s, prefix, times):
    with ExitStack() as ctx:
        moments, scales = s.moments, s.scales
        sb = lambda name, shape: ctx.enter_context(nc.sbuf_tensor(prefix + name, shape, F32))
        st6, eps, half = sb("st6", [TP, NT, 6]), sb("eps", [TP, NT]), sb("half", [TP, NT])
        block = ctx.enter_context(nc.Block())

        @block.vector
        def _(dve):
            ln_moments(nc, dve, s.x, st6, s.mv, eps, half)
            nc.vector.memset(st6[:], 0.0).then_inc(moments, 1)
            dve.wait_ge(scales, times)

        @block.gpsimd
        def _(pool):
            pool.wait_ge(moments, times)
            nc.gpsimd.tensor_tensor(s.rstd[:], eps[:], half[:], ALU.pow).then_inc(scales, 1)


def tile_of(buf, t):
    return buf[:, bass.ds(t, 1), :].rearrange("p t d -> p (t d)")


def stage_join(nc, s):
    with ExitStack() as ctx:
        sem = lambda name: ctx.enter_context(nc.semaphore("j_" + name))
        sb = lambda name, shape, dt: ctx.enter_context(nc.sbuf_tensor("j_" + name, shape, dt))
        sums, weights = sb("sums", [128, 2, TP], F32), sb("weights", [A1P * (HEADS + 1), TP], F32)
        rs, v, low, ev, part = sb("rs", [TP, HEADS + 1], F32), sb("v", [TP, D], F32), sb("low", [TP, D], F32), sb("ev", [TP, D], F32), sb("part", [TP, D], F32)
        taken, turned, low_ready, exp_ready, read = [sem(n) for n in ("taken", "turned", "low_ready", "exp_ready", "read")]
        ps = s.ps
        block = ctx.enter_context(nc.Block())

        @block.sync
        def _(sp):
            open_counts(sp, taken, turned, low_ready, exp_ready, read)

        @block.scalar
        def _(act):
            with act.Fori(0, NT) as t:
                act.wait_ge(turned, OPEN + t)
                nc.scalar.copy(weights[:], s.ndT[:, bass.ds(t * TP, TP)])
                nc.scalar.copy(sums[:], s.accT[:, :, bass.ds(t * TP, TP)]).then_inc(taken, 1)
                act.wait_ge(low_ready, OPEN + t + 1)
                nc.scalar.activation(ev[:], low[:], ACT.Exp).then_inc(exp_ready, 1)

        @block.tensor
        def _(pe):
            with pe.Fori(0, NT) as t:
                pe.wait_ge(taken, OPEN + t + 1)
                pe.wait_ge(read, OPEN + t)
                for c in range(2):
                    nc.tensor.transpose(ps[0:TP, 0, c * 128:(c + 1) * 128], sums[:, c, :], s.ident[:])
                nc.tensor.matmul(ps[0:TP, 1, 0:HEADS + 1], weights[:], s.fold[:], start=True, stop=True).then_inc(turned, 1)

        @block.vector
        def _(dve):
            with dve.Fori(0, NT) as t:
                dve.wait_ge(turned, OPEN + t + 1)
                nc.vector.tensor_scalar(rs[:, 0:HEADS], ps[0:TP, 1, 0:HEADS], 1e-30, None, ALU.max)
                nc.vector.tensor_scalar(rs[:, HEADS:HEADS + 1], ps[0:TP, 1, HEADS:HEADS + 1], 1.0, None, ALU.max)
                dve.drain()
                nc.vector.reciprocal(rs[:], rs[:])
                dve.drain()
                nc.vector.tensor_tensor(v[:].rearrange("p (h d) -> p h d", h=HEADS), ps[0:TP, 0, 0:D].rearrange("p (h d) -> p h d", h=HEADS),
                                        bc(rs[:, 0:HEADS], 2, HD), ALU.mult).then_inc(read, 1)
                nc.vector.tensor_copy(s.rdeg[:, bass.ds(t, 1)], rs[:, HEADS:HEADS + 1])
                dve.drain()
                nc.vector.tensor_scalar(low[:], v[:], 0.0, None, ALU.min).then_inc(low_ready, 1)
                nc.vector.scalar_tensor_tensor(out=part[:], in0=v[:], scalar=0.0, in1=tile_of(s.x, t), op0=ALU.max, op1=ALU.add)
                dve.drain()
                dve.wait_ge(exp_ready, OPEN + t + 1)
                nc.vector.scalar_tensor_tensor(out=tile_of(s.x, t), in0=ev[:], scalar=-1.0, in1=part[:], op0=ALU.add, op1=ALU.add)
            nc.vector.memset(s.accT[:], 0.0)
    normalise(nc, s, "n1_", 1)


def stage_share(nc, s):
    with ExitStack() as ctx:
        sem = lambda name: ctx.enter_context(nc.semaphore("s_" + name))
        sb = lambda name, shape, dt: ctx.enter_context(nc.sbuf_tensor("s_" + name, shape, dt))
        w, brow = sb("w", [128, 2, D], F32), sb("brow", [1, D], F32)
        h, hT = sb("h", [TP, D], F32), sb("hT", [128, 2, TP], F32)
        w_in, h_ready, h_out, h_free, turned, hT_ready, summed, kept = [sem(n) for n in ("w_in", "h_ready", "h_out", "h_free", "turned", "hT_ready", "summed", "kept")]
        ps = s.ps
        block = ctx.enter_context(nc.Block())

        @block.sync
        def _(sp):
            open_counts(sp, h_ready, h_free, turned, hT_ready, summed, kept)
            sp.dma_start(w[:], s.ins["L1_gnn_W_self"].rearrange("(c k) n -> k c n", k=128)).then_inc(w_in, 16)
            sp.dma_start(brow[:], rows(s.ins["L1_gnn_b"], 1)).then_inc(w_in, 16)
            with sp.Fori(0, NT) as t:
                sp.wait_ge(h_ready, OPEN + t + 1)
                sp.dma_start(s.htab[bass.ds(t * TP, TP), :], h[:]).then_inc(h_out, 16)
                sp.wait_ge(h_out, 16 * t + 16)
                sp.sem_inc(h_free, 1)

        @block.vector
        def _(dve):
            with dve.Fori(0, NT) as t:
                dve.wait_ge(turned, OPEN + t)
                dve.wait_ge(h_free, OPEN + t)
                nc.vector.tensor_scalar(h[:], tile_of(s.x, t), s.mv[:, bass.ds(t, 1), 0], s.rstd[:, bass.ds(t, 1)],
                                        ALU.subtract, ALU.mult).then_inc(h_ready, 1)
                dve.wait_ge(summed, OPEN + t + 1)
                nc.vector.tensor_copy(tile_of(s.own, t), ps[0:TP, 1, 0:D]).then_inc(kept, 1)

        @block.tensor
        def _(pe):
            pe.wait_ge(w_in, 32)
            with pe.Fori(0, NT) as t:
                pe.wait_ge(h_ready, OPEN + t + 1)
                pe.wait_ge(hT_ready, OPEN + t)
                for c in range(2):
                    last = nc.tensor.transpose(ps[:, 0, c * 128:c * 128 + TP], h[:, c * 128:(c + 1) * 128], s.ident[0:TP, 0:TP])
                last.then_inc(turned, 1)
                pe.wait_ge(hT_ready, OPEN + t + 1)
                pe.wait_ge(kept, OPEN + t)
                nc.tensor.matmul(ps[0:TP, 1, 0:D], s.ones[0:1, 0:TP], brow[:], start=True, stop=False)
                for c in range(2):
                    last = nc.tensor.matmul(ps[0:TP, 1, 0:D], hT[:, c, :], w[:, c, :], start=False, stop=c == 1)
                last.then_inc(summed, 1)

        @block.scalar
        def _(act):
            with act.Fori(0, NT) as t:
                act.wait_ge(turned, OPEN + t + 1)
                act.wait_ge(summed, OPEN + t)
                nc.scalar.copy(hT[:], ps[:, 0, 0:256].rearrange("p (c n) -> p c n", c=2)[:, :, 0:TP]).then_inc(hT_ready, 1)


def stage_aggregate(nc, s):
    with ExitStack() as ctx:
        sem = lambda name: ctx.enter_context(nc.semaphore("g_" + name))
        sb = lambda name, shape, dt: ctx.enter_context(nc.sbuf_tensor("g_" + name, shape, dt))
        two_sb = lambda name, shape, dt: [sb(f"{name}{p}", shape, dt) for p in range(2)]
        sidx, drel, oh = two_sb("sidx", [128, 2 * GT], I32), two_sb("drel", [128, 2 * GT], F32), two_sb("oh", [128, 2 * GT, W64], F32)
        hg = [sb(f"hg{u}", [128, GT, D], F32) for u in range(SL)]
        first, firstw, base = sb("first", [128, NG], F32), sb("firstw", [128, NG], F32), sb("base", [1, NG], I32)
        gathered = [sem(f"gathered{u}") for u in range(SL)]
        idx_ready, oh_ready, summed, added = [sem(n) for n in ("idx_ready", "oh_ready", "summed", "added")]
        ps = s.ps
        acc = [ps[:, 4 + u, 0:2 * W64].rearrange("p (c w) -> p c w", c=2) for u in range(SL)]
        block = ctx.enter_context(nc.Block())

        @block.sync
        def _(sp):
            open_counts(sp, idx_ready, oh_ready, summed, added)

        @block.gpsimd
        def _(pool):
            gather_rows(nc, pool, s, W64, sidx, hg, s.htab, idx_ready, gathered, summed)

        @block.tensor
        def _(pe):
            with pe.Fori(0, passes(pe, s, W64)) as r:
                with pe.Fori(0, NGS) as k:
                    b = r * NGS + k
                    for u in range(SL):
                        pe.wait_ge(oh_ready, OPEN + b * 2 + u // 2 + 1)
                        pe.wait_ge(added, OPEN + b * SL + u + 1 - SL)
                        pe.wait_ge(gathered[u], b * (16 * GT) + 16 * GT)
                        for c in range(2):
                            for j in range(GT):
                                last = nc.tensor.matmul(acc[u][:, c, :], hg[u][:, j, c * 128:(c + 1) * 128], oh[u // 2][:, (u % 2) * GT + j, :],
                                                        start=j == 0, stop=j == GT - 1)
                        last.then_inc(summed, 1)

        @block.vector
        def _(dve):
            start_windows(nc, dve, s, first, firstw, 0)
            with dve.Fori(0, passes(dve, s, W64)) as r:
                nc.vector.tensor_scalar(base[:], first[0:1, :], float(N), None, ALU.min)
                dve.drain()
                with dve.Fori(0, NGS) as k:
                    i = (r * NGS + k) * SL
                    for p in range(2):
                        pair_offsets(nc, s, drel[p], first, k, p)
                    dve.drain()
                    for p in range(2):
                        dve.wait_ge(summed, OPEN + i + 2 * p + 2 - SL)
                        nc.vector.tensor_tensor(oh[p][:], bc(s.iota64[:], 1, 2 * GT), bc(drel[p][:], 2, W64), ALU.is_equal).then_inc(oh_ready, 1)
                    for u in range(SL):
                        at = dve.value_load(base[0:1, bass.ds(k * SL + u, 1)], min_val=0, max_val=N)
                        dve.drain()
                        dve.wait_ge(summed, OPEN + i + u + 1)
                        w = s.accT[:, :, bass.ds(at, W64)]
                        nc.vector.tensor_tensor(w, w, acc[u], ALU.add).then_inc(added, 1)
                next_windows(nc, dve, first, firstw, W64)


def stage_join2(nc, s):
    with ExitStack() as ctx:
        sem = lambda name: ctx.enter_context(nc.semaphore("k_" + name))
        sb = lambda name, shape, dt: ctx.enter_context(nc.sbuf_tensor("k_" + name, shape, dt))
        w, sums, v = sb("w", [128, 2, D], F32), sb("sums", [128, 2, TP], F32), sb("v", [TP, D], F32)
        w_in, taken, summed, read = [sem(n) for n in ("w_in", "taken", "summed", "read")]
        ps = s.ps
        block = ctx.enter_context(nc.Block())

        @block.sync
        def _(sp):
            open_counts(sp, taken, summed, read)
            sp.dma_start(w[:], s.ins["L1_gnn_W_neigh"].rearrange("(c k) n -> k c n", k=128)).then_inc(w_in, 16)

        @block.scalar
        def _(act):
            with act.Fori(0, NT) as t:
                act.wait_ge(summed, OPEN + t)
                nc.scalar.copy(sums[:], s.accT[:, :, bass.ds(t * TP, TP)]).then_inc(taken, 1)

        @block.tensor
        def _(pe):
            pe.wait_ge(w_in, 16)
            with pe.Fori(0, NT) as t:
                pe.wait_ge(taken, OPEN + t + 1)
                pe.wait_ge(read, OPEN + t)
                for c in range(2):
                    last = nc.tensor.matmul(ps[0:TP, 0, 0:D], sums[:, c, :], w[:, c, :], start=c == 0, stop=c == 1)
                last.then_inc(summed, 1)

        @block.vector
        def _(dve):
            with dve.Fori(0, NT) as t:
                dve.wait_ge(summed, OPEN + t + 1)
                nc.vector.scalar_tensor_tensor(out=v[:], in0=ps[0:TP, 0, 0:D], scalar=s.rdeg[:, bass.ds(t, 1)], in1=tile_of(s.own, t),
                                               op0=ALU.mult, op1=ALU.add).then_inc(read, 1)
                dve.drain()
                nc.vector.scalar_tensor_tensor(out=tile_of(s.x, t), in0=v[:], scalar=0.0, in1=tile_of(s.x, t), op0=ALU.max, op1=ALU.add)
                dve.drain()
    normalise(nc, s, "n2_", 3)


class Mixture:

    def __init__(self, prefix, experts, hidden, out, out_chunks, out_bias):
        self.prefix, self.experts, self.hidden, self.out = prefix, experts, hidden, out
        self.out_chunks, self.out_bias = out_chunks, out_bias
        self.width = sum(n * kc * 128 for _, _, n, kc in hidden) + out_chunks * D


def stage_mixture(nc, s, m, second):
    with ExitStack() as ctx:
        X = m.experts
        sb = lambda name, shape, dt: ctx.enter_context(nc.sbuf_tensor(m.prefix + name, shape, dt))
        chosen, w12, pos = sb("chosen", [TP, NT, 2], F32), sb("w12", [TP, NT, 2], F32), sb("pos", [TP, 2 * NT], I32)
        expert, tiles = sb("expert", [1, TM], I32), sb("tiles", [1, 1], I32)
        route(nc, s, m, second, chosen, w12, pos, expert, tiles)
        run_experts(nc, s, m, expert, tiles)
        combine(nc, s, m, second, w12, pos)


def route(nc, s, m, second, chosen, w12, pos, expert, tiles):
    X = m.experts
    XP = max(X, 8)
    with ExitStack() as ctx:
        sem = lambda name: ctx.enter_context(nc.semaphore(m.prefix + name))
        sb = lambda name, shape, dt: ctx.enter_context(nc.sbuf_tensor(m.prefix + name, shape, dt))
        xn, xT = sb("xn", [TP, BT, D], F32), sb("xT", [128, 2, TOK], F32)
        gw, gb = sb("gw", [128, 2, 128], F32), sb("gb", [1, 16], F32)
        rh, rb1, rw2 = sb("rh", [128, TOK], F32), sb("rb1", [128, 1], F32), sb("rw2", [128, 16], F32)
        score, ex = sb("score", [TP, NT, XP], F32), sb("ex", [TP, NT, X], F32)
        mxs, tot, gap, q = [sb(n, [TP, NT], F32) for n in ("mxs", "tot", "gap", "q")]
        top, topi = sb("top", [TP, NT, 8], F32), sb("topi", [TP, NT, 8], U32)
        picks = [sb(f"pick{c}", [TP, NT, X], F32) for c in range(2)]
        both, place, before = sb("both", [TP, NT, X], F32), sb("place", [TP, NT, X], F32), sb("before", [TP, NT + 1, X], F32)
        lower, all_ones = sb("lower", [TP, TP], F32), sb("all_ones", [TP, TP], F32)
        marks, full = sb("marks", [TP, NT], F32), sb("full", [TP, X, NT], F32)
        used, begins = sb("used", [TP, X], F32), sb("begins", [TP, X + 1], F32)
        past, expert_f, posf = sb("past", [1, TM, X], F32), sb("expert_f", [1, TM], F32), sb("posf", [TP, NT, 2], F32)
        consts, xn_ready, kept, turned, xT_ready, scored, taken = [sem(n) for n in (
            "consts", "xn_ready", "kept", "turned", "xT_ready", "scored", "taken")]
        rh_sum, rh_ready = (None, None) if second else (sem("rh_sum"), sem("rh_ready"))
        asked, answered, masks, both_ready, ranked, placed, sent = [sem(n) for n in (
            "asked", "answered", "masks", "both_ready", "ranked", "placed", "sent")]
        ps = s.ps
        block = ctx.enter_context(nc.Block())

        @block.sync
        def _(sp):
            open_counts(sp, xn_ready, kept, turned, xT_ready, scored, taken, [] if second else [rh_sum, rh_ready])
            i = s.ins
            if second:
                sp.dma_start(gw[:, :, 0:X], i["L1_ffn_gate_w"].rearrange("(c k) n -> k c n", k=128)).then_inc(consts, 16)
                sp.dma_start(gb[:, 0:X], rows(i["L1_ffn_gate_b"], 1)).then_inc(consts, 16)
            else:
                sp.dma_start(gw[:], i["L0_ffn_router_w1"].rearrange("(c k) n -> k c n", k=128)).then_inc(consts, 16)
                sp.dma_start(gb[:, 0:X], rows(i["L0_ffn_router_b2"], 1)).then_inc(consts, 16)
                sp.dma_start(rb1[:], i["L0_ffn_router_b1"].rearrange("(p a) -> p a", a=1)).then_inc(consts, 16)
                sp.dma_start(rw2[:, 0:X], i["L0_ffn_router_w2"]).then_inc(consts, 16)

        @block.gpsimd
        def _(pool):
            nc.gpsimd.memset(all_ones[:], 1.0)
            nc.gpsimd.memset(lower[:], 1.0)
            pool.drain()
            nc.gpsimd.affine_select(out=lower[:], in_=lower[:], compare_op=ALU.is_gt, fill=0.0, base=0,
                                    pattern=[[1, TP]], channel_multiplier=-1).then_inc(masks, 1)
            with pool.Fori(0, NB) as b:
                pool.wait_ge(xn_ready, OPEN + b + 1)
                nc.gpsimd.tensor_copy(s.own[:, bass.ds(b * BT, BT), :], xn[:]).then_inc(kept, 1)
            pool.wait_ge(placed, 1)
            pool.wait_ge(kept, OPEN + NB)
            for t in range(NT):
                for c in range(2):
                    nc.gpsimd.indirect_dma_start(out=s.xs, out_offset=bass.IndirectOffsetOnAxis(ap=pos[:, 2 * t + c:2 * t + c + 1], axis=0),
                                                 in_=s.own[:, t, :], in_offset=None).then_inc(sent, 16)
            pool.wait_ge(sent, 16 * 2 * NT)

        @block.tensor
        def _(pe):
            pe.wait_ge(consts, 32 if second else 64)
            with pe.Fori(0, NB) as b:
                pe.wait_ge(xn_ready, OPEN + b + 1)
                pe.wait_ge(xT_ready, OPEN + b)
                for j in range(BT):
                    for c in range(2):
                        last = nc.tensor.transpose(ps[:, j, c * 128:c * 128 + TP], xn[:, j, c * 128:(c + 1) * 128], s.ident[0:TP, 0:TP])
                last.then_inc(turned, 1)
                pe.wait_ge(xT_ready, OPEN + b + 1)
                pe.wait_ge(taken, OPEN + b)
                if second:
                    for j in range(BT):
                        o = ps[0:TP, 7, j * 16:j * 16 + X]
                        for c in range(2):
                            nc.tensor.matmul(o, xT[:, c, j * TP:(j + 1) * TP], gw[:, c, 0:X], start=c == 0, stop=False)
                        last = nc.tensor.matmul(o, s.ones[0:1, 0:TP], gb[0:1, 0:X], start=False, stop=True)
                else:
                    pe.wait_ge(rh_ready, OPEN + b)
                    for k, (a, n) in enumerate(CUTS):
                        for c in range(2):
                            last = nc.tensor.matmul(ps[:, 5 + k, 0:n], gw[:, c, :], xT[:, c, a:a + n], start=c == 0, stop=c == 1)
                    last.then_inc(rh_sum, 1)
                    pe.wait_ge(rh_ready, OPEN + b + 1)
                    for j in range(BT):
                        o = ps[0:TP, 7, j * 16:j * 16 + X]
                        nc.tensor.matmul(o, rh[:, j * TP:(j + 1) * TP], rw2[:, 0:X], start=True, stop=False)
                        last = nc.tensor.matmul(o, s.ones[0:1, 0:TP], gb[0:1, 0:X], start=False, stop=True)
                last.then_inc(scored, 1)
            pe.wait_ge(masks, 1)
            pe.wait_ge(both_ready, 1)
            pe.wait_ge(xT_ready, OPEN + NB)
            nc.tensor.matmul(ps[0:TP, 0, 0:NT * X], lower[:], both[:].rearrange("p t x -> p (t x)"), start=True, stop=True)
            nc.tensor.matmul(ps[0:TP, 1, 0:NT * X], all_ones[:], both[:].rearrange("p t x -> p (t x)"), start=True, stop=True).then_inc(ranked, 1)

        @block.scalar
        def _(act):
            act.wait_ge(consts, 32 if second else 64)
            with act.Fori(0, NB) as b:
                act.wait_ge(turned, OPEN + b + 1)
                act.wait_ge(scored, OPEN + b)
                nc.scalar.copy(xT[:].rearrange("p c (j n) -> p j c n", j=BT),
                               ps[:, 0:BT, 0:256].rearrange("p j (c n) -> p j c n", c=2)[:, :, :, 0:TP]).then_inc(xT_ready, 1)
                if not second:
                    act.wait_ge(rh_sum, OPEN + b + 1)
                    for k, (a, n) in enumerate(CUTS):
                        last = nc.scalar.activation(rh[:, a:a + n], ps[:, 5 + k, 0:n], ACT.Relu, bias=rb1[:])
                    last.then_inc(rh_ready, 1)
            if not second:
                act.wait_ge(asked, 1)
                nc.scalar.activation(ex[:], score[:, :, 0:X], ACT.Exp).then_inc(answered, 1)
            act.wait_ge(asked, 1 if second else 2)
            nc.scalar.activation(q[:], gap[:], ACT.Exp).then_inc(answered, 1)

        @block.vector
        def _(dve):
            nc.vector.memset(score[:], -1.0)
            nc.vector.memset(before[:], 0.0)
            nc.vector.memset(begins[:], 0.0)
            nc.vector.tensor_scalar(marks[:], s.iota64[0:TP, 0:NT], 128.0, None, ALU.mult)
            dve.drain()
            with dve.Fori(0, NB) as b:
                dve.wait_ge(turned, OPEN + b)
                dve.wait_ge(kept, OPEN + b)
                for j in range(BT):
                    t = b * BT + j
                    last = nc.vector.tensor_scalar(xn[:, j, :], tile_of(s.x, t), s.mv[:, bass.ds(t, 1), 0], s.rstd[:, bass.ds(t, 1)],
                                                   ALU.subtract, ALU.mult)
                last.then_inc(xn_ready, 1)
                dve.wait_ge(scored, OPEN + b + 1)
                nc.vector.tensor_copy(score[:, bass.ds(b * BT, BT), 0:X],
                                      ps[0:TP, 7, 0:BT * 16].rearrange("p (j x) -> p j x", j=BT)[:, :, 0:X]).then_inc(taken, 1)
            dve.drain()
            if not second:
                nc.vector.tensor_reduce(mxs[:], score[:, :, 0:X], AX_X, ALU.max)
                dve.drain()
                nc.vector.tensor_tensor(score[:, :, 0:X], score[:, :, 0:X], bc(mxs[:], 2, X), ALU.subtract).then_inc(asked, 1)
                dve.wait_ge(answered, 1)
                nc.vector.tensor_reduce(tot[:], ex[:], AX_X, ALU.add)
                dve.drain()
                nc.vector.reciprocal(tot[:], tot[:])
                dve.drain()
                nc.vector.tensor_tensor(score[:, :, 0:X], ex[:], bc(tot[:], 2, X), ALU.mult)
                dve.drain()
            for t in range(NT):
                nc.vector.max(top[:, t, :], score[:, t, :])
            dve.drain()
            nc.vector.tensor_tensor(gap[:], top[:, :, 1], top[:, :, 0], ALU.subtract).then_inc(asked, 1)
            for t in range(NT):
                nc.vector.max_index(topi[:, t, :], top[:, t, :], score[:, t, :])
            dve.drain()
            nc.vector.tensor_copy(chosen[:], topi[:, :, 0:2])
            dve.drain()
            for c in range(2):
                nc.vector.tensor_tensor(picks[c][:], bc(s.iota64[0:TP, 0:X], 1, NT), bc(chosen[:, :, c], 2, X), ALU.is_equal)
            dve.drain()
            nc.vector.tensor_tensor(both[:], picks[0][:], picks[1][:], ALU.add).then_inc(both_ready, 1)
            dve.wait_ge(answered, 1 if second else 2)
            nc.vector.tensor_scalar(tot[:], q[:], 1.0, None, ALU.add)
            dve.drain()
            nc.vector.reciprocal(w12[:, :, 0], tot[:])
            dve.drain()
            nc.vector.tensor_tensor(w12[:, :, 1], q[:], w12[:, :, 0], ALU.mult)
            dve.wait_ge(ranked, 1)
            totals = ps[0:TP, 1, 0:NT * X].rearrange("p (t x) -> p t x", t=NT)
            for t in range(NT):
                nc.vector.tensor_tensor(before[:, t + 1, :], before[:, t, :], totals[:, t, :], ALU.add)
                dve.drain()
            nc.vector.tensor_tensor(full[:], bc(marks[:], 1, X), bc(before[:, NT, :], 2, NT), ALU.is_lt)
            dve.drain()
            nc.vector.tensor_reduce(used[:], full[:], AX_X, ALU.add)
            dve.drain()
            for x in range(X):
                nc.vector.tensor_tensor(begins[:, x + 1:x + 2], begins[:, x:x + 1], used[:, x:x + 1], ALU.add)
                dve.drain()
            nc.vector.tensor_copy(tiles[:], begins[0:1, X:X + 1])
            nc.vector.tensor_tensor(past[:], bc(begins[0:1, 1:X + 1], 1, TM), bc(s.iota64[0:1, 0:TM], 2, X), ALU.is_le)
            nc.vector.tensor_scalar(used[:], begins[:, 0:X], 128.0, None, ALU.mult)
            nc.vector.tensor_tensor(place[:], before[:, 0:NT, :], ps[0:TP, 0, 0:NT * X].rearrange("p (t x) -> p t x", t=NT), ALU.add)
            dve.drain()
            nc.vector.tensor_reduce(expert_f[:], past[:], AX_X, ALU.add)
            nc.vector.tensor_tensor(place[:], place[:], bc(used[:], 1, NT), ALU.add)
            dve.drain()
            nc.vector.tensor_scalar(expert[:], expert_f[:], float(X - 1), None, ALU.min)
            for c in range(2):
                nc.vector.tensor_tensor(picks[c][:], picks[c][:], place[:], ALU.mult)
            dve.drain()
            for c in range(2):
                nc.vector.tensor_reduce(posf[:, :, c:c + 1], picks[c][:], AX_X, ALU.add)
            dve.drain()
            nc.vector.tensor_copy(pos[:], posf[:].rearrange("p t c -> p (t c)")).then_inc(placed, 1)


def run_experts(nc, s, m, expert, tiles):
    X, H = m.experts, m.hidden
    L = len(H)
    with ExitStack() as ctx:
        sem = lambda name: ctx.enter_context(nc.semaphore(m.prefix + name))
        sb = lambda name, shape, dt: ctx.enter_context(nc.sbuf_tensor(m.prefix + name, shape, dt))
        slots = lambda name, shape, n=SL: [sb(f"{name}{u}", shape, F32) for u in range(n)]
        xr, wts, y = slots("xr", [128, D]), slots("wts", [128, m.width]), slots("y", [128, D])
        eT = slots("eT", [128, 2, 128], 2)
        h = [slots(f"h{k}_", [128, n, 128], 2) for k, (_, _, n, _) in enumerate(H)]
        bias = [sb(f"bias{k}", [128, X, n], F32) for k, (_, _, n, _) in enumerate(H)]
        obias = sb("obias", [128, X, D], F32)
        rows_in = [sem(f"rows_in{u}") for u in range(SL)]
        y_out, y_free = sem("y_out"), sem("y_free")
        e_consts, e_turned, eT_ready, out_sum, y_ready = [sem(n) for n in ("e_consts", "e_turned", "eT_ready", "out_sum", "y_ready")]
        hid_sum, hid_ready = [[sem(f"{n}{k}") for k in range(L)] for n in ("hid_sum", "hid_ready")]
        n_consts = 16 * (1 + sum(n for _, _, n, _ in H))
        n_in = 16 * (2 + L)
        ps = s.ps
        xT_ps = [ps[:, z, 0:256].rearrange("p (c n) -> p c n", c=2) for z in range(2)]
        out_ps = [ps[:, 2 + z, 0:D] for z in range(2)]
        hid = [[ps[:, 4 + 2 * k + z, 0:n * 128].rearrange("p (f n) -> p f n", f=n) for z in range(2)] for k, (_, _, n, _) in enumerate(H)]
        bodies = lambda eng: (eng.value_load(tiles[0:1, 0:1], min_val=1, max_val=TM) + (SL - 1)) // SL
        block = ctx.enter_context(nc.Block())

        def in_turn(steps):
            for turn in range(SL + len(steps) - 1):
                for lag, step in enumerate(steps):
                    if 0 <= turn - lag < SL:
                        step(turn - lag)

        @block.sync
        def _(sp):
            open_counts(sp, e_turned, eT_ready, out_sum, y_ready, y_free, hid_sum, hid_ready)
            sp.dma_start(obias[:], rows(s.ins[m.out_bias].rearrange("x d -> (x d)"), 128)).then_inc(e_consts, 16)
            with nc.allow_non_contiguous_dma(reason="biases by partition"):
                for k, (_, bname, n, _) in enumerate(H):
                    for f in range(n):
                        sp.dma_start(bias[k][:, :, f], s.ins[bname][:, f * 128:(f + 1) * 128].rearrange("x p -> p x")).then_inc(e_consts, 16)
            with sp.Fori(0, bodies(sp)) as b:
                for u in range(SL):
                    i = b * SL + u
                    e = sp.value_load(expert[0:1, bass.ds(i, 1)], min_val=0, max_val=X - 1)
                    sp.wait_ge(out_sum, OPEN + b * SL + u + 1 - SL)
                    sp.dma_start(xr[u][:], s.xs[bass.ds(i * 128, 128), :]).then_inc(rows_in[u], 16)
                    at = 0
                    for name, _, n, kc in H:
                        src = s.ins[name][bass.ds(e, 1)].rearrange("x (c k) n -> k (x c) n", k=128)
                        sp.dma_start(wts[u][:, at:at + kc * n * 128].rearrange("p (c n) -> p c n", c=kc), src).then_inc(rows_in[u], 16)
                        at += kc * n * 128
                    src = s.ins[m.out][bass.ds(e, 1)].rearrange("x (c k) n -> k (x c) n", k=128)
                    sp.dma_start(wts[u][:, at:at + m.out_chunks * D].rearrange("p (c n) -> p c n", c=m.out_chunks), src).then_inc(rows_in[u], 16)

        @block.gpsimd
        def _(pool):
            with pool.Fori(0, bodies(pool)) as b:
                for u in range(SL):
                    pool.drain()
                    pool.wait_ge(y_ready, OPEN + b * SL + u + 1)
                    nc.gpsimd.tensor_tensor(s.tick[0:1, 0:1], s.tick[0:1, 2:3], s.tick[0:1, 3:4], ALU.add)
                    pool.dma_start(s.ys[bass.ds((b * SL + u) * 128, 128), :], y[u][:]).then_inc(y_out, 16)
                    pool.wait_ge(y_out, (b * SL + u) * 16 + 16)
                    nc.gpsimd.tensor_tensor(s.tick[0:1, 1:2], s.tick[0:1, 2:3], s.tick[0:1, 3:4], ALU.add).then_inc(y_free, 1)

        @block.tensor
        def _(pe):
            with pe.Fori(0, bodies(pe)) as b:
                i = b * SL

                def turn(u):
                    pe.wait_ge(rows_in[u], b * n_in + n_in)
                    pe.wait_ge(eT_ready, OPEN + i + u + 1 - 2)
                    for c in range(2):
                        last = nc.tensor.transpose(xT_ps[u % 2][:, c, :], xr[u][:, c * 128:(c + 1) * 128], s.ident[:])
                    last.then_inc(e_turned, 1)

                def hidden(k, at):
                    _, _, n, kc = H[k]

                    def step(u):
                        if k == 0:
                            pe.wait_ge(eT_ready, OPEN + i + u + 1)
                        else:
                            pe.wait_ge(hid_ready[k - 1], OPEN + i + u + 1)
                        pe.wait_ge(hid_ready[k], OPEN + i + u + 1 - 2)
                        frm = h[k - 1][u % 2] if k else eT[u % 2]
                        for f in range(n):
                            for c in range(kc):
                                last = nc.tensor.matmul(hid[k][u % 2][:, f, :], wts[u][:, at + (c * n + f) * 128:at + (c * n + f + 1) * 128], frm[:, c, :],
                                                        start=c == 0, stop=c == kc - 1)
                        last.then_inc(hid_sum[k], 1)
                    return step

                def output(u):
                    pe.wait_ge(hid_ready[L - 1], OPEN + i + u + 1)
                    pe.wait_ge(y_ready, OPEN + i + u + 1 - 2)
                    at = m.width - m.out_chunks * D
                    for c in range(m.out_chunks):
                        last = nc.tensor.matmul(out_ps[u % 2], h[L - 1][u % 2][:, c, :], wts[u][:, at + c * D:at + (c + 1) * D],
                                                start=c == 0, stop=c == m.out_chunks - 1)
                    last.then_inc(out_sum, 1)

                starts = np.cumsum([0] + [n * kc * 128 for _, _, n, kc in H])
                in_turn([turn] + [hidden(k, int(starts[k])) for k in range(L)] + [output])

        @block.scalar
        def _(act):
            act.wait_ge(e_consts, n_consts)
            with act.Fori(0, bodies(act)) as b:
                i = b * SL

                def take(u):
                    act.wait_ge(e_turned, OPEN + i + u + 1)
                    act.wait_ge(hid_sum[0], OPEN + i + u + 1 - 2)
                    nc.scalar.copy(eT[u % 2][:], xT_ps[u % 2]).then_inc(eT_ready, 1)

                def activate(k):
                    def step(u):
                        e = act.value_load(expert[0:1, bass.ds(i + u, 1)], min_val=0, max_val=X - 1)
                        act.wait_ge(hid_sum[k], OPEN + i + u + 1)
                        act.wait_ge(hid_sum[k + 1] if k + 1 < L else out_sum, OPEN + i + u + 1 - 2)
                        for f in range(H[k][2]):
                            last = nc.scalar.activation(h[k][u % 2][:, f, :], hid[k][u % 2][:, f, :], ACT.Relu,
                                                        bias=bias[k][:, bass.ds(e, 1), f:f + 1].rearrange("p x f -> p (x f)"))
                        last.then_inc(hid_ready[k], 1)
                    return step

                in_turn([take] + [activate(k) for k in range(L)])

        @block.vector
        def _(dve):
            dve.wait_ge(e_consts, n_consts)
            with dve.Fori(0, bodies(dve)) as b:
                for u in range(SL):
                    e = dve.value_load(expert[0:1, bass.ds(b * SL + u, 1)], min_val=0, max_val=X - 1)
                    dve.wait_ge(out_sum, OPEN + b * SL + u + 1)
                    dve.wait_ge(y_free, OPEN + b * SL + u + 1 - SL)
                    nc.vector.tensor_tensor(y[u][:], out_ps[u % 2], obias[:, bass.ds(e, 1), :].rearrange("p x d -> p (x d)"), ALU.add).then_inc(y_ready, 1)


def combine(nc, s, m, second, w12, pos):
    with ExitStack() as ctx:
        sem = lambda name: ctx.enter_context(nc.semaphore(m.prefix + name))
        sb = lambda name, shape, dt: ctx.enter_context(nc.sbuf_tensor(m.prefix + name, shape, dt))
        yg = [sb(f"yg{z}", [TP, BT, 2, D], F32) for z in range(2)]
        fetched, used_up = [sem(f"fetched{z}") for z in range(2)], sem("used_up")
        if second:
            gamma, beta = sb("gamma", [TP, D], F32), sb("beta", [TP, D], F32)
            ob = [sb(f"ob{z}", [TP, BT, D], F32) for z in range(2)]
            st6, mv, eps, half, rstd = sb("st6", [TP, BT, 6], F32), sb("mv", [TP, BT, 2], F32), sb("eps", [TP, BT], F32), sb("half", [TP, BT], F32), sb("rstd", [TP, BT], F32)
            gb_in, ob_ready, ob_out0, ob_out1 = [sem(n) for n in ("gb_in", "ob_ready", "ob_out0", "ob_out1")]
            moments, scales, counted = s.moments, s.scales, 3
            ob_out = [ob_out0, ob_out1]
        block = ctx.enter_context(nc.Block())

        @block.sync
        def _(sp):
            if second:
                sp.dma_start(gamma[:], rows(s.ins["L1_ffn_gamma"], TP)).then_inc(gb_in, 16)
                sp.dma_start(beta[:], rows(s.ins["L1_ffn_beta"], TP)).then_inc(gb_in, 16)
                for b in range(NB):
                    sp.wait_ge(ob_ready, b + 1)
                    sp.dma_start(s.out[b * TOK:(b + 1) * TOK, :].rearrange("(t p) d -> p t d", p=TP), ob[b % 2][:]).then_inc(ob_out[b % 2], 16)
                for z in range(2):
                    sp.wait_ge(ob_out[z], 16 * len(range(z, NB, 2)))

        @block.gpsimd
        def _(pool):
            def scale(b):
                pool.wait_ge(moments, counted + b + 1)
                nc.gpsimd.tensor_tensor(rstd[:], eps[:], half[:], ALU.pow).then_inc(scales, 1)

            for b in range(NB):
                if b >= 2:
                    pool.wait_ge(used_up, b - 1)
                for j in range(BT):
                    for c in range(2):
                        at = 2 * (b * BT + j) + c
                        nc.gpsimd.indirect_dma_start(out=yg[b % 2][:, j, c, :], out_offset=None, in_=s.ys,
                                                     in_offset=bass.IndirectOffsetOnAxis(ap=pos[:, at:at + 1], axis=0)).then_inc(fetched[b % 2], 16)
                if second and b:
                    scale(b - 1)
            if second:
                scale(NB - 1)

        @block.vector
        def _(dve):
            if second:
                nc.vector.memset(half[:], -0.5)
                dve.wait_ge(gb_in, 32)
            for b in range(NB):
                dve.wait_ge(fetched[b % 2], 16 * 2 * BT * (b // 2 + 1))
                for c in range(2):
                    for j in range(BT):
                        t = b * BT + j
                        row = s.own[:, t, :] if second else s.x[:, t, :]
                        last = nc.vector.scalar_tensor_tensor(out=row, in0=yg[b % 2][:, j, c, :], scalar=w12[:, t, c:c + 1], in1=row, op0=ALU.mult, op1=ALU.add)
                    if c:
                        last.then_inc(used_up, 1)
                    dve.drain()
                if not second:
                    continue
                for j in range(BT):
                    nc.vector.bn_stats(st6[:, j, :], s.own[:, b * BT + j, :])
                dve.drain()
                for j in range(BT):
                    nc.vector.bn_aggr(mv[:, j, :], st6[:, j, :])
                dve.drain()
                nc.vector.tensor_scalar(eps[:], mv[:, :, 1], EPS, None, ALU.add).then_inc(moments, 1)
                dve.wait_ge(scales, counted + b + 1)
                o = ob[b % 2]
                if b >= 2:
                    dve.wait_ge(ob_out[b % 2], 16 * (b // 2))
                for j in range(BT):
                    nc.vector.tensor_scalar(o[:, j, :], s.own[:, b * BT + j, :], mv[:, j, 0:1], rstd[:, j:j + 1], ALU.subtract, ALU.mult)
                dve.drain()
                nc.vector.tensor_tensor(o[:], o[:], bc(gamma[:], 1, BT), ALU.mult)
                dve.drain()
                nc.vector.tensor_tensor(o[:], o[:], bc(beta[:], 1, BT), ALU.add)
                dve.drain()
                nc.vector.tensor_tensor(o[:], o[:], s.x[:, b * BT:(b + 1) * BT, :], ALU.add).then_inc(ob_ready, 1)


def stage_experts(nc, s):
    m = Mixture("x_", 6, (("L0_ffn_expert_w1", "L0_ffn_expert_b1", 2, 2), ("L0_ffn_expert_w2", "L0_ffn_expert_b2", 2, 2)),
                "L0_ffn_expert_w3", 2, "L0_ffn_expert_b3")
    stage_mixture(nc, s, m, False)
    normalise(nc, s, "n3_", 2)


def stage_experts2(nc, s):
    m = Mixture("y_", 16, (("L1_ffn_w1", "L1_ffn_b1", 4, 2),), "L1_ffn_w2", 4, "L1_ffn_b2")
    stage_mixture(nc, s, m, True)


class Shared:
    pass


def program(nc, ins, out, stages=99):
    s = Shared()
    s.x_dram, s.src, s.dst, s.W, s.attn_l, s.attn_r = [ins[n] for n in ("x", "src", "dst", "L0_gnn_W", "L0_gnn_attn_l", "L0_gnn_attn_r")]
    s.ins, s.out = ins, out
    s.dpad = nc.dram_tensor("dpad", (NG * GE,), I32, kind="Internal").ap()
    s.grp = nc.dram_tensor("grp", (NG, 2), F32, kind="Internal").ap()
    s.a1tab = nc.dram_tensor("a1tab", (N, A1P * HEADS), BF16, kind="Internal").ap()
    s.ftab = nc.dram_tensor("ftab", (N, FTW), F32, kind="Internal").ap()
    s.tab = nc.dram_tensor("tab", (NPAD, TW), BF16, kind="Internal").ap()
    s.htab = nc.dram_tensor("htab", (N, D), F32, kind="Internal").ap()
    s.xs = nc.dram_tensor("xs", (TM * 128, D), F32, kind="Internal").ap()
    s.ys = nc.dram_tensor("ys", (TM * 128, D), F32, kind="Internal").ap()
    with ExitStack() as ctx:
        sb = lambda name, shape, dt: ctx.enter_context(nc.sbuf_tensor(name, shape, dt))
        s.moments, s.scales = [ctx.enter_context(nc.semaphore(n)) for n in ("moments", "scales")]
        s.ps = ctx.enter_context(nc.psum_tensor("ps", [128, 8, 512], F32))
        s.ident, s.identb = sb("ident", [128, 128], F32), sb("identb", [128, 128], BF16)
        s.sel = sb("sel", [GT * A1P * HEADS, HEADS, 128], BF16)
        s.iota64, s.part = sb("iota64", [128, W64], F32), sb("part", [128, 2], F32)
        s.tick = sb("tick", [1, 4], F32)
        s.fold = sb("fold", [A1P * (HEADS + 1), HEADS + 1], F32)
        s.ones = sb("ones", [1, 128], F32)
        s.dcol, s.scol = sb("dcol", [128, CH * 128], F32), sb("scol", [128, CH * 128], I32)
        s.gmm, s.widest = sb("gmm", [128, 2 * NG], F32), sb("widest", [128, 1], I32)
        s.x = sb("x", [TP, NT, D], F32)
        s.a2 = sb("a2", [TP, NT, HEADS], F32)
        s.accT = sb("accT", [128, 2, NPAD], F32)
        s.ndT = sb("ndT", [A1P * (HEADS + 1), NPAD], F32)
        s.mv, s.rstd = sb("mv", [TP, NT, 2], F32), sb("rstd", [TP, NT], F32)
        s.rdeg = sb("rdeg", [TP, NT], F32)
        s.own = sb("own", [TP, NT, D], F32)
        for n, stage in enumerate((stage_edges, stage_project, stage_maxima, stage_attend, stage_join, stage_experts, stage_share, stage_aggregate, stage_join2, stage_experts2)):
            if n < stages:
                stage(nc, s)


def kernel(**inputs):
    import concourse.bacc as bacc
    from concourse.bass_utils import run_bass_kernel_spmd

    nc = bacc.Bacc("TRN2", target_bir_lowering=False, num_devices=1)
    arrays, aps = {}, {}
    for name, value in inputs.items():
        a = np.ascontiguousarray(value)
        arrays[f"in_{name}_dram"] = a
        aps[name] = nc.dram_tensor(f"in_{name}_dram", a.shape, mybir.dt.from_np(a.dtype), kind="ExternalInput").ap()
    out = nc.dram_tensor("out_dram", (N, D), F32, kind="ExternalOutput").ap()
    program(nc, aps, out)
    r = run_bass_kernel_spmd(nc, [arrays], core_ids=[0])
    return r.results[0]["out_dram"]
```

```python
from contextlib import ExitStack

import numpy as np
import concourse.bass as bass
from concourse import mybir

F32 = mybir.dt.float32
BF16 = mybir.dt.bfloat16
I32 = mybir.dt.int32
U32 = mybir.dt.uint32
ALU = mybir.AluOpType
ACT = mybir.ActivationFunctionType
AX_X = mybir.AxisListType.X

N, E, D = 3125, 103125, 256
HEADS, HD = 8, 32
TP, NT = 125, 25
GT = 4
GE = GT * 128
SL = 4
NG = -(-E // (GE * SL)) * SL
NGS = NG // SL
NG2 = NG // 2
ETILES = -(-E // 128)
CH = 7
W32, W64 = 32, 64
NPAD = N + W64
FTW = D + HEADS
BIG = 1.0e30
TM = 64
BT = 5
NB = NT // BT
TOK = BT * TP
CUTS = ((0, 313), (313, 312))
EPS = 1e-5
A1P = 3
TW = A1P * 2 * HEADS + HEADS
OPEN = SL
assert NG % SL == 0 and (2 * N + 16 * 127) // 128 <= TM and TM % SL == 0 and TP * NT == N and (CH - 1) * 128 < NG * GT <= CH * 128


def bc(ap, axis, n):
    a = ap.unsqueeze(axis)
    shape = list(a.shape)
    shape[axis] = n
    return a.broadcast_to(shape)


def rows(ap, n):
    return ap.partition_broadcast(n)


def open_counts(sp, *sems):
    for sem in sems:
        for one in sem if isinstance(sem, list) else [sem]:
            sp.sem_inc(one, OPEN)


def stage_edges(nc, s):
    with ExitStack() as ctx:
        sem = lambda name: ctx.enter_context(nc.semaphore("e_" + name))
        sb = lambda name, shape, dt: ctx.enter_context(nc.sbuf_tensor("e_" + name, shape, dt))
        d_rows, s_rows = sb("d_rows", [128, CH, 128], I32), sb("s_rows", [128, CH, 128], I32)
        d_f, s_f = sb("d_f", [128, CH, 128], F32), sb("s_f", [128, CH, 128], F32)
        tail = sb("tail", [1, NG * GE - E], I32)
        zrow = sb("zrow", [W64, TW], BF16)
        d_grp = sb("d_grp", [NG2, 2, GE], I32)
        low = sb("low", [NG2, 2, GE], F32)
        ext = sb("ext", [NG2, 2, 2], F32)
        span = sb("span", [128, NG], F32)
        smax = sb("smax", [128, 1], F32)
        sel_f = sb("sel_f", [GT * A1P * HEADS, HEADS, 128], F32)
        ioti = sb("ioti", [128, W64], I32)
        parti = sb("parti", [128, 2], I32)
        cleared, padded, loaded, floats, turned, stats, stored, spread, pool_c = [
            sem(n) for n in ("cleared", "padded", "loaded", "floats", "turned", "stats", "stored", "spread", "pool_c")]
        ps = s.ps
        full = ETILES - 1
        rest = E - full * 128
        block = ctx.enter_context(nc.Block())

        @block.gpsimd
        def _(pool):
            nc.gpsimd.memset(tail[:], -1).then_inc(cleared, 1)
            nc.gpsimd.memset(s.zero_rows[:], 0.0).then_inc(cleared, 1)
            nc.gpsimd.memset(sel_f[:], 0.0)
            nc.gpsimd.memset(s.tick[:], 0.0)
            nc.gpsimd.memset(s_rows[:, CH - 1, :], 0).then_inc(cleared, 1)
            nc.gpsimd.memset(d_rows[:, CH - 1, :], -1).then_inc(cleared, 1)
            nc.gpsimd.memset(zrow[:], 0.0).then_inc(cleared, 1)
            nc.gpsimd.memset(s.ident[:], 0.0)
            nc.gpsimd.memset(s.fold[:], 0.0)
            pool.drain()
            nc.gpsimd.affine_select(out=s.ident[:], in_=s.ident[:], compare_op=ALU.not_equal, fill=1.0, base=0,
                                    pattern=[[-1, 128]], channel_multiplier=1).then_inc(pool_c, 1)
            for a in range(A1P):
                pool.drain()
                nc.gpsimd.affine_select(out=sel_f[:], in_=sel_f[:], compare_op=ALU.not_equal, fill=1.0, base=-a * HEADS,
                                        pattern=[[-1, HEADS], [-A1P * HEADS, GT], [0, W32]], channel_multiplier=1)
            pool.drain()
            for a in range(A1P):
                nc.gpsimd.affine_select(out=s.fold[:], in_=s.fold[:], compare_op=ALU.not_equal, fill=1.0, base=-a * (HEADS + 1),
                                        pattern=[[-1, HEADS + 1]], channel_multiplier=1)
                pool.drain()
            nc.gpsimd.iota(ioti[:], pattern=[[1, W64]], base=0, channel_multiplier=0).then_inc(pool_c, 1)
            nc.gpsimd.iota(parti[:, 0:1], pattern=[[1, 1]], base=0, channel_multiplier=1).then_inc(pool_c, 1)
            for j in range(GT):
                pool.drain()
                nc.gpsimd.iota(parti[32 * j:32 * j + 32, 1:2], pattern=[[1, 1]], base=0,
                               channel_multiplier=1).then_inc(pool_c, 1)

        @block.sync
        def _(sp):
            sp.wait_ge(cleared, 5)
            sp.dma_start(s.dpad[0:E], s.dst).then_inc(padded, 16)
            sp.dma_start(s.dpad[E:NG * GE], tail[:]).then_inc(padded, 16)
            sp.dma_start(s.tab[N:N + W64, :], zrow[:]).then_inc(padded, 16)
            for c in range(CH - 1):
                sp.dma_start(s_rows[:, c, :], s.src[c * 16384:(c + 1) * 16384].rearrange("(p e) -> p e", e=128)).then_inc(loaded, 16)
            a = (CH - 1) * 16384
            sp.dma_start(s_rows[0:full - 128 * (CH - 1), CH - 1, :], s.src[a:full * 128].rearrange("(p e) -> p e", e=128)).then_inc(loaded, 16)
            r = full - 128 * (CH - 1)
            sp.dma_start(s_rows[r:r + 1, CH - 1, 0:rest], s.src[full * 128:E].rearrange("(p e) -> p e", p=1)).then_inc(loaded, 16)
            sp.wait_ge(padded, 48)
            for c in range(CH):
                n = min(128, NG * GT - c * 128)
                sp.dma_start(d_rows[0:n, c, :], s.dpad[c * 16384:c * 16384 + n * 128].rearrange("(p e) -> p e", e=128)).then_inc(loaded, 16)
            sp.dma_start(d_grp[:], s.dpad[0:NG * GE].rearrange("(q p e) -> p q e", q=2, e=GE)).then_inc(loaded, 16)
            sp.wait_ge(stats, 1)
            with nc.allow_non_contiguous_dma(reason="one number per group"):
                for q in range(2):
                    sp.dma_start(s.grp[q * NG2:(q + 1) * NG2, :], ext[:, q, :]).then_inc(stored, 16)
            sp.wait_ge(stored, 32)
            sp.dma_start(s.gmm[:], rows(s.grp.rearrange("g m -> (g m)"), 128)).then_inc(spread, 16)
            sp.dma_start(s.x[:], s.x_dram.rearrange("(t p) d -> p t d", p=TP)).then_inc(s.x_in, 16)
            sp.wait_ge(spread, 16)

        @block.vector
        def _(dve):
            dve.wait_ge(loaded, 16 * (CH + 1 + CH + 1))
            nc.vector.tensor_copy(s_f[:], s_rows[:]).then_inc(floats, 1)
            nc.vector.tensor_copy(d_f[:], d_rows[:]).then_inc(floats, 1)
            nc.vector.tensor_scalar(low[:], d_grp[:], 0.0, 8192.0, ALU.is_lt, ALU.mult)
            dve.drain()
            nc.vector.tensor_tensor(low[:], low[:], d_grp[:], ALU.add)
            dve.drain()
            nc.vector.tensor_reduce(ext[:, :, 0:1], low[:], AX_X, ALU.min)
            nc.vector.tensor_reduce(ext[:, :, 1:2], d_grp[:], AX_X, ALU.max)
            dve.drain()
            nc.vector.tensor_copy(smax[0:1, :], ext[0:1, 0, 0:1]).then_inc(stats, 1)
            dve.wait_ge(pool_c, 7)
            nc.vector.tensor_copy(s.iota64[:], ioti[:])
            nc.vector.tensor_copy(s.part[:], parti[:])
            nc.vector.tensor_copy(s.identb[:], s.ident[:])
            nc.vector.tensor_copy(s.sel[:], sel_f[:])
            nc.vector.memset(s.ones[:], 1.0)
            dve.wait_ge(turned, 1)
            nc.vector.tensor_copy(s.scol[:], ps[:, 0:2, :].rearrange("p b c -> p (b c)")[:, 0:CH * 128])
            nc.vector.tensor_copy(s.dcol[:], ps[:, 2:4, :].rearrange("p b c -> p (b c)")[:, 0:CH * 128])
            dve.wait_ge(spread, 16)
            g = s.gmm[:].rearrange("p (g m) -> p g m", m=2)
            nc.vector.tensor_tensor(span[:], g[:, :, 1], g[:, :, 0], ALU.subtract)
            dve.drain()
            nc.vector.tensor_reduce(smax[:], span[:], AX_X, ALU.max)
            dve.drain()
            nc.vector.tensor_copy(s.widest[:], smax[:])

        @block.tensor
        def _(pe):
            pe.wait_ge(pool_c, 7)
            pe.wait_ge(floats, 2)
            for k, f in ((0, s_f), (2, d_f)):
                for c in range(CH):
                    o = ps[:, k + c // 4, 128 * (c % 4):128 * (c % 4) + 128]
                    last = nc.tensor.transpose(o, f[:, c, :], s.ident[:])
            last.then_inc(turned, 1)


def stage_project(nc, s):
    with ExitStack() as ctx:
        sem = lambda name: ctx.enter_context(nc.semaphore("p_" + name))
        sb = lambda name, shape, dt: ctx.enter_context(nc.sbuf_tensor("p_" + name, shape, dt))
        wide = sb("wide", [128, 2, D + 2 * HEADS], F32)
        prod = sb("prod", [128, 2, D], F32)
        attn = sb("attn", [128, 2, D], F32)
        st6, mv = sb("st6", [TP, NT, 6], F32), sb("mv", [TP, NT, 2], F32)
        eps, half, rstd = sb("eps", [TP, NT], F32), sb("half", [TP, NT], F32), sb("rstd", [TP, NT], F32)
        xn, xT = sb("xn", [TP, BT, D], F32), [sb(f"xT{z}", [128, 2, TP], F32) for z in range(2)]
        row, parts, left = sb("row", [TP, NT, FTW], F32), sb("parts", [TP, NT, A1P, HEADS], BF16), sb("left", [TP, NT, HEADS], F32)
        w_in, moments, scales, xn_ready, turned, xT_ready, summed, row_ready, row_out, parts_ready = [
            sem(n) for n in ("w_in", "moments", "scales", "xn_ready", "turned", "xT_ready", "summed", "row_ready", "row_out", "parts_ready")]
        ps = s.ps
        block = ctx.enter_context(nc.Block())

        @block.sync
        def _(sp):
            open_counts(sp, moments, scales, xn_ready, turned, xT_ready, summed, row_ready, parts_ready)
            sp.dma_start(wide[:, :, 0:D], s.W.rearrange("(c k) n -> k c n", k=128)).then_inc(w_in, 16)
            sp.dma_start(attn[:, 0, :], rows(s.attn_l.rearrange("h d -> (h d)"), 128)).then_inc(w_in, 16)
            sp.dma_start(attn[:, 1, :], rows(s.attn_r.rearrange("h d -> (h d)"), 128)).then_inc(w_in, 16)
            sp.dma_start(s.xs.rearrange("(t p) d -> p t d", p=128), bc(s.zero_rows[:], 1, TM)).then_inc(s.slots_out, 16)
            least = 2 * N // 128
            sp.dma_start(s.ys[least * 128:, :].rearrange("(t p) d -> p t d", p=128), bc(s.zero_rows[:], 1, TM - least)).then_inc(s.slots_out, 16)
            with sp.Fori(0, NB) as b:
                sp.wait_ge(row_ready, OPEN + b * BT + BT)
                sp.dma_start(s.ftab[bass.ds(b * TOK, TOK), :].rearrange("(t p) d -> p t d", p=TP), row[:, bass.ds(b * BT, BT), :]).then_inc(row_out, 16)
            sp.wait_ge(parts_ready, OPEN + 1)
            sp.dma_start(s.a1tab.rearrange("(t p) c -> p t c", p=TP), parts[:].rearrange("p t a h -> p t (a h)")).then_inc(row_out, 16)
            sp.wait_ge(row_out, 16 * NB + 16)

        @block.gpsimd
        def _(pool):
            pool.wait_ge(moments, OPEN + 1)
            nc.gpsimd.tensor_tensor(rstd[:], eps[:], half[:], ALU.pow).then_inc(scales, 1)

        @block.vector
        def _(dve):
            dve.wait_ge(w_in, 48)
            for side in range(2):
                nc.vector.tensor_tensor(prod[:], wide[:, :, 0:D], bc(attn[:, side, :], 1, 2), ALU.mult)
                dve.drain()
                for c in range(2):
                    nc.vector.tensor_reduce(wide[:, c, D + HEADS * side:D + HEADS * (side + 1)],
                                            prod[:, c, :].rearrange("p (h d) -> p h d", h=HEADS), AX_X, ALU.add)
                dve.drain()
            dve.wait_ge(s.x_in, 16)
            ln_moments(nc, dve, s.x, st6, mv, eps, half)
            nc.vector.memset(s.ndT[:], -BIG).then_inc(moments, 1)
            dve.wait_ge(scales, OPEN + 1)
            with dve.Fori(0, NB) as b:
                for u in range(BT):
                    t = b * BT + u
                    dve.wait_ge(turned, OPEN + t + 1 - SL)
                    nc.vector.tensor_scalar(xn[:, u, :], tile_of(s.x, t), mv[:, bass.ds(t, 1), 0], rstd[:, bass.ds(t, 1)],
                                            ALU.subtract, ALU.mult).then_inc(xn_ready, 1)
            dve.wait_ge(row_ready, OPEN + NT)
            a1 = row[:, :, D:FTW]
            for a in range(A1P):
                nc.vector.tensor_copy(parts[:, :, a, :], left[:] if a else a1)
                dve.drain()
                if a < A1P - 1:
                    nc.vector.tensor_tensor(left[:], left[:] if a else a1, parts[:, :, a, :], ALU.subtract)
                    dve.drain()
            nc.vector.memset(s.accT[:, 0, 0:1], 0.0).then_inc(parts_ready, 1)

        @block.tensor
        def _(pe):
            with pe.Fori(0, NB) as b:
                i = b * BT

                def turn(u):
                    pe.wait_ge(xn_ready, OPEN + i + u + 1)
                    pe.wait_ge(xT_ready, OPEN + i + u + 1 - ago(u))
                    for c in range(2):
                        last = nc.tensor.transpose(ps[:, u % 2, c * 128:c * 128 + TP], xn[:, u, c * 128:(c + 1) * 128], s.ident[0:TP, 0:TP])
                    last.then_inc(turned, 1)

                def multiply(u):
                    pe.wait_ge(xT_ready, OPEN + i + u + 1)
                    pe.wait_ge(row_ready, OPEN + i + u + 1 - ago(u))
                    for c in range(2):
                        last = nc.tensor.matmul(ps[0:TP, 2 + u % 2, 0:D + 2 * HEADS], xT[u % 2][:, c, :], wide[:, c, :], start=c == 0, stop=c == 1)
                    last.then_inc(summed, 1)

                in_turn(BT, [turn, multiply])

        @block.scalar
        def _(act):
            with act.Fori(0, NB) as b:
                i = b * BT

                def take(u):
                    act.wait_ge(turned, OPEN + i + u + 1)
                    act.wait_ge(summed, OPEN + i + u + 1 - ago(u))
                    nc.scalar.copy(xT[u % 2][:], ps[:, u % 2, 0:256].rearrange("p (c n) -> p c n", c=2)[:, :, 0:TP]).then_inc(xT_ready, 1)

                def keep(u):
                    act.wait_ge(summed, OPEN + i + u + 1)
                    nc.scalar.copy(tile_of(s.a2, i + u), ps[0:TP, 2 + u % 2, FTW:FTW + HEADS])
                    nc.scalar.copy(tile_of(row, i + u), ps[0:TP, 2 + u % 2, 0:FTW]).then_inc(row_ready, 1)

                in_turn(BT, [take, keep])


def tile_of(buf, t):
    return buf[:, bass.ds(t, 1), :].rearrange("p t d -> p (t d)")


def in_turn(n, steps):
    for turn in range(n + len(steps) - 1):
        for lag, step in enumerate(steps):
            if 0 <= turn - lag < n:
                step(turn - lag)


def ago(u):
    return 2 if u else 1


def ln_moments(nc, dve, x, st6, mv, eps, half):
    with dve.Fori(0, NB) as b:
        for j in range(BT):
            nc.vector.bn_stats(tile_of(st6, b * BT + j), tile_of(x, b * BT + j))
    dve.drain()
    for t in range(NT):
        nc.vector.bn_aggr(mv[:, t, :], st6[:, t, :])
    dve.drain()
    nc.vector.tensor_scalar(eps[:], mv[:, :, 1], EPS, None, ALU.add)
    nc.vector.memset(half[:], -0.5)
    dve.drain()


def passes(eng, s, width):
    return eng.value_load(s.widest[0:1, 0:1], min_val=0, max_val=N - 1) // width + 1


def gather_rows(nc, pool, s, width, sidx, dest, table, idx_ready, gathered, ticked):
    with pool.Fori(0, passes(pool, s, width)) as r:
        with pool.Fori(0, NGS) as k:
            for p in range(2):
                pool.wait_ge(idx_ready, OPEN + (r * NGS + k) * 2 + p + 1)
                nc.gpsimd.tensor_tensor(s.tick[0:1, p:p + 1], s.tick[0:1, 2:3], s.tick[0:1, 3:4], ALU.add).then_inc(ticked, 1)
                for u in (2 * p, 2 * p + 1):
                    for j in range(GT):
                        at = (u - 2 * p) * GT + j
                        nc.gpsimd.indirect_dma_start(out=dest[u][:, j, :], out_offset=None, in_=table,
                                                     in_offset=bass.IndirectOffsetOnAxis(ap=sidx[p][:, at:at + 1], axis=0)
                                                     ).then_inc(gathered[u], 16)


def put_indices(nc, act, s, sidx, idx_ready, free, ticked, b, k, p):
    act.wait_ge(ticked, OPEN + b * 2 + p - 1)
    act.wait_ge(free, OPEN + b * SL + 2 * p + 2 - SL)
    nc.scalar.copy(sidx[p][:], s.scol[:, bass.ds(k * (SL * GT) + p * 2 * GT, 2 * GT)]).then_inc(idx_ready, 1)


def stage_maxima(nc, s):
    with ExitStack() as ctx:
        sem = lambda name: ctx.enter_context(nc.semaphore("m_" + name))
        sb = lambda name, shape, dt: ctx.enter_context(nc.sbuf_tensor("m_" + name, shape, dt))
        AW = A1P * HEADS
        slots = lambda name, shape, dt, n=SL: [sb(f"{name}{u}", shape, dt) for u in range(n)]
        sidx = slots("sidx", [128, 2 * GT], I32, 2)
        a1g, a1T = slots("a1g", [128, GT, AW], BF16), slots("a1T", [GT * AW, 128], BF16)
        drow, mask = sb("drow", [128, SL, 128], I32), slots("mask", [128, 128], BF16)
        mx, win = slots("mx", [128, HEADS], F32), slots("win", [HEADS, W32], F32)
        first = sb("first", [128, NG], F32)
        firstw = sb("firstw", [128, NG], F32)
        base = sb("base", [1, NG], I32)
        tabs, vals, left = sb("tabs", [TP, NT, TW], BF16), sb("vals", [TP, NT, 2 * HEADS], F32), sb("left", [TP, NT, 2 * HEADS], F32)
        z = sb("z", [TP, NT, HEADS], F32)
        gathered = [sem(f"gathered{u}") for u in range(SL)]
        idx_ready, ticked, turned, a1T_ready, d_in, mask_ready, spread, mx_ready, mxT_ready, won = [
            sem(n) for n in ("idx_ready", "ticked", "turned", "a1T_ready", "d_in", "mask_ready", "spread", "mx_ready", "mxT_ready", "won")]
        maxima, nodes_turned, tab_out = [sem(n) for n in ("maxima", "nodes_turned", "tab_out")]
        ps = s.ps
        wide = [ps[:, 2 * z:2 * z + 2, :].rearrange("p b c -> p (b c)").rearrange("p (h e) -> p h e", h=HEADS) for z in range(2)]
        a1T_ps = [ps[0:GT * AW, 4 + u % 2, (u // 2) * 128:(u // 2) * 128 + 128] for u in range(SL)]
        mxT_ps = [ps[0:HEADS, 6 + u % 2, (u // 2) * 128:(u // 2) * 128 + 128] for u in range(SL)]
        block = ctx.enter_context(nc.Block())

        @block.gpsimd
        def _(pool):
            gather_rows(nc, pool, s, W32, sidx, a1g, s.a1tab, idx_ready, gathered, ticked)

        @block.sync
        def _(sp):
            open_counts(sp, idx_ready, ticked, turned, a1T_ready, mask_ready, spread, mx_ready, mxT_ready, won, maxima, nodes_turned)
            with sp.Fori(0, passes(sp, s, W32)) as r:
                with sp.Fori(0, NGS) as k:
                    b = r * NGS + k
                    sp.wait_ge(mask_ready, OPEN + b * SL)
                    e = s.dpad[bass.ds(k * SL * GE, SL * GE)].rearrange("(u j e) -> j u e", j=GT, e=128)
                    for j in range(GT):
                        sp.dma_start(drow[j * W32:(j + 1) * W32, :, :], bc(e[j], 0, W32)).then_inc(d_in, 16)
            sp.wait_ge(maxima, OPEN + 2)
            sp.dma_start(s.tab[0:N, :].rearrange("(t p) c -> p t c", p=TP), tabs[:]).then_inc(tab_out, 16)
            sp.wait_ge(tab_out, 16)
            sp.wait_ge(s.slots_out, 32)

        @block.tensor
        def _(pe):
            with pe.Fori(0, passes(pe, s, W32)) as r:
                with pe.Fori(0, NGS) as k:
                    b = r * NGS + k
                    i = b * SL

                    def turn(u):
                        pe.wait_ge(gathered[u], b * (16 * GT) + 16 * GT)
                        pe.wait_ge(a1T_ready, OPEN + i + u + 1 - SL)
                        nc.tensor.matmul(a1T_ps[u], a1g[u][:].rearrange("p j h -> p (j h)"), s.identb[:],
                                         start=True, stop=True).then_inc(turned, 1)

                    def scatter(u):
                        pe.wait_ge(a1T_ready, OPEN + i + u + 1)
                        pe.wait_ge(mask_ready, OPEN + i + u + 1)
                        pe.wait_ge(mx_ready, OPEN + i + u + 1 - 2)
                        for h in range(HEADS):
                            nc.tensor.matmul(wide[u % 2][:, h, :], s.sel[:, h, :], a1T[u][:], start=h % 4 == 0, stop=False, skip_group_check=True)
                        for h in range(HEADS):
                            last = nc.tensor.matmul(wide[u % 2][:, h, :], s.identb[:], mask[u][:], start=False, stop=True, skip_group_check=True)
                        last.then_inc(spread, 1)

                    def fold(u):
                        pe.wait_ge(mx_ready, OPEN + i + u + 1)
                        pe.wait_ge(won, OPEN + i + u + 1 - SL)
                        nc.tensor.transpose(mxT_ps[u], mx[u][:], s.ident[:]).then_inc(mxT_ready, 1)

                    turn(0)
                    turn(1)
                    scatter(0)
                    turn(2)
                    scatter(1)
                    fold(0)
                    turn(3)
                    scatter(2)
                    fold(1)
                    scatter(3)
                    fold(2)
                    fold(3)
            pe.wait_ge(maxima, OPEN + 1)
            for t in range(NT):
                last = nc.tensor.transpose(ps[0:TP, 0, t * HEADS:(t + 1) * HEADS], s.ndT[0:HEADS, t * TP:(t + 1) * TP], s.ident[0:HEADS, 0:HEADS])
            last.then_inc(nodes_turned, 1)

        @block.scalar
        def _(act):
            with act.Fori(0, passes(act, s, W32)) as r:
                def indices(k, p):
                    put_indices(nc, act, s, sidx, idx_ready, turned, ticked, r * NGS + k, k, p)

                def take(k, p):
                    i = (r * NGS + k) * SL
                    for u in (2 * p, 2 * p + 1):
                        act.wait_ge(turned, OPEN + i + u + 1)
                        act.wait_ge(spread, OPEN + i + u + 1 - SL)
                        nc.scalar.copy(a1T[u][:], a1T_ps[u]).then_inc(a1T_ready, 1)

                def body(k, last_body):
                    indices(k, 1)
                    take(k, 0)
                    if not last_body:
                        indices(k + 1, 0)
                    take(k, 1)

                indices(0, 0)
                with act.Fori(0, NGS - 1) as k:
                    body(k, False)
                body(NGS - 1, True)

        @block.vector
        def _(dve):
            start_windows(nc, dve, s, first, firstw, 1)
            with dve.Fori(0, passes(dve, s, W32)) as r:
                nc.vector.tensor_scalar(base[:], first[0:1, :], float(N), None, ALU.min)
                dve.drain()
                with dve.Fori(0, NGS) as k:
                    b = r * NGS + k
                    i = b * SL

                    def maximum(u):
                        dve.wait_ge(spread, OPEN + i + u + 1)
                        dve.wait_ge(mxT_ready, OPEN + i + u + 1 - SL)
                        nc.vector.tensor_reduce(mx[u][:], wide[u % 2], AX_X, ALU.max).then_inc(mx_ready, 1)

                    def keep(u):
                        at = dve.value_load(base[0:1, bass.ds(k * SL + u, 1)], min_val=0, max_val=N)
                        dve.wait_ge(mxT_ready, OPEN + i + u + 1)
                        nc.vector.tensor_reduce(win[u][:], mxT_ps[u].rearrange("h (j w) -> h w j", j=GT), AX_X, ALU.max).then_inc(won, 1)
                        w = s.ndT[0:HEADS, bass.ds(at, W32)]
                        dve.drain()
                        nc.vector.tensor_tensor(w, w, win[u][:], ALU.max)

                    dve.wait_ge(d_in, b * (16 * GT) + 16 * GT)
                    for u in range(SL):
                        dve.wait_ge(spread, OPEN + i + u + 1 - SL)
                        nc.vector.tensor_scalar(mask[u][:], drow[:, u, :], firstw[:, bass.ds(k * SL + u, 1)], -BIG,
                                                ALU.not_equal, ALU.mult).then_inc(mask_ready, 1)
                    maximum(0)
                    maximum(1)
                    keep(0)
                    maximum(2)
                    keep(1)
                    maximum(3)
                    keep(2)
                    keep(3)
                next_windows(nc, dve, first, firstw, W32)
            nc.vector.memset(tabs[:], 1.0).then_inc(maxima, 1)
            dve.wait_ge(nodes_turned, OPEN + 1)
            nc.vector.tensor_tensor(z[:], s.a2[:], ps[0:TP, 0, 0:NT * HEADS].rearrange("p (t h) -> p t h", t=NT), ALU.add)
            dve.drain()
            nc.vector.scalar_tensor_tensor(out=vals[:, :, HEADS:2 * HEADS], in0=z[:], scalar=0.2, in1=z[:], op0=ALU.mult, op1=ALU.max)
            nc.vector.tensor_copy(vals[:, :, 0:HEADS], s.a2[:])
            dve.drain()
            for a in range(A1P):
                part = tabs[:, :, a * 2 * HEADS:(a + 1) * 2 * HEADS]
                nc.vector.tensor_copy(part, (left if a else vals)[:])
                dve.drain()
                if a < A1P - 1:
                    nc.vector.tensor_tensor(left[:], (left if a else vals)[:], part, ALU.subtract)
                    dve.drain()
            nc.vector.memset(s.accT[:], 0.0)
            nc.vector.memset(s.ndT[:], 0.0)
            dve.drain()
            nc.vector.memset(z[:], 0.0).then_inc(maxima, 1)


def start_windows(nc, dve, s, first, firstw, col):
    g = s.gmm[:].rearrange("p (g m) -> p g m", m=2)
    nc.vector.tensor_copy(first[:], g[:, :, 0])
    nc.vector.tensor_scalar(firstw[:], g[:, :, 0], s.part[:, col:col + 1], None, ALU.add)
    dve.drain()


def next_windows(nc, dve, first, firstw, width):
    dve.drain()
    nc.vector.tensor_scalar(first[:], first[:], float(width), None, ALU.add)
    nc.vector.tensor_scalar(firstw[:], firstw[:], float(width), None, ALU.add)
    dve.drain()


def pair_offsets(nc, s, drel, first, k, p):
    nc.vector.tensor_tensor(drel[:].rearrange("p (g j) -> p g j", g=2),
                            s.dcol[:, bass.ds(k * (SL * GT) + p * 2 * GT, 2 * GT)].rearrange("p (g j) -> p g j", g=2),
                            bc(first[:, bass.ds(k * SL + 2 * p, 2)], 2, GT), ALU.subtract)


def stage_attend(nc, s):
    with ExitStack() as ctx:
        sem = lambda name: ctx.enter_context(nc.semaphore("w_" + name))
        sb = lambda name, shape, dt: ctx.enter_context(nc.sbuf_tensor("w_" + name, shape, dt))
        two_sb = lambda name, shape, dt: [sb(f"{name}{p}", shape, dt) for p in range(2)]
        PT = 2 * GT
        EW = A1P * (HEADS + 1)
        sidx, ftp = two_sb("sidx", [128, PT], I32), two_sb("ftp", [128, PT, FTW], F32)
        drow, ohT = two_sb("drow", [W64, 2 * GE], I32), [sb(f"ohT{u}", [W64, GE], BF16) for u in range(SL)]
        tabw = [sb(f"tabw{u}", [W64, TW], BF16) for u in range(SL)]
        z, pen, zl = two_sb("z", [128, PT, HEADS], F32), two_sb("pen", [128, PT, HEADS], F32), two_sb("zl", [128, PT, HEADS], F32)
        looked_up, ohb = two_sb("looked_up", [128, PT, 2 * HEADS], F32), two_sb("ohb", [128, PT, W64], BF16)
        exb, rem = two_sb("exb", [128, PT, A1P, HEADS + 1], BF16), two_sb("rem", [128, PT, HEADS + 1], F32)
        arg = two_sb("arg", [128, PT, HEADS], F32)
        ex = two_sb("ex", [128, PT, HEADS + 1], F32)
        drel, oh = two_sb("drel", [128, PT], F32), two_sb("oh", [128, PT, W64], F32)
        msg = two_sb("msg", [128, PT, D], F32)
        away, nfirstw, one = sb("away", [W64, 2 * GE], F32), sb("nfirstw", [W64, NG], F32), sb("one", [W64, 1], F32)
        first, firstw, base = sb("first", [128, NG], F32), sb("firstw", [128, NG], F32), sb("base", [1, NG], I32)
        slot = lambda pairs, u: pairs[u // 2][:, (u % 2) * GT:(u % 2 + 1) * GT]
        ftg = [slot(ftp, u) for u in range(SL)]
        gathered, tab_in = [[sem(f"{n}{u}") for u in range(SL)] for n in ("gathered", "tab_in")]
        d_in = [sem(f"d_in{p}") for p in range(2)]
        idx_ready, ticked, ohT_ready, looked, arg_ready, ex_ready, ohb_ready, parts_ready, msg_ready, summed, added, base_ready, ones_ready = [sem(n) for n in (
            "idx_ready", "ticked", "ohT_ready", "looked", "arg_ready", "ex_ready", "ohb_ready", "parts_ready", "msg_ready", "summed", "added", "base_ready", "ones_ready")]
        ps = s.ps
        look = [ps[:, p, 0:PT * TW].rearrange("p (j c) -> p j c", j=PT) for p in range(2)]
        acc = [ps[:, 4 + u, 0:3 * W64].rearrange("p (c w) -> p c w", c=3) for u in range(SL)]
        block = ctx.enter_context(nc.Block())

        @block.gpsimd
        def _(pool):
            gather_rows(nc, pool, s, W64, sidx, ftg, s.ftab, idx_ready, gathered, ticked)

        @block.sync
        def _(sp):
            open_counts(sp, idx_ready, ticked, ohT_ready, looked, arg_ready, ex_ready, ohb_ready, parts_ready, msg_ready, summed, added,
                        base_ready, ones_ready)
            with sp.Fori(0, passes(sp, s, W64)) as r:
                with sp.Fori(0, NGS) as k:
                    i = (r * NGS + k) * SL
                    sp.wait_ge(base_ready, OPEN + r + 1)
                    for p in range(2):
                        sp.wait_ge(ohT_ready, OPEN + i + 2 * p + 2 - SL)
                        sp.dma_start(drow[p][:], rows(s.dpad[bass.ds(k * SL * GE + p * 2 * GE, 2 * GE)], W64)).then_inc(d_in[p], 16)
                        for u in (2 * p, 2 * p + 1):
                            sp.wait_ge(looked, OPEN + i + u + 1 - SL)
                            at = sp.value_load(base[0:1, bass.ds(k * SL + u, 1)], min_val=0, max_val=N)
                            sp.dma_start(tabw[u][:], s.tab[bass.ds(at, W64), :]).then_inc(tab_in[u], 16)

        @block.tensor
        def _(pe):
            pe.wait_ge(ones_ready, OPEN + 1)
            with pe.Fori(0, passes(pe, s, W64)) as r:
                def look_up(k, p):
                    b = r * NGS + k
                    for u in (2 * p, 2 * p + 1):
                        pe.wait_ge(ohT_ready, OPEN + b * SL + u + 1)
                        pe.wait_ge(tab_in[u], b * 16 + 16)
                        pe.wait_ge(arg_ready, OPEN + b * 2 + p - 1)
                        for j in range(GT):
                            last = nc.tensor.matmul(look[p][:, (u % 2) * GT + j, :], ohT[u][:, j * 128:(j + 1) * 128], tabw[u][:], start=True, stop=True)
                        last.then_inc(looked, 1)

                def sum_up(k, p):
                    i = (r * NGS + k) * SL
                    for u in (2 * p, 2 * p + 1):
                        m, o, w, ob = slot(msg, u), slot(oh, u), slot(exb, u), slot(ohb, u)
                        pe.wait_ge(msg_ready, OPEN + i + u + 1)
                        pe.wait_ge(added, OPEN + i + u + 1 - SL)
                        for c in range(2):
                            for j in range(GT):
                                nc.tensor.matmul(acc[u][:, c, :], m[:, j, c * 128:(c + 1) * 128], o[:, j, :], start=j == 0, stop=j == GT - 1)
                        pe.wait_ge(parts_ready, OPEN + (r * NGS + k) * 2 + p + 1)
                        pe.wait_ge(ohb_ready, OPEN + (r * NGS + k) * 2 + p + 1)
                        for j in range(GT):
                            last = nc.tensor.matmul(acc[u][0:EW, 2, :], w[:, j].rearrange("p a h -> p (a h)"), ob[:, j, :], start=j == 0, stop=j == GT - 1)
                        last.then_inc(summed, 1)

                def body(k, last_body):
                    look_up(k, 1)
                    sum_up(k, 0)
                    if not last_body:
                        look_up(k + 1, 0)
                    sum_up(k, 1)

                look_up(0, 0)
                with pe.Fori(0, NGS - 1) as k:
                    body(k, False)
                body(NGS - 1, True)

        @block.scalar
        def _(act):
            act.wait_ge(ones_ready, OPEN + 1)
            with act.Fori(0, passes(act, s, W64)) as r:
                def indices(k, p):
                    put_indices(nc, act, s, sidx, idx_ready, msg_ready, ticked, r * NGS + k, k, p)

                def one_hot(k, p):
                    b = r * NGS + k
                    act.drain()
                    act.wait_ge(base_ready, OPEN + r + 1)
                    act.wait_ge(d_in[p], b * 16 + 16)
                    for q in range(2):
                        nc.scalar.activation(away[:, q * GE:(q + 1) * GE], drow[p][:, q * GE:(q + 1) * GE], ACT.Abs,
                                             bias=nfirstw[:, bass.ds(k * SL + 2 * p + q, 1)])
                    act.drain()
                    for q in range(2):
                        act.wait_ge(looked, OPEN + b * SL + 2 * p + q + 1 - SL)
                        nc.scalar.activation(ohT[2 * p + q][:], away[:, q * GE:(q + 1) * GE], ACT.Relu, bias=one[:], scale=-1.0).then_inc(ohT_ready, 1)

                def weights(k, p):
                    b = r * NGS + k
                    act.wait_ge(arg_ready, OPEN + b * 2 + p + 1)
                    act.wait_ge(summed, OPEN + b * SL + 2 * p + 2 - SL)
                    nc.scalar.activation(ex[p][:, :, 0:HEADS], arg[p][:], ACT.Exp)
                    act.drain()
                    nc.scalar.copy(exb[p][:, :, 0, :], ex[p][:]).then_inc(ex_ready, 1)
                    nc.scalar.copy(ohb[p][:], oh[p][:]).then_inc(ohb_ready, 1)

                def body(k, last_body):
                    indices(k, 1)
                    one_hot(k, 1)
                    weights(k, 0)
                    if not last_body:
                        one_hot(k + 1, 0)
                        indices(k + 1, 0)
                    weights(k, 1)

                indices(0, 0)
                one_hot(0, 0)
                with act.Fori(0, NGS - 1) as k:
                    body(k, False)
                body(NGS - 1, True)

        @block.vector
        def _(dve):
            for p in range(2):
                nc.vector.memset(ex[p][:], 1.0)
            start_windows(nc, dve, s, first, firstw, 0)
            nc.vector.memset(one[:], 1.0)
            nc.vector.memset(z[0][:], 0.0).then_inc(ones_ready, 1)
            with dve.Fori(0, passes(dve, s, W64)) as r:
                nc.vector.tensor_scalar(nfirstw[:], firstw[0:W64, :], -1.0, None, ALU.mult)
                nc.vector.tensor_scalar(base[:], first[0:1, :], float(N), None, ALU.min)
                dve.drain()
                nc.vector.memset(z[0][:], 0.0).then_inc(base_ready, 1)
                def arguments(k, p):
                    b = r * NGS + k
                    pair_offsets(nc, s, drel[p], first, k, p)
                    dve.drain()
                    dve.wait_ge(summed, OPEN + b * SL + 2 * p + 2 - SL)
                    nc.vector.tensor_tensor(oh[p][:], bc(s.iota64[:], 1, PT), bc(drel[p][:], 2, W64), ALU.is_equal)
                    dve.wait_ge(looked, OPEN + b * SL + 2 * p + 2)
                    nc.vector.tensor_scalar(pen[p][:], look[p][:, :, TW - HEADS:TW], 1.0, BIG, ALU.subtract, ALU.mult)
                    parts = [look[p][:, :, a * 2 * HEADS:(a + 1) * 2 * HEADS] for a in range(A1P)]
                    nc.vector.tensor_copy(looked_up[p][:], parts[0])
                    for part in parts[1:]:
                        dve.drain()
                        nc.vector.tensor_tensor(looked_up[p][:], looked_up[p][:], part, ALU.add)
                    dve.drain()
                    for u in (2 * p, 2 * p + 1):
                        dve.wait_ge(gathered[u], b * (16 * GT) + 16 * GT)
                    nc.vector.tensor_tensor(z[p][:], ftp[p][:, :, D:FTW], looked_up[p][:, :, 0:HEADS], ALU.add)
                    dve.drain()
                    nc.vector.scalar_tensor_tensor(out=zl[p][:], in0=z[p][:], scalar=0.2, in1=z[p][:], op0=ALU.mult, op1=ALU.max)
                    dve.drain()
                    dve.wait_ge(ex_ready, OPEN + b * 2 + p - 1)
                    nc.vector.tensor_tensor(z[p][:], zl[p][:], looked_up[p][:, :, HEADS:2 * HEADS], ALU.subtract)
                    dve.drain()
                    nc.vector.tensor_tensor(arg[p][:], z[p][:], pen[p][:], ALU.min).then_inc(arg_ready, 1)

                def messages(k, p):
                    dve.wait_ge(ex_ready, OPEN + (r * NGS + k) * 2 + p + 1)
                    hi, mid, lo = [exb[p][:, :, a, :] for a in range(A1P)]
                    nc.vector.tensor_tensor(rem[p][:], ex[p][:], hi, ALU.subtract)
                    for u in (2 * p, 2 * p + 1):
                        nc.vector.tensor_tensor(slot(msg, u).rearrange("p j (h d) -> p j h d", h=HEADS),
                                                ftg[u][:, :, 0:D].rearrange("p j (h d) -> p j h d", h=HEADS),
                                                bc(slot(ex, u)[:, :, 0:HEADS], 3, HD), ALU.mult).then_inc(msg_ready, 1)
                        dve.drain()
                        if u % 2 == 0:
                            nc.vector.tensor_copy(mid, rem[p][:])
                        else:
                            nc.vector.tensor_tensor(lo, rem[p][:], mid, ALU.subtract).then_inc(parts_ready, 1)

                def add(k, p):
                    for u in (2 * p, 2 * p + 1):
                        at = dve.value_load(base[0:1, bass.ds(k * SL + u, 1)], min_val=0, max_val=N)
                        dve.drain()
                        dve.wait_ge(summed, OPEN + (r * NGS + k) * SL + u + 1)
                        w = s.accT[:, :, bass.ds(at, W64)]
                        nc.vector.tensor_tensor(w, w, acc[u][:, 0:2, :], ALU.add)
                        w = s.ndT[:, bass.ds(at, W64)]
                        nc.vector.tensor_tensor(w, w, acc[u][0:EW, 2, :], ALU.add).then_inc(added, 1)

                def body(k, last_body):
                    arguments(k, 1)
                    messages(k, 1)
                    add(k, 0)
                    if not last_body:
                        arguments(k + 1, 0)
                        messages(k + 1, 0)
                    add(k, 1)

                arguments(0, 0)
                messages(0, 0)
                with dve.Fori(0, NGS - 1) as k:
                    body(k, False)
                body(NGS - 1, True)
                next_windows(nc, dve, first, firstw, W64)


def normalise(nc, s, prefix, times):
    with ExitStack() as ctx:
        moments, scales = s.moments, s.scales
        sb = lambda name, shape: ctx.enter_context(nc.sbuf_tensor(prefix + name, shape, F32))
        st6, eps, half = sb("st6", [TP, NT, 6]), sb("eps", [TP, NT]), sb("half", [TP, NT])
        block = ctx.enter_context(nc.Block())

        @block.vector
        def _(dve):
            ln_moments(nc, dve, s.x, st6, s.mv, eps, half)
            nc.vector.memset(st6[:], 0.0).then_inc(moments, 1)
            dve.wait_ge(scales, times)

        @block.gpsimd
        def _(pool):
            pool.wait_ge(moments, times)
            nc.gpsimd.tensor_tensor(s.rstd[:], eps[:], half[:], ALU.pow).then_inc(scales, 1)


def stage_join(nc, s):
    with ExitStack() as ctx:
        sem = lambda name: ctx.enter_context(nc.semaphore("j_" + name))
        sb = lambda name, shape, dt: ctx.enter_context(nc.sbuf_tensor("j_" + name, shape, dt))
        sums, weights = sb("sums", [128, 2, TOK], F32), sb("weights", [A1P * (HEADS + 1), TOK], F32)
        rs = sb("rs", [TP, BT, HEADS + 1], F32)
        v, low, ev, part = [sb(n, [TP, BT, D], F32) for n in ("v", "low", "ev", "part")]
        taken, turned, low_ready, exp_ready, read = [sem(n) for n in ("taken", "turned", "low_ready", "exp_ready", "read")]
        ps = s.ps
        block = ctx.enter_context(nc.Block())

        @block.sync
        def _(sp):
            open_counts(sp, taken, turned, low_ready, exp_ready, read)

        @block.scalar
        def _(act):
            with act.Fori(0, NB) as b:
                act.wait_ge(turned, OPEN + b)
                nc.scalar.copy(weights[:], s.ndT[:, bass.ds(b * TOK, TOK)])
                nc.scalar.copy(sums[:], s.accT[:, :, bass.ds(b * TOK, TOK)]).then_inc(taken, 1)
                act.wait_ge(low_ready, OPEN + b + 1)
                nc.scalar.activation(ev[:], low[:], ACT.Exp).then_inc(exp_ready, 1)

        @block.tensor
        def _(pe):
            with pe.Fori(0, NB) as b:
                pe.wait_ge(taken, OPEN + b + 1)
                pe.wait_ge(read, OPEN + b)
                for j in range(BT):
                    for c in range(2):
                        nc.tensor.transpose(ps[0:TP, j, c * 128:(c + 1) * 128], sums[:, c, j * TP:(j + 1) * TP], s.ident[:])
                    last = nc.tensor.matmul(ps[0:TP, BT, j * 16:j * 16 + HEADS + 1], weights[:, j * TP:(j + 1) * TP], s.fold[:], start=True, stop=True)
                last.then_inc(turned, 1)

        @block.vector
        def _(dve):
            with dve.Fori(0, NB) as b:
                dve.wait_ge(turned, OPEN + b + 1)
                totals = ps[0:TP, BT, 0:BT * 16].rearrange("p (j h) -> p j h", j=BT)
                nc.vector.tensor_scalar(rs[:, :, 0:HEADS], totals[:, :, 0:HEADS], 1e-30, None, ALU.max)
                nc.vector.tensor_scalar(rs[:, :, HEADS:HEADS + 1], totals[:, :, HEADS:HEADS + 1], 1.0, None, ALU.max)
                dve.drain()
                nc.vector.reciprocal(rs[:], rs[:])
                dve.drain()
                for j in range(BT):
                    last = nc.vector.tensor_tensor(v[:, j, :].rearrange("p (h d) -> p h d", h=HEADS), ps[0:TP, j, 0:D].rearrange("p (h d) -> p h d", h=HEADS),
                                                   bc(rs[:, j, 0:HEADS], 2, HD), ALU.mult)
                last.then_inc(read, 1)
                nc.vector.tensor_copy(s.rdeg[:, bass.ds(b * BT, BT)], rs[:, :, HEADS])
                dve.drain()
                nc.vector.tensor_scalar(low[:], v[:], 0.0, None, ALU.min).then_inc(low_ready, 1)
                x = s.x[:, bass.ds(b * BT, BT), :]
                nc.vector.scalar_tensor_tensor(out=part[:], in0=v[:], scalar=0.0, in1=x, op0=ALU.max, op1=ALU.add)
                dve.drain()
                dve.wait_ge(exp_ready, OPEN + b + 1)
                nc.vector.scalar_tensor_tensor(out=x, in0=ev[:], scalar=-1.0, in1=part[:], op0=ALU.add, op1=ALU.add)
            nc.vector.memset(s.accT[:], 0.0)
    normalise(nc, s, "n1_", 1)


def stage_share(nc, s):
    with ExitStack() as ctx:
        sem = lambda name: ctx.enter_context(nc.semaphore("s_" + name))
        sb = lambda name, shape, dt: ctx.enter_context(nc.sbuf_tensor("s_" + name, shape, dt))
        w, brow = sb("w", [128, 2, D], F32), sb("brow", [1, D], F32)
        h, hT = sb("h", [TP, BT, D], F32), [sb(f"hT{z}", [128, 2, TP], F32) for z in range(2)]
        w_in, h_ready, h_out, h_free, turned, hT_ready, summed, kept = [sem(n) for n in ("w_in", "h_ready", "h_out", "h_free", "turned", "hT_ready", "summed", "kept")]
        ps = s.ps
        block = ctx.enter_context(nc.Block())

        @block.sync
        def _(sp):
            open_counts(sp, h_ready, h_free, turned, hT_ready, summed, kept)
            sp.dma_start(w[:], s.ins["L1_gnn_W_self"].rearrange("(c k) n -> k c n", k=128)).then_inc(w_in, 16)
            sp.dma_start(brow[:], rows(s.ins["L1_gnn_b"], 1)).then_inc(w_in, 16)
            with sp.Fori(0, NB) as b:
                sp.wait_ge(h_ready, OPEN + b * BT + BT)
                sp.dma_start(s.htab[bass.ds(b * TOK, TOK), :].rearrange("(t p) d -> p t d", p=TP), h[:]).then_inc(h_out, 16)
                sp.wait_ge(h_out, 16 * b + 16)
                sp.sem_inc(h_free, 1)

        @block.vector
        def _(dve):
            with dve.Fori(0, NB) as b:
                i = b * BT
                dve.wait_ge(h_free, OPEN + b)
                for u in range(BT):
                    dve.wait_ge(turned, OPEN + i + u + 1 - SL)
                    nc.vector.tensor_scalar(h[:, u, :], tile_of(s.x, i + u), s.mv[:, bass.ds(i + u, 1), 0], s.rstd[:, bass.ds(i + u, 1)],
                                            ALU.subtract, ALU.mult).then_inc(h_ready, 1)
                for u in range(BT):
                    dve.wait_ge(summed, OPEN + i + u + 1)
                    nc.vector.tensor_copy(tile_of(s.own, i + u), ps[0:TP, 2 + u % 2, 0:D]).then_inc(kept, 1)

        @block.tensor
        def _(pe):
            pe.wait_ge(w_in, 32)
            with pe.Fori(0, NB) as b:
                i = b * BT

                def turn(u):
                    pe.wait_ge(h_ready, OPEN + i + u + 1)
                    pe.wait_ge(hT_ready, OPEN + i + u + 1 - ago(u))
                    for c in range(2):
                        last = nc.tensor.transpose(ps[:, u % 2, c * 128:c * 128 + TP], h[:, u, c * 128:(c + 1) * 128], s.ident[0:TP, 0:TP])
                    last.then_inc(turned, 1)

                def multiply(u):
                    pe.wait_ge(hT_ready, OPEN + i + u + 1)
                    pe.wait_ge(kept, OPEN + i + u + 1 - ago(u))
                    nc.tensor.matmul(ps[0:TP, 2 + u % 2, 0:D], s.ones[0:1, 0:TP], brow[:], start=True, stop=False)
                    for c in range(2):
                        last = nc.tensor.matmul(ps[0:TP, 2 + u % 2, 0:D], hT[u % 2][:, c, :], w[:, c, :], start=False, stop=c == 1)
                    last.then_inc(summed, 1)

                in_turn(BT, [turn, multiply])

        @block.scalar
        def _(act):
            with act.Fori(0, NB) as b:
                for u in range(BT):
                    act.wait_ge(turned, OPEN + b * BT + u + 1)
                    act.wait_ge(summed, OPEN + b * BT + u + 1 - ago(u))
                    nc.scalar.copy(hT[u % 2][:], ps[:, u % 2, 0:256].rearrange("p (c n) -> p c n", c=2)[:, :, 0:TP]).then_inc(hT_ready, 1)


def stage_aggregate(nc, s):
    with ExitStack() as ctx:
        sem = lambda name: ctx.enter_context(nc.semaphore("g_" + name))
        sb = lambda name, shape, dt: ctx.enter_context(nc.sbuf_tensor("g_" + name, shape, dt))
        two_sb = lambda name, shape, dt: [sb(f"{name}{p}", shape, dt) for p in range(2)]
        sidx, drel, oh = two_sb("sidx", [128, 2 * GT], I32), two_sb("drel", [128, 2 * GT], F32), two_sb("oh", [128, 2 * GT, W64], F32)
        hg = [sb(f"hg{u}", [128, GT, D], F32) for u in range(SL)]
        first, firstw, base = sb("first", [128, NG], F32), sb("firstw", [128, NG], F32), sb("base", [1, NG], I32)
        gathered = [sem(f"gathered{u}") for u in range(SL)]
        idx_ready, ticked, oh_ready, summed, added = [sem(n) for n in ("idx_ready", "ticked", "oh_ready", "summed", "added")]
        ps = s.ps
        acc = [ps[:, 4 + u, 0:2 * W64].rearrange("p (c w) -> p c w", c=2) for u in range(SL)]
        block = ctx.enter_context(nc.Block())

        @block.sync
        def _(sp):
            open_counts(sp, idx_ready, ticked, oh_ready, summed, added)

        @block.gpsimd
        def _(pool):
            gather_rows(nc, pool, s, W64, sidx, hg, s.htab, idx_ready, gathered, ticked)

        @block.scalar
        def _(act):
            with act.Fori(0, passes(act, s, W64)) as r:
                def indices(k, p):
                    put_indices(nc, act, s, sidx, idx_ready, summed, ticked, r * NGS + k, k, p)

                indices(0, 0)
                with act.Fori(0, NGS - 1) as k:
                    indices(k, 1)
                    indices(k + 1, 0)
                indices(NGS - 1, 1)

        @block.tensor
        def _(pe):
            with pe.Fori(0, passes(pe, s, W64)) as r:
                with pe.Fori(0, NGS) as k:
                    b = r * NGS + k
                    for u in range(SL):
                        pe.wait_ge(oh_ready, OPEN + b * 2 + u // 2 + 1)
                        pe.wait_ge(added, OPEN + b * SL + u + 1 - SL)
                        pe.wait_ge(gathered[u], b * (16 * GT) + 16 * GT)
                        for c in range(2):
                            for j in range(GT):
                                last = nc.tensor.matmul(acc[u][:, c, :], hg[u][:, j, c * 128:(c + 1) * 128], oh[u // 2][:, (u % 2) * GT + j, :],
                                                        start=j == 0, stop=j == GT - 1)
                        last.then_inc(summed, 1)

        @block.vector
        def _(dve):
            start_windows(nc, dve, s, first, firstw, 0)
            with dve.Fori(0, passes(dve, s, W64)) as r:
                nc.vector.tensor_scalar(base[:], first[0:1, :], float(N), None, ALU.min)
                dve.drain()
                with dve.Fori(0, NGS) as k:
                    i = (r * NGS + k) * SL
                    for p in range(2):
                        pair_offsets(nc, s, drel[p], first, k, p)
                    dve.drain()
                    for p in range(2):
                        dve.wait_ge(summed, OPEN + i + 2 * p + 2 - SL)
                        nc.vector.tensor_tensor(oh[p][:], bc(s.iota64[:], 1, 2 * GT), bc(drel[p][:], 2, W64), ALU.is_equal).then_inc(oh_ready, 1)
                    for u in range(SL):
                        at = dve.value_load(base[0:1, bass.ds(k * SL + u, 1)], min_val=0, max_val=N)
                        dve.drain()
                        dve.wait_ge(summed, OPEN + i + u + 1)
                        w = s.accT[:, :, bass.ds(at, W64)]
                        nc.vector.tensor_tensor(w, w, acc[u], ALU.add).then_inc(added, 1)
                next_windows(nc, dve, first, firstw, W64)


def stage_join2(nc, s):
    with ExitStack() as ctx:
        sem = lambda name: ctx.enter_context(nc.semaphore("k_" + name))
        sb = lambda name, shape, dt: ctx.enter_context(nc.sbuf_tensor("k_" + name, shape, dt))
        w, sums = sb("w", [128, 2, D], F32), [sb(f"sums{z}", [128, 2, TP], F32) for z in range(2)]
        v = sb("v", [TP, BT, D], F32)
        w_in, taken, summed, read = [sem(n) for n in ("w_in", "taken", "summed", "read")]
        ps = s.ps
        block = ctx.enter_context(nc.Block())

        @block.sync
        def _(sp):
            open_counts(sp, taken, summed, read)
            sp.dma_start(w[:], s.ins["L1_gnn_W_neigh"].rearrange("(c k) n -> k c n", k=128)).then_inc(w_in, 16)

        @block.scalar
        def _(act):
            with act.Fori(0, NB) as b:
                for u in range(BT):
                    act.wait_ge(summed, OPEN + b * BT + u + 1 - ago(u))
                    nc.scalar.copy(sums[u % 2][:], s.accT[:, :, bass.ds((b * BT + u) * TP, TP)]).then_inc(taken, 1)

        @block.tensor
        def _(pe):
            pe.wait_ge(w_in, 16)
            with pe.Fori(0, NB) as b:
                for u in range(BT):
                    pe.wait_ge(taken, OPEN + b * BT + u + 1)
                    pe.wait_ge(read, OPEN + b * BT + u + 1 - ago(u))
                    for c in range(2):
                        last = nc.tensor.matmul(ps[0:TP, u % 2, 0:D], sums[u % 2][:, c, :], w[:, c, :], start=c == 0, stop=c == 1)
                    last.then_inc(summed, 1)

        @block.vector
        def _(dve):
            with dve.Fori(0, NB) as b:
                for u in range(BT):
                    t = b * BT + u
                    dve.wait_ge(summed, OPEN + t + 1)
                    nc.vector.scalar_tensor_tensor(out=v[:, u, :], in0=ps[0:TP, u % 2, 0:D], scalar=s.rdeg[:, bass.ds(t, 1)], in1=tile_of(s.own, t),
                                                   op0=ALU.mult, op1=ALU.add).then_inc(read, 1)
                dve.drain()
                x = s.x[:, bass.ds(b * BT, BT), :]
                nc.vector.scalar_tensor_tensor(out=x, in0=v[:], scalar=0.0, in1=x, op0=ALU.max, op1=ALU.add)
                dve.drain()
    normalise(nc, s, "n2_", 3)


class Mixture:

    def __init__(self, prefix, experts, hidden, out, out_chunks, out_bias):
        self.prefix, self.experts, self.hidden, self.out = prefix, experts, hidden, out
        self.out_chunks, self.out_bias = out_chunks, out_bias
        self.width = sum(n * kc * 128 for _, _, n, kc in hidden) + out_chunks * D


def stage_mixture(nc, s, m, second):
    with ExitStack() as ctx:
        X = m.experts
        sb = lambda name, shape, dt: ctx.enter_context(nc.sbuf_tensor(m.prefix + name, shape, dt))
        chosen, w12, pos = sb("chosen", [TP, NT, 2], F32), sb("w12", [TP, NT, 2], F32), sb("pos", [TP, 2 * NT], I32)
        expert, tiles = sb("expert", [1, TM], I32), sb("tiles", [1, 1], I32)
        route(nc, s, m, second, chosen, w12, pos, expert, tiles)
        run_experts(nc, s, m, expert, tiles)
        combine(nc, s, m, second, w12, pos)


def route(nc, s, m, second, chosen, w12, pos, expert, tiles):
    X = m.experts
    XP = max(X, 8)
    with ExitStack() as ctx:
        sem = lambda name: ctx.enter_context(nc.semaphore(m.prefix + name))
        sb = lambda name, shape, dt: ctx.enter_context(nc.sbuf_tensor(m.prefix + name, shape, dt))
        xT = [sb(f"xT{z}", [128, 2, TOK], F32) for z in range(2)]
        gw, gb = sb("gw", [128, 2, 128], F32), sb("gb", [1, 16], F32)
        rh, rb1, rw2 = sb("rh", [128, TOK], F32), sb("rb1", [128, 1], F32), sb("rw2", [128, 16], F32)
        score, ex = sb("score", [TP, NT, XP], F32), sb("ex", [TP, NT, X], F32)
        mxs, tot, gap, q = [sb(n, [TP, NT], F32) for n in ("mxs", "tot", "gap", "q")]
        top, topi = sb("top", [TP, NT, 8], F32), sb("topi", [TP, NT, 8], U32)
        picks = [sb(f"pick{c}", [TP, NT, X], F32) for c in range(2)]
        both, place, before = sb("both", [TP, NT, X], F32), sb("place", [TP, NT, X], F32), sb("before", [TP, NT + 1, X], F32)
        lower, all_ones = sb("lower", [TP, TP], F32), sb("all_ones", [TP, TP], F32)
        marks, full = sb("marks", [TP, NT], F32), sb("full", [TP, X, NT], F32)
        used, begins = sb("used", [TP, X], F32), sb("begins", [TP, X + 1], F32)
        past, expert_f, posf = sb("past", [1, TM, X], F32), sb("expert_f", [1, TM], F32), sb("posf", [TP, NT, 2], F32)
        consts, xn_ready, turned, xT_ready, scored, taken = [sem(n) for n in (
            "consts", "xn_ready", "turned", "xT_ready", "scored", "taken")]
        rh_sum, rh_ready = (None, None) if second else (sem("rh_sum"), sem("rh_ready"))
        asked, answered, masks, placing, ranked, sent = [sem(n) for n in (
            "asked", "answered", "masks", "placing", "ranked", "sent")]
        ps = s.ps
        block = ctx.enter_context(nc.Block())

        @block.sync
        def _(sp):
            i = s.ins
            if second:
                sp.dma_start(gw[:, :, 0:X], i["L1_ffn_gate_w"].rearrange("(c k) n -> k c n", k=128)).then_inc(consts, 16)
                sp.dma_start(gb[:, 0:X], rows(i["L1_ffn_gate_b"], 1)).then_inc(consts, 16)
            else:
                sp.dma_start(gw[:], i["L0_ffn_router_w1"].rearrange("(c k) n -> k c n", k=128)).then_inc(consts, 16)
                sp.dma_start(gb[:, 0:X], rows(i["L0_ffn_router_b2"], 1)).then_inc(consts, 16)
                sp.dma_start(rb1[:], i["L0_ffn_router_b1"].rearrange("(p a) -> p a", a=1)).then_inc(consts, 16)
                sp.dma_start(rw2[:, 0:X], i["L0_ffn_router_w2"]).then_inc(consts, 16)

        @block.gpsimd
        def _(pool):
            nc.gpsimd.memset(all_ones[:], 1.0)
            nc.gpsimd.memset(lower[:], 1.0)
            pool.drain()
            nc.gpsimd.affine_select(out=lower[:], in_=lower[:], compare_op=ALU.is_gt, fill=0.0, base=0,
                                    pattern=[[1, TP]], channel_multiplier=-1).then_inc(masks, 1)
            pool.wait_ge(placing, 2)
            pool.wait_ge(xn_ready, NB)
            for t in range(NT):
                for c in range(2):
                    nc.gpsimd.indirect_dma_start(out=s.xs, out_offset=bass.IndirectOffsetOnAxis(ap=pos[:, 2 * t + c:2 * t + c + 1], axis=0),
                                                 in_=s.own[:, t, :], in_offset=None).then_inc(sent, 16)
            pool.wait_ge(sent, 16 * 2 * NT)

        @block.tensor
        def _(pe):
            pe.wait_ge(consts, 32 if second else 64)

            def turn(b):
                pe.wait_ge(xn_ready, b + 1)
                if b:
                    pe.wait_ge(xT_ready, b)
                for j in range(BT):
                    for c in range(2):
                        last = nc.tensor.transpose(ps[:, j, c * 128:c * 128 + TP], s.own[:, b * BT + j, c * 128:(c + 1) * 128], s.ident[0:TP, 0:TP])
                last.then_inc(turned, 1)

            def score_tokens(b):
                pe.wait_ge(xT_ready, b + 1)
                if b:
                    pe.wait_ge(taken, b)
                if not second:
                    for k, (a, n) in enumerate(CUTS):
                        for c in range(2):
                            last = nc.tensor.matmul(ps[:, 5 + k, 0:n], gw[:, c, :], xT[b % 2][:, c, a:a + n], start=c == 0, stop=c == 1)
                    last.then_inc(rh_sum, 1)
                    pe.wait_ge(rh_ready, b + 1)
                for j in range(BT):
                    o = ps[0:TP, 7, j * 16:j * 16 + X]
                    if second:
                        for c in range(2):
                            nc.tensor.matmul(o, xT[b % 2][:, c, j * TP:(j + 1) * TP], gw[:, c, 0:X], start=c == 0, stop=False)
                    else:
                        nc.tensor.matmul(o, rh[:, j * TP:(j + 1) * TP], rw2[:, 0:X], start=True, stop=False)
                    last = nc.tensor.matmul(o, s.ones[0:1, 0:TP], gb[0:1, 0:X], start=False, stop=True)
                last.then_inc(scored, 1)

            in_turn(NB, [turn, score_tokens])
            pe.wait_ge(masks, 1)
            pe.wait_ge(placing, 1)
            nc.tensor.matmul(ps[0:TP, 0, 0:NT * X], lower[:], both[:].rearrange("p t x -> p (t x)"), start=True, stop=True)
            nc.tensor.matmul(ps[0:TP, 1, 0:NT * X], all_ones[:], both[:].rearrange("p t x -> p (t x)"), start=True, stop=True).then_inc(ranked, 1)

        @block.scalar
        def _(act):
            act.wait_ge(consts, 32 if second else 64)

            def take(b):
                act.wait_ge(turned, b + 1)
                if b >= 2:
                    act.wait_ge(scored, b - 1)
                nc.scalar.copy(xT[b % 2][:].rearrange("p c (j n) -> p j c n", j=BT),
                               ps[:, 0:BT, 0:256].rearrange("p j (c n) -> p j c n", c=2)[:, :, :, 0:TP]).then_inc(xT_ready, 1)

            def hide(b):
                act.wait_ge(rh_sum, b + 1)
                for k, (a, n) in enumerate(CUTS):
                    last = nc.scalar.activation(rh[:, a:a + n], ps[:, 5 + k, 0:n], ACT.Relu, bias=rb1[:])
                last.then_inc(rh_ready, 1)

            in_turn(NB, [take] if second else [take, hide])
            if not second:
                act.wait_ge(asked, 1)
                nc.scalar.activation(ex[:], score[:, :, 0:X], ACT.Exp).then_inc(answered, 1)
            act.wait_ge(asked, 1 if second else 2)
            nc.scalar.activation(q[:], gap[:], ACT.Exp).then_inc(answered, 1)

        @block.vector
        def _(dve):
            nc.vector.memset(score[:], -1.0)
            nc.vector.memset(before[:], 0.0)
            nc.vector.memset(begins[:], 0.0)
            nc.vector.tensor_scalar(marks[:], s.iota64[0:TP, 0:NT], 128.0, None, ALU.mult)
            dve.drain()

            def scale(b):
                for t in range(b * BT, (b + 1) * BT):
                    last = nc.vector.tensor_scalar(s.own[:, t, :], s.x[:, t, :], s.mv[:, t, 0:1], s.rstd[:, t:t + 1], ALU.subtract, ALU.mult)
                last.then_inc(xn_ready, 1)

            def keep(b):
                dve.wait_ge(scored, b + 1)
                nc.vector.tensor_copy(score[:, b * BT:(b + 1) * BT, 0:X],
                                      ps[0:TP, 7, 0:BT * 16].rearrange("p (j x) -> p j x", j=BT)[:, :, 0:X]).then_inc(taken, 1)

            in_turn(NB, [scale, keep])
            dve.drain()
            if not second:
                nc.vector.tensor_reduce(mxs[:], score[:, :, 0:X], AX_X, ALU.max)
                dve.drain()
                nc.vector.tensor_tensor(score[:, :, 0:X], score[:, :, 0:X], bc(mxs[:], 2, X), ALU.subtract).then_inc(asked, 1)
                dve.wait_ge(answered, 1)
                nc.vector.tensor_reduce(tot[:], ex[:], AX_X, ALU.add)
                dve.drain()
                nc.vector.reciprocal(tot[:], tot[:])
                dve.drain()
                nc.vector.tensor_tensor(score[:, :, 0:X], ex[:], bc(tot[:], 2, X), ALU.mult)
                dve.drain()
            for t in range(NT):
                nc.vector.max(top[:, t, :], score[:, t, :])
            dve.drain()
            nc.vector.tensor_tensor(gap[:], top[:, :, 1], top[:, :, 0], ALU.subtract).then_inc(asked, 1)
            for t in range(NT):
                nc.vector.max_index(topi[:, t, :], top[:, t, :], score[:, t, :])
            dve.drain()
            nc.vector.tensor_copy(chosen[:], topi[:, :, 0:2])
            dve.drain()
            for c in range(2):
                nc.vector.tensor_tensor(picks[c][:], bc(s.iota64[0:TP, 0:X], 1, NT), bc(chosen[:, :, c], 2, X), ALU.is_equal)
            dve.drain()
            nc.vector.tensor_tensor(both[:], picks[0][:], picks[1][:], ALU.add).then_inc(placing, 1)
            dve.wait_ge(answered, 1 if second else 2)
            nc.vector.tensor_scalar(tot[:], q[:], 1.0, None, ALU.add)
            dve.drain()
            nc.vector.reciprocal(w12[:, :, 0], tot[:])
            dve.drain()
            nc.vector.tensor_tensor(w12[:, :, 1], q[:], w12[:, :, 0], ALU.mult)
            dve.wait_ge(ranked, 1)
            totals = ps[0:TP, 1, 0:NT * X].rearrange("p (t x) -> p t x", t=NT)
            for t in range(NT):
                nc.vector.tensor_tensor(before[:, t + 1, :], before[:, t, :], totals[:, t, :], ALU.add)
                dve.drain()
            nc.vector.tensor_tensor(full[:], bc(marks[:], 1, X), bc(before[:, NT, :], 2, NT), ALU.is_lt)
            dve.drain()
            nc.vector.tensor_reduce(used[:], full[:], AX_X, ALU.add)
            dve.drain()
            for x in range(X):
                nc.vector.tensor_tensor(begins[:, x + 1:x + 2], begins[:, x:x + 1], used[:, x:x + 1], ALU.add)
                dve.drain()
            nc.vector.tensor_copy(tiles[:], begins[0:1, X:X + 1])
            nc.vector.tensor_tensor(past[:], bc(begins[0:1, 1:X + 1], 1, TM), bc(s.iota64[0:1, 0:TM], 2, X), ALU.is_le)
            nc.vector.tensor_scalar(used[:], begins[:, 0:X], 128.0, None, ALU.mult)
            nc.vector.tensor_tensor(place[:], before[:, 0:NT, :], ps[0:TP, 0, 0:NT * X].rearrange("p (t x) -> p t x", t=NT), ALU.add)
            dve.drain()
            nc.vector.tensor_reduce(expert_f[:], past[:], AX_X, ALU.add)
            nc.vector.tensor_tensor(place[:], place[:], bc(used[:], 1, NT), ALU.add)
            dve.drain()
            nc.vector.tensor_scalar(expert[:], expert_f[:], float(X - 1), None, ALU.min)
            for c in range(2):
                nc.vector.tensor_tensor(picks[c][:], picks[c][:], place[:], ALU.mult)
            dve.drain()
            for c in range(2):
                nc.vector.tensor_reduce(posf[:, :, c:c + 1], picks[c][:], AX_X, ALU.add)
            dve.drain()
            nc.vector.tensor_copy(pos[:], posf[:].rearrange("p t c -> p (t c)")).then_inc(placing, 1)


def run_experts(nc, s, m, expert, tiles):
    X, H = m.experts, m.hidden
    L = len(H)
    with ExitStack() as ctx:
        sem = lambda name: ctx.enter_context(nc.semaphore(m.prefix + name))
        sb = lambda name, shape, dt: ctx.enter_context(nc.sbuf_tensor(m.prefix + name, shape, dt))
        slots = lambda name, shape, n=SL: [sb(f"{name}{u}", shape, F32) for u in range(n)]
        xr, wts, y = slots("xr", [128, D]), slots("wts", [128, m.width]), slots("y", [128, D])
        eT = slots("eT", [128, 2, 128], 2)
        h = [slots(f"h{k}_", [128, n, 128], 2) for k, (_, _, n, _) in enumerate(H)]
        bias = [sb(f"bias{k}", [128, X, n], F32) for k, (_, _, n, _) in enumerate(H)]
        obias = sb("obias", [128, X, D], F32)
        rows_in = [sem(f"rows_in{u}") for u in range(SL)]
        y_out, y_free = sem("y_out"), sem("y_free")
        e_consts, e_turned, eT_ready, out_sum, y_ready = [sem(n) for n in ("e_consts", "e_turned", "eT_ready", "out_sum", "y_ready")]
        hid_sum, hid_ready = [[sem(f"{n}{k}") for k in range(L)] for n in ("hid_sum", "hid_ready")]
        n_consts = 16 * (1 + sum(n for _, _, n, _ in H))
        n_in = 16 * (2 + L)
        ps = s.ps
        xT_ps = [ps[:, z, 0:256].rearrange("p (c n) -> p c n", c=2) for z in range(2)]
        out_ps = [ps[:, 2 + z, 0:D] for z in range(2)]
        hid = [[ps[:, 4 + 2 * k + z, 0:n * 128].rearrange("p (f n) -> p f n", f=n) for z in range(2)] for k, (_, _, n, _) in enumerate(H)]
        bodies = lambda eng: (eng.value_load(tiles[0:1, 0:1], min_val=1, max_val=TM) + (SL - 1)) // SL
        block = ctx.enter_context(nc.Block())

        @block.sync
        def _(sp):
            open_counts(sp, e_turned, eT_ready, out_sum, y_ready, y_free, hid_sum, hid_ready)
            sp.dma_start(obias[:], rows(s.ins[m.out_bias].rearrange("x d -> (x d)"), 128)).then_inc(e_consts, 16)
            with nc.allow_non_contiguous_dma(reason="biases by partition"):
                for k, (_, bname, n, _) in enumerate(H):
                    for f in range(n):
                        sp.dma_start(bias[k][:, :, f], s.ins[bname][:, f * 128:(f + 1) * 128].rearrange("x p -> p x")).then_inc(e_consts, 16)
            with sp.Fori(0, bodies(sp)) as b:
                for u in range(SL):
                    i = b * SL + u
                    e = sp.value_load(expert[0:1, bass.ds(i, 1)], min_val=0, max_val=X - 1)
                    sp.wait_ge(out_sum, OPEN + b * SL + u + 1 - SL)
                    sp.dma_start(xr[u][:], s.xs[bass.ds(i * 128, 128), :]).then_inc(rows_in[u], 16)
                    at = 0
                    for name, _, n, kc in H:
                        src = s.ins[name][bass.ds(e, 1)].rearrange("x (c k) n -> k (x c) n", k=128)
                        sp.dma_start(wts[u][:, at:at + kc * n * 128].rearrange("p (c n) -> p c n", c=kc), src).then_inc(rows_in[u], 16)
                        at += kc * n * 128
                    src = s.ins[m.out][bass.ds(e, 1)].rearrange("x (c k) n -> k (x c) n", k=128)
                    sp.dma_start(wts[u][:, at:at + m.out_chunks * D].rearrange("p (c n) -> p c n", c=m.out_chunks), src).then_inc(rows_in[u], 16)

        @block.gpsimd
        def _(pool):
            with pool.Fori(0, bodies(pool)) as b:
                for u in range(SL):
                    pool.drain()
                    pool.wait_ge(y_ready, OPEN + b * SL + u + 1)
                    nc.gpsimd.tensor_tensor(s.tick[0:1, 0:1], s.tick[0:1, 2:3], s.tick[0:1, 3:4], ALU.add)
                    pool.dma_start(s.ys[bass.ds((b * SL + u) * 128, 128), :], y[u][:]).then_inc(y_out, 16)
                    pool.wait_ge(y_out, (b * SL + u) * 16 + 16)
                    nc.gpsimd.tensor_tensor(s.tick[0:1, 1:2], s.tick[0:1, 2:3], s.tick[0:1, 3:4], ALU.add).then_inc(y_free, 1)

        @block.tensor
        def _(pe):
            with pe.Fori(0, bodies(pe)) as b:
                i = b * SL

                def turn(u):
                    pe.wait_ge(rows_in[u], b * n_in + n_in)
                    pe.wait_ge(eT_ready, OPEN + i + u + 1 - 2)
                    for c in range(2):
                        last = nc.tensor.transpose(xT_ps[u % 2][:, c, :], xr[u][:, c * 128:(c + 1) * 128], s.ident[:])
                    last.then_inc(e_turned, 1)

                def hidden(k, at):
                    _, _, n, kc = H[k]

                    def step(u):
                        if k == 0:
                            pe.wait_ge(eT_ready, OPEN + i + u + 1)
                        else:
                            pe.wait_ge(hid_ready[k - 1], OPEN + i + u + 1)
                        pe.wait_ge(hid_ready[k], OPEN + i + u + 1 - 2)
                        frm = h[k - 1][u % 2] if k else eT[u % 2]
                        for f in range(n):
                            for c in range(kc):
                                last = nc.tensor.matmul(hid[k][u % 2][:, f, :], wts[u][:, at + (c * n + f) * 128:at + (c * n + f + 1) * 128], frm[:, c, :],
                                                        start=c == 0, stop=c == kc - 1)
                        last.then_inc(hid_sum[k], 1)
                    return step

                def output(u):
                    pe.wait_ge(hid_ready[L - 1], OPEN + i + u + 1)
                    pe.wait_ge(y_ready, OPEN + i + u + 1 - 2)
                    at = m.width - m.out_chunks * D
                    for c in range(m.out_chunks):
                        last = nc.tensor.matmul(out_ps[u % 2], h[L - 1][u % 2][:, c, :], wts[u][:, at + c * D:at + (c + 1) * D],
                                                start=c == 0, stop=c == m.out_chunks - 1)
                    last.then_inc(out_sum, 1)

                starts = np.cumsum([0] + [n * kc * 128 for _, _, n, kc in H])
                in_turn(SL, [turn] + [hidden(k, int(starts[k])) for k in range(L)] + [output])

        @block.scalar
        def _(act):
            act.wait_ge(e_consts, n_consts)
            with act.Fori(0, bodies(act)) as b:
                i = b * SL

                def take(u):
                    act.wait_ge(e_turned, OPEN + i + u + 1)
                    act.wait_ge(hid_sum[0], OPEN + i + u + 1 - 2)
                    nc.scalar.copy(eT[u % 2][:], xT_ps[u % 2]).then_inc(eT_ready, 1)

                def activate(k):
                    def step(u):
                        e = act.value_load(expert[0:1, bass.ds(i + u, 1)], min_val=0, max_val=X - 1)
                        act.wait_ge(hid_sum[k], OPEN + i + u + 1)
                        act.wait_ge(hid_sum[k + 1] if k + 1 < L else out_sum, OPEN + i + u + 1 - 2)
                        for f in range(H[k][2]):
                            last = nc.scalar.activation(h[k][u % 2][:, f, :], hid[k][u % 2][:, f, :], ACT.Relu,
                                                        bias=bias[k][:, bass.ds(e, 1), f:f + 1].rearrange("p x f -> p (x f)"))
                        last.then_inc(hid_ready[k], 1)
                    return step

                in_turn(SL, [take] + [activate(k) for k in range(L)])

        @block.vector
        def _(dve):
            dve.wait_ge(e_consts, n_consts)
            with dve.Fori(0, bodies(dve)) as b:
                for u in range(SL):
                    e = dve.value_load(expert[0:1, bass.ds(b * SL + u, 1)], min_val=0, max_val=X - 1)
                    dve.wait_ge(out_sum, OPEN + b * SL + u + 1)
                    dve.wait_ge(y_free, OPEN + b * SL + u + 1 - SL)
                    nc.vector.tensor_tensor(y[u][:], out_ps[u % 2], obias[:, bass.ds(e, 1), :].rearrange("p x d -> p (x d)"), ALU.add).then_inc(y_ready, 1)


def combine(nc, s, m, second, w12, pos):
    with ExitStack() as ctx:
        sem = lambda name: ctx.enter_context(nc.semaphore(m.prefix + name))
        sb = lambda name, shape, dt: ctx.enter_context(nc.sbuf_tensor(m.prefix + name, shape, dt))
        yg = [sb(f"yg{z}", [TP, BT, 2, D], F32) for z in range(2)]
        fetched, used_up = [sem(f"fetched{z}") for z in range(2)], sem("used_up")
        if second:
            gamma, beta = sb("gamma", [TP, D], F32), sb("beta", [TP, D], F32)
            ob = [sb(f"ob{z}", [TP, BT, D], F32) for z in range(2)]
            st6, mv, eps, half, rstd = sb("st6", [TP, BT, 6], F32), sb("mv", [TP, BT, 2], F32), sb("eps", [TP, BT], F32), sb("half", [TP, BT], F32), sb("rstd", [TP, BT], F32)
            gb_in, ob_ready, ob_out0, ob_out1 = [sem(n) for n in ("gb_in", "ob_ready", "ob_out0", "ob_out1")]
            moments, scales, counted = s.moments, s.scales, 3
            ob_out = [ob_out0, ob_out1]
        block = ctx.enter_context(nc.Block())

        @block.sync
        def _(sp):
            if second:
                sp.dma_start(gamma[:], rows(s.ins["L1_ffn_gamma"], TP)).then_inc(gb_in, 16)
                sp.dma_start(beta[:], rows(s.ins["L1_ffn_beta"], TP)).then_inc(gb_in, 16)
                for b in range(NB):
                    sp.wait_ge(ob_ready, b + 1)
                    sp.dma_start(s.out[b * TOK:(b + 1) * TOK, :].rearrange("(t p) d -> p t d", p=TP), ob[b % 2][:]).then_inc(ob_out[b % 2], 16)
                for z in range(2):
                    sp.wait_ge(ob_out[z], 16 * len(range(z, NB, 2)))

        @block.gpsimd
        def _(pool):
            def scale(b):
                pool.wait_ge(moments, counted + b + 1)
                nc.gpsimd.tensor_tensor(rstd[:], eps[:], half[:], ALU.pow).then_inc(scales, 1)

            for b in range(NB):
                if b >= 2:
                    pool.wait_ge(used_up, b - 1)
                for j in range(BT):
                    for c in range(2):
                        at = 2 * (b * BT + j) + c
                        nc.gpsimd.indirect_dma_start(out=yg[b % 2][:, j, c, :], out_offset=None, in_=s.ys,
                                                     in_offset=bass.IndirectOffsetOnAxis(ap=pos[:, at:at + 1], axis=0)).then_inc(fetched[b % 2], 16)
                if second and b:
                    scale(b - 1)
            if second:
                scale(NB - 1)

        @block.vector
        def _(dve):
            if second:
                nc.vector.memset(half[:], -0.5)
                dve.wait_ge(gb_in, 32)
            for b in range(NB):
                dve.wait_ge(fetched[b % 2], 16 * 2 * BT * (b // 2 + 1))
                for c in range(2):
                    for j in range(BT):
                        t = b * BT + j
                        row = s.own[:, t, :] if second else s.x[:, t, :]
                        last = nc.vector.scalar_tensor_tensor(out=row, in0=yg[b % 2][:, j, c, :], scalar=w12[:, t, c:c + 1], in1=row, op0=ALU.mult, op1=ALU.add)
                    if c:
                        last.then_inc(used_up, 1)
                    dve.drain()
                if not second:
                    continue
                for j in range(BT):
                    nc.vector.bn_stats(st6[:, j, :], s.own[:, b * BT + j, :])
                dve.drain()
                for j in range(BT):
                    nc.vector.bn_aggr(mv[:, j, :], st6[:, j, :])
                dve.drain()
                nc.vector.tensor_scalar(eps[:], mv[:, :, 1], EPS, None, ALU.add).then_inc(moments, 1)
                dve.wait_ge(scales, counted + b + 1)
                o = ob[b % 2]
                if b >= 2:
                    dve.wait_ge(ob_out[b % 2], 16 * (b // 2))
                for j in range(BT):
                    nc.vector.tensor_scalar(o[:, j, :], s.own[:, b * BT + j, :], mv[:, j, 0:1], rstd[:, j:j + 1], ALU.subtract, ALU.mult)
                dve.drain()
                nc.vector.tensor_tensor(o[:], o[:], bc(gamma[:], 1, BT), ALU.mult)
                dve.drain()
                nc.vector.tensor_tensor(o[:], o[:], bc(beta[:], 1, BT), ALU.add)
                dve.drain()
                nc.vector.tensor_tensor(o[:], o[:], s.x[:, b * BT:(b + 1) * BT, :], ALU.add).then_inc(ob_ready, 1)


def stage_experts(nc, s):
    m = Mixture("x_", 6, (("L0_ffn_expert_w1", "L0_ffn_expert_b1", 2, 2), ("L0_ffn_expert_w2", "L0_ffn_expert_b2", 2, 2)),
                "L0_ffn_expert_w3", 2, "L0_ffn_expert_b3")
    stage_mixture(nc, s, m, False)
    normalise(nc, s, "n3_", 2)


def stage_experts2(nc, s):
    m = Mixture("y_", 16, (("L1_ffn_w1", "L1_ffn_b1", 4, 2),), "L1_ffn_w2", 4, "L1_ffn_b2")
    stage_mixture(nc, s, m, True)


class Shared:
    pass


def program(nc, ins, out, stages=99):
    s = Shared()
    s.x_dram, s.src, s.dst, s.W, s.attn_l, s.attn_r = [ins[n] for n in ("x", "src", "dst", "L0_gnn_W", "L0_gnn_attn_l", "L0_gnn_attn_r")]
    s.ins, s.out = ins, out
    s.dpad = nc.dram_tensor("dpad", (NG * GE,), I32, kind="Internal").ap()
    s.grp = nc.dram_tensor("grp", (NG, 2), F32, kind="Internal").ap()
    s.a1tab = nc.dram_tensor("a1tab", (N, A1P * HEADS), BF16, kind="Internal").ap()
    s.ftab = nc.dram_tensor("ftab", (N, FTW), F32, kind="Internal").ap()
    s.tab = nc.dram_tensor("tab", (NPAD, TW), BF16, kind="Internal").ap()
    s.htab = nc.dram_tensor("htab", (N, D), F32, kind="Internal").ap()
    s.xs = nc.dram_tensor("xs", (TM * 128, D), F32, kind="Internal").ap()
    s.ys = nc.dram_tensor("ys", (TM * 128, D), F32, kind="Internal").ap()
    with ExitStack() as ctx:
        sb = lambda name, shape, dt: ctx.enter_context(nc.sbuf_tensor(name, shape, dt))
        s.moments, s.scales, s.x_in, s.slots_out = [ctx.enter_context(nc.semaphore(n)) for n in ("moments", "scales", "x_in", "slots_out")]
        s.ps = ctx.enter_context(nc.psum_tensor("ps", [128, 8, 512], F32))
        s.ident, s.identb = sb("ident", [128, 128], F32), sb("identb", [128, 128], BF16)
        s.sel = sb("sel", [GT * A1P * HEADS, HEADS, 128], BF16)
        s.iota64, s.part = sb("iota64", [128, W64], F32), sb("part", [128, 2], F32)
        s.tick = sb("tick", [1, 4], F32)
        s.fold = sb("fold", [A1P * (HEADS + 1), HEADS + 1], F32)
        s.zero_rows = sb("zero_rows", [128, D], F32)
        s.ones = sb("ones", [1, 128], F32)
        s.dcol, s.scol = sb("dcol", [128, CH * 128], F32), sb("scol", [128, CH * 128], I32)
        s.gmm, s.widest = sb("gmm", [128, 2 * NG], F32), sb("widest", [128, 1], I32)
        s.x = sb("x", [TP, NT, D], F32)
        s.a2 = sb("a2", [TP, NT, HEADS], F32)
        s.accT = sb("accT", [128, 2, NPAD], F32)
        s.ndT = sb("ndT", [A1P * (HEADS + 1), NPAD], F32)
        s.mv, s.rstd = sb("mv", [TP, NT, 2], F32), sb("rstd", [TP, NT], F32)
        s.rdeg = sb("rdeg", [TP, NT], F32)
        s.own = sb("own", [TP, NT, D], F32)
        for n, stage in enumerate((stage_edges, stage_project, stage_maxima, stage_attend, stage_join, stage_experts, stage_share, stage_aggregate, stage_join2, stage_experts2)):
            if n < stages:
                stage(nc, s)


def kernel(**inputs):
    import concourse.bacc as bacc
    from concourse.bass_utils import run_bass_kernel_spmd

    nc = bacc.Bacc("TRN2", target_bir_lowering=False, num_devices=1)
    arrays, aps = {}, {}
    for name, value in inputs.items():
        a = np.ascontiguousarray(value)
        arrays[f"in_{name}_dram"] = a
        aps[name] = nc.dram_tensor(f"in_{name}_dram", a.shape, mybir.dt.from_np(a.dtype), kind="ExternalInput").ap()
    out = nc.dram_tensor("out_dram", (N, D), F32, kind="ExternalOutput").ap()
    program(nc, aps, out)
    r = run_bass_kernel_spmd(nc, [arrays], core_ids=[0])
    return r.results[0]["out_dram"]
```
